# Optimizing a Trainium2 kernel written in Bass

```python
import numpy as np
import jax
import jax.numpy as jnp

def _softmax(x, axis=-1):
    return jax.nn.softmax(x, axis=axis)

def _gelu(x):
    return jax.nn.gelu(x, approximate=True)

def _silu(x):
    return jax.nn.silu(x)

def _sigmoid(x):
    return jax.nn.sigmoid(x)

def _layernorm(x, axis=-1, eps=1e-05):
    m = jnp.mean(x, axis=axis, keepdims=True)
    v = jnp.var(x, axis=axis, keepdims=True)
    return (x - m) / jnp.sqrt(v + eps)

def _scatter_add(tgt, idx, src, axis=0):
    return tgt.at[idx].add(src)

def _segment_sum(src, seg, n):
    return jax.ops.segment_sum(src, seg, n)
kernel_name = 'mk_adaln_ffn_d2_seqx_r8_b864f3'

def setup_inputs(seed: int=0):
    np.random.seed(seed)
    _w = jnp.asarray

    def _rec_inputs():
        import jax
        import jax.numpy as jnp
        _rk = jax.random.key(seed)
        x = 4.136e-05 + 0.9999 * jax.random.normal(jax.random.fold_in(_rk, 1), (32, 128, 128), jnp.float32)
        _lenS = 128 - jax.random.randint(jax.random.fold_in(_rk, 7), (32,), 0, max(1, 128 // 4) + 1, jnp.int32)
        _lenS2 = 128 - jax.random.randint(jax.random.fold_in(_rk, 8), (32,), 0, max(1, 128 // 4) + 1, jnp.int32)
        cond_1024 = -0.00608245 + 1.00131 * jax.random.normal(jax.random.fold_in(_rk, 11), (32, 128), jnp.float32)
        return (x, cond_1024)
    x, cond_1024 = _rec_inputs()

    def _L0_cond_setup():
        import jax, jax.numpy as jnp
        import numpy as np
        B, T, D_IN, V_IN, E = (64, 128, 128, 128, 128)
        key = jax.random.key(seed)
        ks = jax.random.split(key, 16)
        s = 0.01
        return {'video': jax.random.normal(ks[0], (B, V_IN), jnp.float32), 'seq': jax.random.normal(ks[1], (B, T, D_IN), jnp.float32), 'W_z': jax.random.normal(ks[2], (D_IN, E), jnp.float32) * s, 'U_z': jax.random.normal(ks[3], (E, E), jnp.float32) * s, 'C_z': jax.random.normal(ks[4], (V_IN, E), jnp.float32) * s, 'b_z': jnp.zeros((E,), jnp.float32), 'W_r': jax.random.normal(ks[5], (D_IN, E), jnp.float32) * s, 'U_r': jax.random.normal(ks[6], (E, E), jnp.float32) * s, 'C_r': jax.random.normal(ks[7], (V_IN, E), jnp.float32) * s, 'b_r': jnp.zeros((E,), jnp.float32), 'W': jax.random.normal(ks[8], (D_IN, E), jnp.float32) * s, 'U': jax.random.normal(ks[9], (E, E), jnp.float32) * s, 'C': jax.random.normal(ks[10], (V_IN, E), jnp.float32) * s, 'b': jnp.zeros((E,), jnp.float32)}
    _L0_cond_all = _L0_cond_setup()
    _L0_cond_in = {k: v for k, v in _L0_cond_all.items() if k in ('W_z', 'U_z', 'C_z', 'b_z', 'W_r', 'U_r', 'C_r', 'b_r', 'W', 'U', 'C', 'b')}
    del _L0_cond_all

    def _L0_ffn_setup():
        import jax, jax.numpy as jnp
        import numpy as np
        D_MODEL = 128
        HIDDEN = 512
        NUM_EXPERTS = 8
        TOP_K = 2
        NUM_SHARED = 2

        def _gelu(x):
            return jax.nn.gelu(x, approximate=False)
        key = jax.random.key(seed)
        ks = jax.random.split(key, 12)
        s = 0.02
        return {'x': jax.random.normal(ks[0], (2, 256, D_MODEL), dtype=jnp.float32), 'rW': jax.random.normal(ks[1], (D_MODEL, NUM_EXPERTS), dtype=jnp.float32) * s, 'rb': jnp.zeros((NUM_EXPERTS,), dtype=jnp.float32), 'W1': jax.random.normal(ks[2], (NUM_EXPERTS, D_MODEL, HIDDEN), dtype=jnp.float32) * s, 'b1': jnp.zeros((NUM_EXPERTS, HIDDEN), dtype=jnp.float32), 'W2': jax.random.normal(ks[3], (NUM_EXPERTS, HIDDEN, D_MODEL), dtype=jnp.float32) * s, 'b2': jnp.zeros((NUM_EXPERTS, D_MODEL), dtype=jnp.float32), 'sW1': jax.random.normal(ks[4], (NUM_SHARED, D_MODEL, HIDDEN), dtype=jnp.float32) * s, 'sb1': jnp.zeros((NUM_SHARED, HIDDEN), dtype=jnp.float32), 'sW2': jax.random.normal(ks[5], (NUM_SHARED, HIDDEN, D_MODEL), dtype=jnp.float32) * s, 'sb2': jnp.zeros((NUM_SHARED, D_MODEL), dtype=jnp.float32)}
    _L0_ffn_all = _L0_ffn_setup()
    _L0_ffn_in = {k: v for k, v in _L0_ffn_all.items() if k in ('rW', 'rb', 'W1', 'b1', 'W2', 'b2', 'sW1', 'sb1', 'sW2', 'sb2')}
    del _L0_ffn_all

    def _L1_cond_setup():
        import jax, jax.numpy as jnp
        import numpy as np
        D = 128
        key = jax.random.key(seed)
        ks = jax.random.split(key, 12)
        sc_in = 1.0 / np.sqrt(D)
        sc_in2 = 1.0 / np.sqrt(2 * D)
        inp = {'X1': jax.random.normal(ks[0], (8, D), dtype=jnp.float32), 'X2': jax.random.normal(ks[1], (8, 256, D), dtype=jnp.float32), 'Wq1': jax.random.normal(ks[2], (D, D), dtype=jnp.float32) * sc_in, 'bq1': jax.random.normal(ks[3], (D,), dtype=jnp.float32) * 0.01, 'Wq2': jax.random.normal(ks[4], (D, D), dtype=jnp.float32) * sc_in, 'bq2': jax.random.normal(ks[5], (D,), dtype=jnp.float32) * 0.01, 'Wk1': jax.random.normal(ks[6], (D, D), dtype=jnp.float32) * sc_in, 'bk1': jax.random.normal(ks[7], (D,), dtype=jnp.float32) * 0.01, 'Wk2': jax.random.normal(ks[8], (D, D), dtype=jnp.float32) * sc_in, 'bk2': jax.random.normal(ks[9], (D,), dtype=jnp.float32) * 0.01, 'Wv': jax.random.normal(ks[10], (2 * D, D), dtype=jnp.float32) * sc_in2, 'bv': jax.random.normal(ks[11], (D,), dtype=jnp.float32) * 0.01, 'alpha': jnp.float32(0.5)}
        return inp
    _L1_cond_all = _L1_cond_setup()
    _L1_cond_in = {k: v for k, v in _L1_cond_all.items() if k in ('Wq1', 'bq1', 'Wq2', 'bq2', 'Wk1', 'bk1', 'Wk2', 'bk2', 'Wv', 'bv', 'alpha')}
    del _L1_cond_all

    def _L1_ffn_setup():
        import jax, jax.numpy as jnp
        import numpy as np
        TOP_K = 2
        CAP_FACTOR = 1.25
        EPS = 1.1920929e-07
        key = jax.random.key(seed)
        ks = jax.random.split(key, 6)
        B, S, D, E, H = (8, 256, 128, 8, 512)
        return {'hidden_states': jax.random.normal(ks[0], (B, S, D), jnp.float32), 'wg': jax.random.normal(ks[1], (D, E), jnp.float32) * 0.02, 'fc1_w': jax.random.normal(ks[2], (E, H, D), jnp.float32) * 0.02, 'fc1_b': jnp.zeros((E, H), jnp.float32), 'fc2_w': jax.random.normal(ks[3], (E, H, D), jnp.float32) * 0.02, 'fc2_b': jnp.zeros((E, D), jnp.float32), 'ln_gamma': jnp.ones((D,), jnp.float32), 'ln_beta': jnp.zeros((D,), jnp.float32)}
    _L1_ffn_all = _L1_ffn_setup()
    _L1_ffn_in = {k: v for k, v in _L1_ffn_all.items() if k in ('wg', 'fc1_w', 'fc1_b', 'fc2_w', 'fc2_b', 'ln_gamma', 'ln_beta')}
    del _L1_ffn_all
    return {'x': x, 'cond_1024': cond_1024, 'L0_cond_W_z': _L0_cond_in['W_z'], 'L0_cond_U_z': _L0_cond_in['U_z'], 'L0_cond_C_z': _L0_cond_in['C_z'], 'L0_cond_b_z': _L0_cond_in['b_z'], 'L0_cond_W_r': _L0_cond_in['W_r'], 'L0_cond_U_r': _L0_cond_in['U_r'], 'L0_cond_C_r': _L0_cond_in['C_r'], 'L0_cond_b_r': _L0_cond_in['b_r'], 'L0_cond_W': _L0_cond_in['W'], 'L0_cond_U': _L0_cond_in['U'], 'L0_cond_C': _L0_cond_in['C'], 'L0_cond_b': _L0_cond_in['b'], 'L0_ffn_rW': _L0_ffn_in['rW'], 'L0_ffn_rb': _L0_ffn_in['rb'], 'L0_ffn_W1': _L0_ffn_in['W1'], 'L0_ffn_b1': _L0_ffn_in['b1'], 'L0_ffn_W2': _L0_ffn_in['W2'], 'L0_ffn_b2': _L0_ffn_in['b2'], 'L0_ffn_sW1': _L0_ffn_in['sW1'], 'L0_ffn_sb1': _L0_ffn_in['sb1'], 'L0_ffn_sW2': _L0_ffn_in['sW2'], 'L0_ffn_sb2': _L0_ffn_in['sb2'], 'L1_cond_Wq1': _L1_cond_in['Wq1'], 'L1_cond_bq1': _L1_cond_in['bq1'], 'L1_cond_Wq2': _L1_cond_in['Wq2'], 'L1_cond_bq2': _L1_cond_in['bq2'], 'L1_cond_Wk1': _L1_cond_in['Wk1'], 'L1_cond_bk1': _L1_cond_in['bk1'], 'L1_cond_Wk2': _L1_cond_in['Wk2'], 'L1_cond_bk2': _L1_cond_in['bk2'], 'L1_cond_Wv': _L1_cond_in['Wv'], 'L1_cond_bv': _L1_cond_in['bv'], 'L1_cond_alpha': _L1_cond_in['alpha'], 'L1_ffn_wg': _L1_ffn_in['wg'], 'L1_ffn_fc1_w': _L1_ffn_in['fc1_w'], 'L1_ffn_fc1_b': _L1_ffn_in['fc1_b'], 'L1_ffn_fc2_w': _L1_ffn_in['fc2_w'], 'L1_ffn_fc2_b': _L1_ffn_in['fc2_b'], 'L1_ffn_ln_gamma': _L1_ffn_in['ln_gamma'], 'L1_ffn_ln_beta': _L1_ffn_in['ln_beta']}

def reference(x, cond_1024, L0_cond_W_z, L0_cond_U_z, L0_cond_C_z, L0_cond_b_z, L0_cond_W_r, L0_cond_U_r, L0_cond_C_r, L0_cond_b_r, L0_cond_W, L0_cond_U, L0_cond_C, L0_cond_b, L0_ffn_rW, L0_ffn_rb, L0_ffn_W1, L0_ffn_b1, L0_ffn_W2, L0_ffn_b2, L0_ffn_sW1, L0_ffn_sb1, L0_ffn_sW2, L0_ffn_sb2, L1_cond_Wq1, L1_cond_bq1, L1_cond_Wq2, L1_cond_bq2, L1_cond_Wk1, L1_cond_bk1, L1_cond_Wk2, L1_cond_bk2, L1_cond_Wv, L1_cond_bv, L1_cond_alpha, L1_ffn_wg, L1_ffn_fc1_w, L1_ffn_fc1_b, L1_ffn_fc2_w, L1_ffn_fc2_b, L1_ffn_ln_gamma, L1_ffn_ln_beta):
    import jax
    import jax.numpy as jnp

    def _L0_cond_ref(video, seq, W_z, U_z, C_z, b_z, W_r, U_r, C_r, b_r, W, U, C, b):
        import jax, jax.numpy as jnp
        import numpy as np
        B, T, D_IN, V_IN, E = (64, 128, 128, 128, 128)
        vz = video @ C_z + b_z
        vr = video @ C_r + b_r
        vh = video @ C + b
        xz = jnp.einsum('btd,de->bte', seq, W_z)
        xr = jnp.einsum('btd,de->bte', seq, W_r)
        xh = jnp.einsum('btd,de->bte', seq, W)

        def step(h, xs):
            xzt, xrt, xht = xs
            z = jax.nn.sigmoid(xzt + h @ U_z + vz)
            r = jax.nn.sigmoid(xrt + h @ U_r + vr)
            hh = jnp.tanh(xht + r * h @ U + vh)
            h_new = (1.0 - z) * h + z * hh
            return (h_new, h_new)
        h0 = jnp.zeros((seq.shape[0], U.shape[0]), seq.dtype)
        xs = (jnp.swapaxes(xz, 0, 1), jnp.swapaxes(xr, 0, 1), jnp.swapaxes(xh, 0, 1))
        _, out_t = jax.lax.scan(step, h0, xs)
        return jnp.swapaxes(out_t, 0, 1)

    def _L0_ffn_ref(x, rW, rb, W1, b1, W2, b2, sW1, sb1, sW2, sb2):
        import jax, jax.numpy as jnp
        import numpy as np
        D_MODEL = 128
        HIDDEN = 512
        NUM_EXPERTS = 8
        TOP_K = 2
        NUM_SHARED = 2

        def _gelu(x):
            return jax.nn.gelu(x, approximate=False)
        B, L, D = x.shape
        xf = x.reshape(-1, D)
        sh = _gelu(jnp.einsum('td,sdh->sth', xf, sW1) + sb1[:, None, :])
        shared = jnp.einsum('sth,shd->std', sh, sW2) + sb2[:, None, :]
        shared = shared.mean(axis=0)
        gates = xf @ rW + rb
        topk_vals, topk_idx = jax.lax.top_k(gates, TOP_K)
        topk_probs = jax.nn.softmax(topk_vals, axis=-1)
        onehot = topk_idx[:, :, None] == jnp.arange(NUM_EXPERTS)[None, None, :]
        w = jnp.sum(topk_probs[:, :, None] * onehot, axis=1)
        h = _gelu(jnp.einsum('td,edh->eth', xf, W1) + b1[:, None, :])
        y = jnp.einsum('eth,ehd->etd', h, W2) + b2[:, None, :]
        moe = jnp.einsum('te,etd->td', w, y)
        return (shared + moe).reshape(B, L, D)

    def _L1_cond_ref(X1, X2, Wq1, bq1, Wq2, bq2, Wk1, bk1, Wk2, bk2, Wv, bv, alpha):
        import jax, jax.numpy as jnp
        import numpy as np
        D = 128
        B, S, Dm = X2.shape
        X1e = jnp.broadcast_to(X1[:, None, :], (B, S, Dm))
        X = jnp.concatenate([X1e, X2], axis=-1)
        Q1 = X1e @ Wq1 + bq1
        K1 = X1e @ Wk1 + bk1
        Q2 = X2 @ Wq2 + bq2
        K2 = X2 @ Wk2 + bk2
        V = X @ Wv + bv
        s = 1.0 / jnp.sqrt(jnp.float32(Dm))
        A1 = jnp.einsum('bqd,bkd->bqk', Q1, K1) * s
        A2 = jnp.einsum('bqd,bkd->bqk', Q2, K2) * s
        A = jax.nn.softmax(A2, axis=-1) - alpha * jax.nn.softmax(A1, axis=-1)
        return jnp.einsum('bqk,bkd->bqd', A, V)

    def _L1_ffn_ref(hidden_states, wg, fc1_w, fc1_b, fc2_w, fc2_b, ln_gamma, ln_beta):
        import jax, jax.numpy as jnp
        import numpy as np
        TOP_K = 2
        CAP_FACTOR = 1.25
        EPS = 1.1920929e-07
        B, S, D = hidden_states.shape
        E = wg.shape[1]
        N = B * S
        k = TOP_K
        C = k * int(CAP_FACTOR * ((N + E - 1) // E))
        x = hidden_states.reshape(N, D)
        scores = jax.nn.softmax(x @ wg, axis=-1)
        gates, idx = jax.lax.top_k(scores, k)
        gates = gates / jnp.clip(jnp.sum(gates, -1, keepdims=True), EPS)
        masks = jax.nn.one_hot(idx, E, dtype=jnp.int32)
        counts = masks.sum(0)
        offsets = jnp.concatenate([jnp.zeros((1, E), jnp.int32), jnp.cumsum(counts, 0)[:-1]], 0)
        loc = jnp.cumsum(masks, 0) - 1 + offsets[None]
        loc_sel = (loc * masks).sum(-1)
        keep = loc_sel < C
        gates = gates * keep.astype(gates.dtype)
        pos = jnp.where(keep, idx * C + loc_sel, E * C)
        xk = jnp.broadcast_to(x[:, None, :], (N, k, D)).reshape(N * k, D)
        buf = jnp.zeros((E * C + 1, D), x.dtype).at[pos.reshape(-1)].set(xk)
        disp = buf[:E * C].reshape(E, C, D)
        h = jax.nn.silu(jnp.einsum('ecd,ehd->ech', disp, fc1_w) + fc1_b[:, None, :])
        y = jnp.einsum('ech,ehd->ecd', h, fc2_w) + fc2_b[:, None, :]
        ybuf = jnp.concatenate([y.reshape(E * C, D), jnp.zeros((1, D), y.dtype)], 0)
        combined = jnp.sum(gates[..., None] * ybuf[pos], axis=1)
        res = hidden_states + combined.reshape(B, S, D)
        mu = jnp.mean(res, -1, keepdims=True)
        var = jnp.var(res, -1, keepdims=True)
        return (res - mu) * jax.lax.rsqrt(var + 1e-05) * ln_gamma + ln_beta
    x = x + _L0_ffn_ref(_L0_cond_ref(cond_1024, x, L0_cond_W_z, L0_cond_U_z, L0_cond_C_z, L0_cond_b_z, L0_cond_W_r, L0_cond_U_r, L0_cond_C_r, L0_cond_b_r, L0_cond_W, L0_cond_U, L0_cond_C, L0_cond_b), L0_ffn_rW, L0_ffn_rb, L0_ffn_W1, L0_ffn_b1, L0_ffn_W2, L0_ffn_b2, L0_ffn_sW1, L0_ffn_sb1, L0_ffn_sW2, L0_ffn_sb2)
    x = x + _L1_ffn_ref(_L1_cond_ref(cond_1024, x, L1_cond_Wq1, L1_cond_bq1, L1_cond_Wq2, L1_cond_bq2, L1_cond_Wk1, L1_cond_bk1, L1_cond_Wk2, L1_cond_bk2, L1_cond_Wv, L1_cond_bv, L1_cond_alpha), L1_ffn_wg, L1_ffn_fc1_w, L1_ffn_fc1_b, L1_ffn_fc2_w, L1_ffn_fc2_b, L1_ffn_ln_gamma, L1_ffn_ln_beta)
    return x

_drawn_inputs = setup_inputs


def setup_inputs(seed=0):
    import zlib

    import numpy as np

    out = dict(_drawn_inputs(seed))
    spreads = {'L0_cond_b_z': (0.0, 2.0),
     'L0_cond_b_r': (0.0, 2.0),
     'L0_cond_b': (0.0, 0.1),
     'L0_ffn_rb': (0.0, 0.1),
     'L0_ffn_b1': (0.0, 0.276),
     'L0_ffn_b2': (0.0, 0.1),
     'L0_ffn_sb1': (0.0, 0.27),
     'L0_ffn_sb2': (0.0, 0.1),
     'L1_ffn_fc1_b': (0.0, 0.27),
     'L1_ffn_fc2_b': (0.0, 0.1),
     'L1_ffn_ln_gamma': (1.0, 0.2),
     'L1_ffn_ln_beta': (0.0, 0.1)}
    factors = {'L0_cond_W_z': 6.059,
     'L0_cond_U_z': 42.054,
     'L0_cond_C_z': 7.076,
     'L0_cond_W_r': 27.933,
     'L0_cond_U_r': 169.338,
     'L0_cond_C_r': 21.456,
     'L0_cond_U': 5.108,
     'L0_ffn_W1': 4.929,
     'L0_ffn_sW1': 5.05,
     'L0_ffn_sW2': 2.788,
     'L1_cond_bq2': 6.621,
     'L1_cond_bk2': 200.0}
    for name, (base, spread) in spreads.items():
        noise = np.random.default_rng([zlib.crc32(name.encode()), seed]).standard_normal(out[name].shape)
        drawn = base * np.exp(spread * noise) if base else spread * noise
        out[name] = jnp.asarray(drawn.astype(out[name].dtype))
    for name, factor in factors.items():
        out[name] = (out[name] * factor).astype(out[name].dtype)
    return out
```

```python
from contextlib import ExitStack

import numpy as np
import concourse.bass as bass
from concourse import mybir

F32 = mybir.dt.float32
F32R = mybir.dt.float32r
U32 = mybir.dt.uint32
ALU = mybir.AluOpType
ACT = mybir.ActivationFunctionType
AX = mybir.AxisListType

P = 128
B, T = 32, 128
N = B * T
H = 512
HB = H // P
E = 8
NSH = 2
NE0 = E + NSH
TOPK = 2
STEPS = 16
CH = STEPS * B
NCH = N // CH
UNITS = NE0 * HB
SG = 4
GRP = 4
NG = B // GRP
CAP = TOPK * int(1.25 * ((N + E - 1) // E))
ST = CAP // P
ROWW = P + 1
FAR = 60000.0
SCALE = 1.0 / float(np.sqrt(np.float32(P)))
EPS_GATE = 1.1920929e-07
EPS_LN = 1e-05

R_SB1, R_B1, R_BZ, R_BR, R_BH = 0, 8, 40, 41, 42
R_SB2, R_B2, R_BQ2, R_BK2, R_FB1, R_FB2, NVEC = 43, 45, 53, 54, 55, 87, 95


def atleast(eng, sem, value):
    if isinstance(value, int) and value <= 0:
        return
    eng.wait_ge(sem, value)


def part_slot(p):
    return (p * UNITS) // (2 * STEPS)


PART_OF_SLOT = {part_slot(p): p for p in range(2 * STEPS)}
NGRP = 1 + E


def group_of(u):
    if u < NSH * HB:
        return 0, u == 0, u == NSH * HB - 1
    k = u // HB - 1
    return k, u % HB == 0, u % HB == HB - 1


def build(nc, d, out):
    with ExitStack() as ctx:
        def sb(name, shape, dt=F32):
            return ctx.enter_context(nc.sbuf_tensor(name, shape, dt))

        def sem(name):
            return ctx.enter_context(nc.semaphore(name))

        bank = [ctx.enter_context(nc.psum_tensor(f"bank{i}", [P, 512], F32)) for i in range(8)]

        w_dram = nc.dram_tensor("w_dram", (E, CH), F32, kind="Internal").ap()
        slots = nc.dram_tensor("slot_rows", (E * CAP, ROWW), F32, kind="Internal").ap()
        results = nc.dram_tensor("result_rows", (TOPK * N, P), F32, kind="Internal").ap()

        ident = sb("ident", [P, P])
        identr = sb("identr", [P, P], F32R)
        vecs = sb("vecs", [P, P])
        vecT = sb("vecT", [P, NVEC])
        iota8 = sb("iota8", [P, E])
        condT = sb("condT", [P, B])
        xT = sb("xT", [P, N])
        x1T = sb("x1T", [P, N])
        wide = sb("wide", [P, B * ROWW])
        w_hi = sb("w_hi", [P, NE0 * 2 * H], F32R)
        w_lo = sb("w_lo", [P, NE0 * 2 * H], F32R)
        raw = [sb(f"raw{i}", [P, 2 * H]) for i in range(2)]
        alphaT = sb("alphaT", [P, B])
        gates_all = sb("gates_all", [P, B * TOPK])
        zt = sb("zt", [P, ST * ROWW])
        g_f = [sb(f"g_f{i}", [P, CH]) for i in range(2)]
        g_hi = [sb(f"g_hi{i}", [P, CH], F32R) for i in range(4)]
        g_lo = [sb(f"g_lo{i}", [P, CH], F32R) for i in range(4)]

        phase_scan(nc, d, locals())
        phase_attention(nc, d, locals())
        phase_experts(nc, d, locals())
        phase_norm(nc, d, locals(), out)


def mm3(pe, out, a_hi, a_lo, b_hi, b_lo, start, stop):
    pe.matmul(out, a_hi, b_hi, start=start, stop=False, skip_group_check=True)
    pe.matmul(out, a_hi, b_lo, start=False, stop=False, skip_group_check=True)
    return pe.matmul(out, a_lo, b_hi, start=False, stop=stop, skip_group_check=True)


def phase_scan(nc, d, m):
    bank, ident, identr, vecs, vecT = m["bank"], m["ident"], m["identr"], m["vecs"], m["vecT"]
    condT, xT, x1T, wide, w_hi, w_lo, raw = (m[k] for k in ("condT", "xT", "x1T", "wide", "w_hi", "w_lo", "raw"))
    iota8, zt, g_f, g_hi, g_lo, alphaT = (m[k] for k in ("iota8", "zt", "g_f", "g_hi", "g_lo", "alphaT"))
    w_dram, slots, results = m["w_dram"], m["slots"], m["results"]
    wb = wide[:, 0:E * CH]

    with ExitStack() as ctx:
        def sb(name, shape, dt=F32):
            return ctx.enter_context(nc.sbuf_tensor(name, shape, dt))

        def sem(name):
            return ctx.enter_context(nc.semaphore(name))

        xrows = [sb(f"xrows{i}", [P, 4 * P]) for i in range(2)]
        condr = sb("condr", [B, P])
        wx = sb("wx", [P, 3 * P])
        wx_hi = sb("wx_hi", [P, 3 * P], F32R)
        wx_lo = sb("wx_lo", [P, 3 * P], F32R)
        uh = sb("uh", [P, 3 * P])
        cv = sb("cv", [P, 3 * P])
        vb = sb("vb", [P, 3 * B])
        vb_hi = sb("vb_hi", [P, 3 * B], F32R)
        vb_lo = sb("vb_lo", [P, 3 * B], F32R)
        x_hi = sb("x_hi", [P, CH], F32R)
        x_lo = sb("x_lo", [P, CH], F32R)
        h = sb("h", [P, CH])
        h_hi = sb("h_hi", [P, CH], F32R)
        h_lo = sb("h_lo", [P, CH], F32R)
        tzr = sb("tzr", [P, 2 * B])
        rh = sb("rh", [P, B])
        z = sb("z", [P, B])
        kept = sb("kept", [P, B])
        hh = sb("hh", [P, B])
        zhh = sb("zhh", [P, B])
        acc = sb("acc", [P, CH])
        tmp = sb("tmp", [P, CH])
        sbias = sb("sbias", [P, 1])
        rw = sb("rw", [P, E])
        rbb = sb("rbb", [P, E])
        lg = sb("lg", [P, 4 * E])
        mx = sb("mx", [P, 4 * 8])
        ix = sb("ix", [P, 4 * 8], U32)
        ixf = sb("ixf", [P, 4 * 2])
        lgmax = sb("lgmax", [P, 1])
        dlt = sb("dlt", [P, 4])
        th = sb("th", [P, 4])
        p0 = sb("p0", [P, 4])
        p1 = sb("p1", [P, 4])
        oh0 = sb("oh0", [P, 4 * E])
        oh1 = sb("oh1", [P, 4 * E])
        wt = sb("wt", [P, 4 * E])
        wT = sb("wT", [E, CH])
        wq1 = sb("wq1", [P, P])
        wk1 = sb("wk1", [P, P])
        bq1 = sb("bq1", [B, P])
        bk1 = sb("bk1", [B, P])
        alph = sb("alph", [B, 1])
        q1 = sb("q1", [B, P])
        k1 = sb("k1", [B, P])
        s1 = sb("s1", [B, 4])
        a1 = sb("a1", [B, P])
        e1 = sb("e1", [B, P])

        small_in = sem("small_in"); x_in = [sem("x_in0"), sem("x_in1")]; w_in = [sem("w_in0"), sem("w_in1")]
        a1_in = sem("a1_in")
        zeroed = sem("zeroed")
        ident_ready = sem("ident_ready"); setup_pe = sem("setup_pe"); setup_dve = sem("setup_dve")
        xt_pe = sem("xt_pe"); xt_done = sem("xt_done"); w_split = sem("w_split"); w_step = sem("w_step")
        zt_ready = sem("zt_ready"); a1_pe = sem("a1_pe"); a1_dve = sem("a1_dve"); a1_act = sem("a1_act")
        x_split = sem("x_split"); prefilled = sem("prefilled")
        zr_acc = sem("zr_acc"); zr_tanh = sem("zr_tanh"); rh_ready = sem("rh_ready"); z_ready = sem("z_ready")
        kept_ready = sem("kept_ready"); hh_acc = sem("hh_acc"); hh_tanh = sem("hh_tanh"); zhh_ready = sem("zhh_ready")
        h_ready = sem("h_ready")
        h_split = sem("h_split"); w1_done = sem("w1_done"); gelu_done = sem("gelu_done"); lo_ready = sem("lo_ready")
        w2_done = sem("w2_done"); y_read = sem("y_read"); acc_ready = sem("acc_ready")
        gate_acc = sem("gate_acc"); gate_step = sem("gate_step"); gate_tanh = sem("gate_tanh"); wT_acc = sem("wT_acc")
        wT_ready = sem("wT_ready"); w_out = sem("w_out"); wb_ready = sem("wb_ready")

        scan_bank = [bank[0], bank[1]]
        w1_bank = [bank[2], bank[3], bank[4]]
        y_bank = [bank[5], bank[6]]
        gate_bank = bank[7]
        x1T_tb = x1T[:].rearrange("p (b t) -> p t b", b=B)
        xT_tb = xT[:].rearrange("p (t b) -> p t b", b=B)
        GSTEPS = 18

        SMALL = 0

        def w1(part, e, hb):
            return part[:, e * 2 * H + hb * P:e * 2 * H + (hb + 1) * P]

        def w2(part, e, hb):
            return part[:, e * 2 * H + H + hb * P:e * 2 * H + H + (hb + 1) * P]

        with nc.Block() as block:
            @block.sync
            def _(sp):
                n = 0
                for dst, src in (
                    (condr[:], d["cond_1024"]),
                    (vecs[R_SB1:R_SB1 + 8, :], d["L0_ffn_sb1"].rearrange("s (m p) -> (s m) p", p=P)),
                    (vecs[R_B1:R_B1 + 32, :], d["L0_ffn_b1"].rearrange("s (m p) -> (s m) p", p=P)),
                    (vecs[R_BZ:R_BZ + 1, :], d["L0_cond_b_z"].rearrange("(a p) -> a p", a=1)),
                    (vecs[R_BR:R_BR + 1, :], d["L0_cond_b_r"].rearrange("(a p) -> a p", a=1)),
                    (vecs[R_BH:R_BH + 1, :], d["L0_cond_b"].rearrange("(a p) -> a p", a=1)),
                    (vecs[R_SB2:R_SB2 + 2, :], d["L0_ffn_sb2"]),
                    (vecs[R_B2:R_B2 + 8, :], d["L0_ffn_b2"]),
                    (vecs[R_BQ2:R_BQ2 + 1, :], d["L1_cond_bq2"].rearrange("(a p) -> a p", a=1)),
                    (vecs[R_BK2:R_BK2 + 1, :], d["L1_cond_bk2"].rearrange("(a p) -> a p", a=1)),
                    (vecs[R_FB1:R_FB1 + 32, :], d["L1_ffn_fc1_b"].rearrange("s (m p) -> (s m) p", p=P)),
                    (vecs[R_FB2:R_FB2 + 8, :], d["L1_ffn_fc2_b"]),
                    (wx[:, 0:P], d["L0_cond_W_z"]), (wx[:, P:2 * P], d["L0_cond_W_r"]), (wx[:, 2 * P:3 * P], d["L0_cond_W"]),
                    (cv[:, 0:P], d["L0_cond_C_z"]), (cv[:, P:2 * P], d["L0_cond_C_r"]), (cv[:, 2 * P:3 * P], d["L0_cond_C"]),
                    (uh[:, 0:P], d["L0_cond_U_z"]), (uh[:, P:2 * P], d["L0_cond_U_r"]), (uh[:, 2 * P:3 * P], d["L0_cond_U"]),
                    (rw[:], d["L0_ffn_rW"]),
                    (rbb[:], d["L0_ffn_rb"].rearrange("(a p) -> a p", a=1).broadcast_to([P, E])),
                ):
                    sp.dma_start(dst, src).then_inc(small_in, 16)
                    n += 16
                assert n == NSMALL
                for dst, src in (
                    (wq1[:], d["L1_cond_Wq1"]), (wk1[:], d["L1_cond_Wk1"]),
                    (bq1[:], d["L1_cond_bq1"].rearrange("(a p) -> a p", a=1).broadcast_to([B, P])),
                    (bk1[:], d["L1_cond_bk1"].rearrange("(a p) -> a p", a=1).broadcast_to([B, P])),
                    (alph[:], d["L1_cond_alpha"].rearrange("(a p) -> a p", a=1).broadcast_to([B, 1])),
                ):
                    sp.dma_start(dst, src).then_inc(a1_in, 16)
                for e in range(NE0):
                    if e >= 2:
                        sp.wait_ge(w_split, 2 * (e - 1))
                    a, b_ = (d["L0_ffn_sW1"][e], d["L0_ffn_sW2"][e]) if e < NSH else (d["L0_ffn_W1"][e - NSH], d["L0_ffn_W2"][e - NSH])
                    sp.dma_start(raw[e % 2][:, 0:H], a).then_inc(w_in[e % 2], 16)
                    sp.dma_start(raw[e % 2][:, H:2 * H].rearrange("p (m n) -> p m n", m=HB), b_.rearrange("(m p) n -> p m n", p=P)).then_inc(w_in[e % 2], 16)
                sp.wait_ge(zt_ready, 2)
                for e in range(E):
                    sp.dma_start(slots[e * CAP:(e + 1) * CAP, :].rearrange("(p n) c -> p (n c)", p=P), zt[:]).then_inc(zeroed, 16)
                rows = TOPK * N // E
                for e in range(E):
                    sp.dma_start(results[e * rows:(e + 1) * rows, :].rearrange("(p n) c -> p n c", p=P),
                                 zt[:].rearrange("p (n c) -> p n c", c=ROWW)[:, 0:rows // P, 0:P]).then_inc(zeroed, 16)

                def routing(c):
                    sp.wait_ge(wT_ready, c + 1)
                    sp.dma_start(w_dram, wT[:]).then_inc(w_out, 16)
                    sp.wait_ge(w_out, (c + 1) * 16)
                    sp.dma_start(wb, w_dram.rearrange("e n -> (e n)").rearrange("(a n) -> a n", a=1).broadcast_to([P, E * CH])).then_inc(wb_ready, 16)

                with sp.Fori(0, NCH) as c:
                    routing(c)
                sp.wait_ge(zeroed, 16 * 2 * E)

            @block.gpsimd
            def _(gp):
                gp.memset(ident[:], 0.0).then_inc(ident_ready, 1)
                gp.wait_ge(ident_ready, 1)
                gp.affine_select(out=ident[:], in_=ident[:], compare_op=ALU.not_equal, fill=1.0, base=0,
                                 pattern=[[-1, P]], channel_multiplier=1).then_inc(ident_ready, 1)
                gp.iota(iota8[:], pattern=[[1, E]], base=0, channel_multiplier=0, allow_small_or_imprecise_dtypes=True).then_inc(ident_ready, 1)
                gp.memset(zt[:], 0.0).then_inc(zt_ready, 1)
                gp.wait_ge(zt_ready, 1)
                gp.memset(zt[:].rearrange("p (n c) -> p n c", c=ROWW)[:, :, P:ROWW], FAR).then_inc(zt_ready, 1)
                for e in range(NE0):
                    gp.wait_ge(w_in[e % 2], 32 * (e // 2 + 1))
                    o = slice(e * 2 * H, (e + 1) * 2 * H)
                    gp.tensor_copy(w_hi[:, o], raw[e % 2][:]).then_inc(w_split, 1)
                    gp.wait_ge(w_split, 2 * e + 1)
                    gp.tensor_tensor(w_lo[:, o], raw[e % 2][:], w_hi[:, o], ALU.subtract).then_inc(w_split, 1)

            @block.tensor
            def _(pe):
                pe.wait_ge(ident_ready, 2)
                for k in range(B // 4):
                    pe.wait_ge(x_in[k % 2], 16 * (k // 2 + 1))
                    if k >= 2:
                        pe.wait_ge(xt_done, k - 1)
                    for j in range(4):
                        t = pe.transpose(w1_bank[k % 2][:, j * P:(j + 1) * P], xrows[k % 2][:, j * P:(j + 1) * P], ident[:])
                    t.then_inc(xt_pe, 1)
                pe.wait_ge(small_in, NSMALL)
                pe.transpose(gate_bank[:, 0:B], condr[:], ident[0:B, 0:B])
                pe.transpose(gate_bank[:, B:B + NVEC], vecs[0:NVEC, :], ident[0:NVEC, 0:NVEC]).then_inc(setup_pe, 1)
                pe.wait_ge(setup_dve, 2)
                for g in range(3):
                    t = pe.matmul(y_bank[0][:, g * B:(g + 1) * B], cv[:, g * P:(g + 1) * P], condT[:], start=(g == 0), stop=(g == 2), skip_group_check=True)
                t.then_inc(setup_pe, 1)
                pe.wait_ge(a1_in, 80)
                pe.matmul(y_bank[1][0:B, 0:P], condT[:], wq1[:], start=True, stop=True, skip_group_check=True)
                pe.matmul(y_bank[1][0:B, P:2 * P], condT[:], wk1[:], start=False, stop=True, skip_group_check=True).then_inc(a1_pe, 1)

                def prefill(g):
                    o = scan_bank[g % 2][:, 0:SG * 3 * B].rearrange("p (s c) -> p s c", s=SG)
                    xs = slice(g * SG * B, (g + 1) * SG * B)
                    for q in range(3):
                        dst = o[:, :, q * B:(q + 1) * B]
                        mm3(pe, dst, wx_hi[:, q * P:(q + 1) * P], wx_lo[:, q * P:(q + 1) * P],
                            x_hi[:, xs].rearrange("p (s b) -> p s b", b=B), x_lo[:, xs].rearrange("p (s b) -> p s b", b=B), q == 0, False)
                        for v in (vb_hi, vb_lo):
                            r = v[:, q * B:(q + 1) * B].unsqueeze(1).broadcast_to([P, SG, B])
                            t = pe.matmul(dst, identr[:], r, start=False, stop=False, skip_group_check=True)
                    t.then_inc(prefilled, 1)

                def scan_part(i, p):
                    t, half = p // 2, p % 2
                    o = scan_bank[(t // SG) % 2][:, (t % SG) * 3 * B:(t % SG + 1) * 3 * B]
                    if half == 0:
                        hp = h[:, ((t - 1) % STEPS) * B:((t - 1) % STEPS + 1) * B]
                        atleast(pe, h_ready, STEPS * i + t + 1)
                        pe.matmul(o[:, B:2 * B], uh[:, P:2 * P], hp, start=False, stop=False, skip_group_check=True)
                        pe.matmul(o[:, 0:B], uh[:, 0:P], hp, start=False, stop=False, skip_group_check=True).then_inc(zr_acc, 1)
                        if t % SG == 0 and t + SG < STEPS:
                            prefill(t // SG + 1)
                    else:
                        atleast(pe, rh_ready, STEPS * i + t + 1)
                        pe.matmul(o[:, 2 * B:3 * B], uh[:, 2 * P:3 * P], rh[:], start=False, stop=False, skip_group_check=True).then_inc(hh_acc, 1)

                def first_layer(c, u):
                    e, hb = u // HB, u % HB
                    if u >= 3:
                        atleast(pe, gelu_done, 2 * (UNITS * c + u - 2))
                    mm3(pe, w1_bank[u % 3][:], w1(w_hi, e, hb), w1(w_lo, e, hb), h_hi[:], h_lo[:], True, True).then_inc(w1_done, 1)

                def second_layer(c, u):
                    e, hb = u // HB, u % HB
                    k, first, last = group_of(u)
                    if first:
                        atleast(pe, y_read, NGRP * c + max(k - 1, 0))
                    pe.wait_ge(lo_ready, UNITS * c + u + 1)
                    mm3(pe, y_bank[k % 2][:], w2(w_hi, e, hb), w2(w_lo, e, hb), g_hi[u % 4][:], g_lo[u % 4][:], first, last).then_inc(w2_done, 1)

                def gates(i):
                    pe.wait_ge(h_ready, STEPS * (i + 1) + 1)
                    atleast(pe, wT_ready, i)
                    for k in range(4):
                        t = pe.matmul(gate_bank[:, k * E:(k + 1) * E], h[:, k * P:(k + 1) * P], rw[:], start=(k == 0), stop=(k == 3), skip_group_check=True)
                    t.then_inc(gate_acc, 1)

                def body(i, c, scan, ffn, more):
                    if ffn:
                        pe.wait_ge(h_split, 2 * (c + 1))
                    for u in range(UNITS):
                        if scan and u in PART_OF_SLOT:
                            scan_part(i, PART_OF_SLOT[u])
                        if ffn:
                            first_layer(c, u)
                            if u >= 2:
                                second_layer(c, u - 2)
                            if u == 4:
                                pe.wait_ge(gate_step, GSTEPS * (c + 1))
                                for k in range(4):
                                    t = pe.transpose(gate_bank[0:E, k * P:(k + 1) * P], wt[:, k * E:(k + 1) * E], ident[:])
                                t.then_inc(wT_acc, 1)
                    if ffn:
                        second_layer(c, UNITS - 2)
                    if more:
                        pe.wait_ge(x_split, 2 * (i + 2))
                        prefill(0)
                    if scan:
                        gates(i)
                    if ffn:
                        second_layer(c, UNITS - 1)

                pe.wait_ge(setup_dve, SETUP_DVE)
                pe.wait_ge(x_split, 2)
                prefill(0)
                body(0, None, True, False, True)
                pe.wait_ge(w_split, 2 * NE0)
                body(1, 0, True, True, True)
                with pe.Fori(2, NCH - 1) as i:
                    body(i, i - 1, True, True, True)
                body(NCH - 1, NCH - 2, True, True, False)
                body(None, NCH - 1, False, True, False)
                pe.wait_ge(a1_dve, A1_DVE)
                pe.transpose(gate_bank[:, 0:B], a1[:], ident[0:B, 0:B]).then_inc(a1_pe, 1)

            @block.scalar
            def _(act):
                act.wait_ge(ident_ready, 3)
                act.activation(th[:, 0:1], iota8[:, 0:1], ACT.Gelu).then_inc(gate_tanh, 1)
                for k in range(B // 4):
                    if k >= 2:
                        act.wait_ge(xt_pe, k - 1)
                    act.dma_start(xrows[k % 2][:].rearrange("p (b c) -> p b c", b=4),
                                  d["x"][4 * k:4 * k + 4].rearrange("b t c -> t b c")).then_inc(x_in[k % 2], 16)

                def scan_part(i, p):
                    t, half = p // 2, p % 2
                    o = scan_bank[(t // SG) % 2][:, (t % SG) * 3 * B:(t % SG + 1) * 3 * B]
                    if half == 0:
                        act.wait_ge(zr_acc, STEPS * i + t + 1)
                        act.activation(tzr[:], o[:, 0:2 * B], ACT.Tanh, scale=0.5).then_inc(zr_tanh, 1)
                    else:
                        act.wait_ge(hh_acc, STEPS * i + t + 1)
                        act.activation(hh[:], o[:, 2 * B:3 * B], ACT.Tanh).then_inc(hh_tanh, 1)

                def gelu(c, u):
                    act.wait_ge(w1_done, UNITS * c + u + 1)
                    atleast(act, lo_ready, UNITS * c + max(u - 1, 0))
                    atleast(act, w2_done, UNITS * c + max(u - 3, 0))
                    bias = vecT[:, R_SB1 + u:R_SB1 + u + 1]
                    act.activation(g_f[u % 2][:], w1_bank[u % 3][:], ACT.Gelu, bias=bias).then_inc(gelu_done, 1)
                    act.activation(g_hi[u % 4][:], w1_bank[u % 3][:], ACT.Gelu, bias=bias).then_inc(gelu_done, 1)

                def body(i, c, scan, ffn):
                    for u in range(UNITS + 1):
                        if scan and u in PART_OF_SLOT:
                            scan_part(i, PART_OF_SLOT[u])
                        if ffn and u >= 1:
                            gelu(c, u - 1)
                        if ffn and u == 1:
                            act.wait_ge(gate_step, GSTEPS * c + 6)
                            act.activation(th[:], dlt[:], ACT.Tanh, scale=0.5).then_inc(gate_tanh, 1)
                        if ffn and u == 5:
                            act.wait_ge(wT_acc, c + 1)
                            act.activation(wT[:], gate_bank[0:E, :], ACT.Copy).then_inc(wT_ready, 1)

                body(0, None, True, False)
                body(1, 0, True, True)
                with act.Fori(2, NCH - 1) as i:
                    body(i, i - 1, True, True)
                body(NCH - 1, NCH - 2, True, True)
                body(None, NCH - 1, False, True)
                act.wait_ge(a1_dve, 5)
                act.activation(e1[:], a1[:], ACT.Exp, bias=s1[:, 1:2], accum_out=s1[:, 2:3]).then_inc(a1_act, 1)

            @block.vector
            def _(dve):
                dve.memset(h[:, CH - B:CH], 0.0).then_inc(h_ready, 1)
                for k in range(B // 4):
                    dve.wait_ge(xt_pe, k + 1)
                    dve.tensor_copy(xT_tb[:, :, 4 * k:4 * k + 4], w1_bank[k % 2][:].rearrange("p (b t) -> p t b", b=4)).then_inc(xt_done, 1)
                dve.wait_ge(setup_pe, 1)
                dve.tensor_copy(condT[:], gate_bank[:, 0:B]).then_inc(setup_dve, 1)
                dve.tensor_copy(vecT[:], gate_bank[:, B:B + NVEC]).then_inc(setup_dve, 1)
                dve.tensor_scalar(uh[:, 2 * P:3 * P], uh[:, 2 * P:3 * P], 0.5, None, ALU.mult).then_inc(setup_dve, 1)
                dve.tensor_copy(wx_hi[:], wx[:]).then_inc(setup_dve, 1)
                dve.wait_ge(ident_ready, 3)
                dve.tensor_copy(identr[:], ident[:]).then_inc(setup_dve, 1)
                dve.wait_ge(setup_dve, 5)
                dve.tensor_tensor(wx_lo[:], wx[:], wx_hi[:], ALU.subtract).then_inc(setup_dve, 1)
                dve.tensor_tensor(sbias[:], vecT[:, R_SB2:R_SB2 + 1], vecT[:, R_SB2 + 1:R_SB2 + 2], ALU.add).then_inc(setup_dve, 1)
                dve.wait_ge(setup_dve, 7)
                dve.tensor_scalar(sbias[:], sbias[:], 0.5, None, ALU.mult).then_inc(setup_dve, 1)
                dve.wait_ge(setup_pe, 2)
                for g, r in enumerate((R_BZ, R_BR, R_BH)):
                    dve.tensor_scalar(vb[:, g * B:(g + 1) * B], y_bank[0][:, g * B:(g + 1) * B], vecT[:, r:r + 1], None, ALU.add).then_inc(setup_dve, 1)
                dve.wait_ge(setup_dve, 11)
                dve.tensor_copy(vb_hi[:], vb[:]).then_inc(setup_dve, 1)
                dve.wait_ge(setup_dve, 12)
                dve.tensor_tensor(vb_lo[:], vb[:], vb_hi[:], ALU.subtract).then_inc(setup_dve, 1)
                dve.wait_ge(a1_pe, 1)
                dve.tensor_tensor(q1[:], y_bank[1][0:B, 0:P], bq1[:], ALU.add).then_inc(a1_dve, 1)
                dve.tensor_tensor(k1[:], y_bank[1][0:B, P:2 * P], bk1[:], ALU.add).then_inc(a1_dve, 1)
                dve.wait_ge(a1_dve, 2)
                dve.tensor_tensor_reduce(out=e1[:], in0=q1[:], in1=k1[:], scale=1.0, scalar=0.0, op0=ALU.mult, op1=ALU.add,
                                         accum_out=s1[:, 0:1]).then_inc(a1_dve, 1)
                dve.wait_ge(a1_dve, 3)
                dve.tensor_scalar(a1[:], s1[:, 0:1].broadcast_to([B, P]), SCALE, None, ALU.mult).then_inc(a1_dve, 1)
                dve.wait_ge(a1_dve, 4)
                dve.tensor_reduce(s1[:, 1:2], a1[:], AX.X, ALU.max, negate=True).then_inc(a1_dve, 1)

                def split_x(i):
                    atleast(dve, prefilled, SG * i)
                    src = xT[:, bass.ds(i * CH, CH)]
                    dve.tensor_scalar(x_hi[:], src, 1.0, None, ALU.mult).then_inc(x_split, 1)
                    dve.wait_ge(x_split, 2 * i + 1)
                    dve.tensor_tensor(x_lo[:], src, x_hi[:], ALU.subtract).then_inc(x_split, 1)

                def scan_part(i, p):
                    t, half = p // 2, p % 2
                    n = STEPS * i + t + 1
                    hp = h[:, ((t - 1) % STEPS) * B:((t - 1) % STEPS + 1) * B]
                    if half == 0:
                        dve.wait_ge(zr_tanh, n)
                        dve.scalar_tensor_tensor(out=rh[:], in0=tzr[:, B:2 * B], scalar=1.0, in1=hp, op0=ALU.add, op1=ALU.mult).then_inc(rh_ready, 1)
                        dve.tensor_scalar(z[:], tzr[:, 0:B], 0.5, 0.5, ALU.mult, ALU.add).then_inc(z_ready, 1)
                        dve.wait_ge(z_ready, n)
                        dve.scalar_tensor_tensor(out=kept[:], in0=z[:], scalar=-1.0, in1=hp, op0=ALU.add, op1=ALU.mult).then_inc(kept_ready, 1)
                    else:
                        dve.wait_ge(hh_tanh, n)
                        dve.tensor_tensor(zhh[:], z[:], hh[:], ALU.mult).then_inc(zhh_ready, 1)
                        dve.wait_ge(zhh_ready, n)
                        dve.wait_ge(kept_ready, n)
                        dve.tensor_tensor(h[:, t * B:(t + 1) * B], zhh[:], kept[:], ALU.subtract).then_inc(h_ready, 1)

                def low_part(c, u):
                    dve.wait_ge(gelu_done, 2 * (UNITS * c + u + 1))
                    atleast(dve, w2_done, UNITS * c + max(u - 3, 0))
                    dve.tensor_tensor(g_lo[u % 4][:], g_f[u % 2][:], g_hi[u % 4][:], ALU.subtract).then_inc(lo_ready, 1)

                def combine(c, k):
                    last = NSH * HB + k * HB
                    dve.wait_ge(w2_done, UNITS * c + last)
                    src = xT[:, bass.ds(c * CH, CH)]
                    y = y_bank[k % 2][:]
                    atleast(dve, acc_ready, NGRP * c + k)
                    if k == 0:
                        dve.scalar_tensor_tensor(out=acc[:], in0=y, scalar=0.5, in1=src, op0=ALU.mult, op1=ALU.add).then_inc(y_read, 1)
                        dve.wait_ge(y_read, NGRP * c + 1)
                        dve.tensor_scalar(acc[:], acc[:], sbias[:], None, ALU.add).then_inc(acc_ready, 1)
                        return
                    if k == 1:
                        dve.wait_ge(wb_ready, 16 * (c + 1))
                    dve.scalar_tensor_tensor(out=tmp[:], in0=y, scalar=vecT[:, R_B2 + k - 1:R_B2 + k], in1=wb[:, (k - 1) * CH:k * CH],
                                             op0=ALU.add, op1=ALU.mult).then_inc(y_read, 1)
                    dve.wait_ge(y_read, NGRP * c + k + 1)
                    if k < E:
                        dve.tensor_tensor(acc[:], acc[:], tmp[:], ALU.add).then_inc(acc_ready, 1)
                    else:
                        dve.tensor_tensor(x1T_tb[:, bass.ds(c * STEPS, STEPS), :], acc[:].rearrange("p (t b) -> p t b", b=B),
                                          tmp[:].rearrange("p (t b) -> p t b", b=B), ALU.add).then_inc(acc_ready, 1)

                def v3(a, w):
                    return a[:].rearrange("p (k e) -> p k e", e=w)

                def gate_a(c):
                    n = GSTEPS * c
                    dve.wait_ge(gate_acc, c + 1)
                    dve.tensor_tensor(v3(lg, E), gate_bank[:, 0:4 * E].rearrange("p (k e) -> p k e", e=E),
                                      rbb[:].unsqueeze(1).broadcast_to([P, 4, E]), ALU.add).then_inc(gate_step, 1)
                    dve.wait_ge(gate_step, n + 1)
                    dve.tensor_scalar(lgmax[:], lg[:, 0:1], 1.0, None, ALU.mult)
                    for k in range(4):
                        dve.max(mx[:, k * 8:(k + 1) * 8], lg[:, k * E:(k + 1) * E]).then_inc(gate_step, 1)
                    dve.wait_ge(gate_step, n + 5)
                    dve.tensor_tensor(dlt[:].unsqueeze(2), v3(mx, 8)[:, :, 0:1], v3(mx, 8)[:, :, 1:2], ALU.subtract).then_inc(gate_step, 1)
                    for k in range(4):
                        dve.max_index(ix[:, k * 8:(k + 1) * 8], mx[:, k * 8:(k + 1) * 8], lg[:, k * E:(k + 1) * E]).then_inc(gate_step, 1)
                    dve.wait_ge(gate_step, n + 10)
                    dve.tensor_scalar(v3(ixf, 2), v3(ix, 8)[:, :, 0:2], 1.0, None, ALU.mult).then_inc(gate_step, 1)

                def gate_b(c):
                    n = GSTEPS * c
                    dve.wait_ge(gate_tanh, c + 2)
                    dve.tensor_scalar(p0[:], th[:], 0.5, 0.5, ALU.mult, ALU.add).then_inc(gate_step, 1)
                    dve.tensor_scalar(p1[:], th[:], -0.5, 0.5, ALU.mult, ALU.add).then_inc(gate_step, 1)
                    dve.wait_ge(gate_step, n + 11)
                    io = iota8[:].unsqueeze(1).broadcast_to([P, 4, E])
                    for q, oh in enumerate((oh0, oh1)):
                        dve.tensor_tensor(v3(oh, E), io, v3(ixf, 2)[:, :, q:q + 1].broadcast_to([P, 4, E]), ALU.is_equal).then_inc(gate_step, 1)
                    dve.wait_ge(gate_step, n + 15)
                    for oh, p in ((oh0, p0), (oh1, p1)):
                        dve.tensor_tensor(v3(oh, E), v3(oh, E), p[:].unsqueeze(2).broadcast_to([P, 4, E]), ALU.mult).then_inc(gate_step, 1)
                    dve.wait_ge(gate_step, n + 17)
                    dve.tensor_tensor(wt[:], oh0[:], oh1[:], ALU.add).then_inc(gate_step, 1)

                def split_h(i, c):
                    dve.wait_ge(h_ready, STEPS * (i + 1) + 1)
                    if c is not None:
                        dve.wait_ge(w1_done, UNITS * (c + 1))
                    dve.tensor_copy(h_hi[:], h[:]).then_inc(h_split, 1)
                    dve.wait_ge(h_split, 2 * i + 1)
                    dve.tensor_tensor(h_lo[:], h[:], h_hi[:], ALU.subtract).then_inc(h_split, 1)

                def body(i, c, scan, ffn, more):
                    for u in range(UNITS + 1):
                        if scan and u in PART_OF_SLOT:
                            scan_part(i, PART_OF_SLOT[u])
                        if ffn and u >= 1:
                            low_part(c, u - 1)
                        if ffn and u == 1:
                            gate_a(c)
                        if ffn and u == 3:
                            gate_b(c)
                        if ffn:
                            for k in range(NGRP - 1):
                                if u == NSH * HB + k * HB + 2:
                                    combine(c, k)
                        if more and u == part_slot(2 * (STEPS - SG)) + 2:
                            split_x(i + 1)
                    if scan:
                        split_h(i, c)
                    if ffn:
                        combine(c, NGRP - 1)

                split_x(0)
                body(0, None, True, False, True)
                body(1, 0, True, True, True)
                with dve.Fori(2, NCH - 1) as i:
                    body(i, i - 1, True, True, True)
                body(NCH - 1, NCH - 2, True, True, False)
                body(None, NCH - 1, False, True, False)
                dve.wait_ge(a1_act, 1)
                dve.reciprocal(s1[:, 3:4], s1[:, 2:3]).then_inc(a1_dve, 1)
                dve.wait_ge(a1_dve, 6)
                dve.tensor_scalar(a1[:], e1[:], s1[:, 3:4], alph[:], ALU.mult, ALU.mult).then_inc(a1_dve, 1)
                dve.wait_ge(a1_pe, 2)
                dve.tensor_copy(alphaT[:], gate_bank[:, 0:B])


NSMALL = 23 * 16
SETUP_DVE = 13
A1_DVE = 7


def phase_attention(nc, d, m):
    bank, ident, identr, vecT = m["bank"], m["ident"], m["identr"], m["vecT"]
    condT, xT, x1T, wide, alphaT, iota8 = (m[k] for k in ("condT", "xT", "x1T", "wide", "alphaT", "iota8"))
    w_hi, w_lo, raw, slots = m["w_hi"], m["w_lo"], m["raw"], m["slots"]
    gates_all = m["gates_all"]
    x1rows, hid = xT, wide
    hid3 = hid[:].rearrange("p (b c) -> p b c", c=ROWW)
    GT = GRP * P
    ME = GRP * TOPK * E

    with ExitStack() as ctx:
        def sb(name, shape, dt=F32):
            return ctx.enter_context(nc.sbuf_tensor(name, shape, dt))

        def sem(name):
            return ctx.enter_context(nc.semaphore(name))

        wv1 = sb("wv1", [P, P])
        bvb = sb("bvb", [P, P])
        wg = sb("wg", [P, E])
        lowtri = sb("lowtri", [P, P])
        lowtri_r = sb("lowtri_r", [P, P], F32R)
        ones_r = sb("ones_r", [P, P], F32R)
        touched = sb("touched2", [P, 1])
        xg = sb("xg", [P, GT])
        xg_hi = sb("xg_hi", [P, GT], F32R)
        xg_lo = sb("xg_lo", [P, GT], F32R)
        condg = sb("condg", [P, GRP])
        qT = sb("qT", [P, GT])
        kT = sb("kT", [P, GT])
        v = sb("v", [P, GT])
        smax = sb("smax", [P, GRP])
        nsmax = sb("nsmax", [P, GRP])
        pr = sb("pr", [P, GT])
        rs = sb("rs", [P, GRP])
        rinv = sb("rinv", [P, GRP])
        am = sb("am", [P, GT])
        amT = sb("amT", [P, GT])
        hg = sb("hg", [P, GRP * ROWW])
        hg3 = hg[:].rearrange("p (b c) -> p b c", c=ROWW)
        hT = sb("hT", [P, GT])
        lmax = sb("lmax", [P, GRP]); lsh = sb("lsh", [P, GRP * E]); lex = sb("lex", [P, GRP * E])
        lsum = sb("lsum", [P, GRP]); lrec = sb("lrec", [P, GRP]); sc = sb("sc", [P, GRP * E])
        mx = sb("mx8", [P, GRP * 8]); ix = sb("ix8", [P, GRP * 8], U32); ixf = sb("ixf8", [P, GRP * TOPK])
        den = sb("den", [P, GRP]); dinv = sb("dinv", [P, GRP]); gt = sb("gt", [P, GRP * TOPK])
        mask = sb("mask", [P, ME], F32R)
        run = sb("run", [P, TOPK * E])
        loc = sb("loc", [P, ME]); sel = sb("sel", [P, ME])
        rank = sb("rank", [P, GRP * TOPK])
        over = sb("over", [P, GRP]); pos = sb("pos", [P, GRP]); keep = sb("keep", [P, GRP])
        posi = sb("posi", [P, GRP], U32)
        mask1 = sb("mask1", [P, B * E]); rank1 = sb("rank1", [P, B]); ex1 = sb("ex1", [P, B])
        sel1 = sb("sel1", [P, B * E]); over1 = sb("over1", [P, B]); pos1 = sb("pos1", [P, B])
        keep1 = sb("keep1", [P, B]); pos1i = sb("pos1i", [P, B], U32)

        att_in = sem("att_in"); w_step = sem("att_w"); w_conv = sem("att_w_ready"); const_step = sem("const_step")
        x_ready = sem("x_ready"); cond_ready = sem("cond_ready"); q_acc = sem("q_acc"); k_acc = sem("k_acc"); v_acc = sem("v_acc")
        q_ready = sem("q_ready"); k_ready = sem("k_ready"); v_ready = sem("v_ready"); rows_acc = sem("rows_acc"); rows_done = sem("rows_done")
        s_acc = sem("s_acc"); smax_ready = sem("smax_ready"); p_ready = sem("p_ready"); a_step = sem("a_step"); a_ready = sem("a_ready")
        aT_acc = sem("aT_acc"); aT_ready = sem("aT_ready"); hid_acc = sem("hid_acc"); hid_copied = sem("hid_copied")
        hidT_acc = sem("hidT_acc"); hidT_ready = sem("hidT_ready"); logit_acc = sem("logit_acc"); hid_kept = sem("hid_kept")
        r_step = sem("r_step"); l_exp = sem("l_exp"); rank_acc = sem("rank_acc"); id_step = sem("id_step")
        pos_ready = sem("pos_ready"); sent0 = sem("sent0"); f_step = sem("f_step"); sent1 = sem("sent1"); touch = sem("touch2")

        LOADS = 6
        bq, bk, bv_, br, bs, ba, bh, bm = bank
        WQ, WK, WV = 0, 1, 2

        def v3(a, w):
            return a[:].rearrange("p (k e) -> p k e", e=w)

        mask4 = mask[:].rearrange("p (k q e) -> p k q e", q=TOPK, e=E)

        with nc.Block() as block:
            @block.sync
            def _(sp):
                for dst, src in ((raw[0][:, 0:P], d["L1_cond_Wq2"]), (raw[0][:, P:2 * P], d["L1_cond_Wk2"]),
                                 (raw[0][:, 2 * P:3 * P], d["L1_cond_Wv"][P:2 * P, :]), (wv1[:], d["L1_cond_Wv"][0:P, :]),
                                 (bvb[:], d["L1_cond_bv"].rearrange("(a p) -> a p", a=1).broadcast_to([P, P])),
                                 (wg[:], d["L1_ffn_wg"])):
                    sp.dma_start(dst, src).then_inc(att_in, 16)

            @block.gpsimd
            def _(gp):
                gp.memset(lowtri[:], 1.0).then_inc(const_step, 1)
                gp.wait_ge(const_step, 1)
                gp.affine_select(out=lowtri[:], in_=lowtri[:], compare_op=ALU.is_ge, fill=0.0, base=0, pattern=[[1, P]],
                                 channel_multiplier=-1).then_inc(const_step, 1)
                gp.iota(hid3[:, :, P:ROWW], pattern=[[P, B], [1, 1]], base=N, channel_multiplier=1, allow_small_or_imprecise_dtypes=True).then_inc(id_step, 1)
                gp.iota(hg3[:, :, P:ROWW], pattern=[[P, GRP], [1, 1]], base=-GT, channel_multiplier=1, allow_small_or_imprecise_dtypes=True).then_inc(id_step, 1)
                last_slot = gp.to_reg(E * CAP - 1)
                with gp.Fori(0, NG) as g:
                    gp.wait_ge(pos_ready, g + 1)
                    gp.tensor_tensor(touched[:], iota8[:, 0:1], iota8[:, 0:1], ALU.add).then_inc(touch, 1)
                    for j in range(GRP):
                        gp.indirect_dma_start(out=slots, out_offset=bass.IndirectOffsetOnAxis(ap=posi[:, j:j + 1], axis=0),
                                              in_=hg[:, j * ROWW:(j + 1) * ROWW], in_offset=None,
                                              bounds_check=last_slot, oob_is_err=False).then_inc(sent0, 16)
                gp.wait_ge(f_step, FSTEPS)
                for b in range(B):
                    gp.indirect_dma_start(out=slots, out_offset=bass.IndirectOffsetOnAxis(ap=pos1i[:, b:b + 1], axis=0),
                                          in_=hid[:, b * ROWW:(b + 1) * ROWW], in_offset=None,
                                          bounds_check=last_slot, oob_is_err=False).then_inc(sent1, 16)
                gp.wait_ge(sent0, 16 * B)
                gp.wait_ge(sent1, 16 * B)

            @block.tensor
            def _(pe):
                pe.wait_ge(w_conv, 4)
                pe.wait_ge(att_in, 16 * LOADS)

                def wpart(t, q):
                    return t[:, q * P:(q + 1) * P]

                with pe.Fori(0, NG) as g:
                    pe.wait_ge(x_ready, 3 * (g + 1))
                    mm3(pe, bq[:], wpart(w_hi, WQ), wpart(w_lo, WQ), xg_hi[:], xg_lo[:], True, True).then_inc(q_acc, 1)
                    mm3(pe, bk[:], wpart(w_hi, WK), wpart(w_lo, WK), xg_hi[:], xg_lo[:], True, True).then_inc(k_acc, 1)
                    pe.wait_ge(cond_ready, g + 1)
                    for j in range(GRP):
                        o = bv_[:, j * P:(j + 1) * P]
                        js = slice(j * P, (j + 1) * P)
                        mm3(pe, o, xg_hi[:, js], xg_lo[:, js], wpart(w_hi, WV), wpart(w_lo, WV), j == 0, False)
                        t = pe.matmul(o, condg[:, j:j + 1].broadcast_to([P, P]), wv1[:], start=False, stop=True, skip_group_check=True)
                    t.then_inc(v_acc, 1)
                    for j in range(GRP):
                        t = pe.transpose(br[:, j * P:(j + 1) * P], xg[:, j * P:(j + 1) * P], ident[:])
                    t.then_inc(rows_acc, 1)
                    pe.wait_ge(q_ready, g + 1)
                    pe.wait_ge(k_ready, g + 1)
                    for j in range(GRP):
                        js = slice(j * P, (j + 1) * P)
                        t = pe.matmul(bs[:, js], qT[:, js], kT[:, js], start=(j == 0), stop=True, skip_group_check=True)
                    t.then_inc(s_acc, 1)
                    pe.wait_ge(a_ready, GRP * (g + 1))
                    for j in range(GRP):
                        js = slice(j * P, (j + 1) * P)
                        t = pe.transpose(ba[:, js], am[:, js], ident[:])
                    t.then_inc(aT_acc, 1)
                    pe.wait_ge(aT_ready, g + 1)
                    pe.wait_ge(v_ready, g + 1)
                    for j in range(GRP):
                        js = slice(j * P, (j + 1) * P)
                        t = pe.matmul(bh[:, js], amT[:, js], v[:, js], start=(j == 0), stop=True, skip_group_check=True)
                    t.then_inc(hid_acc, 1)
                    pe.wait_ge(hid_copied, g + 1)
                    for j in range(GRP):
                        t = pe.transpose(ba[:, j * P:(j + 1) * P], hg[:, j * ROWW:j * ROWW + P], ident[:])
                    t.then_inc(hidT_acc, 1)
                    pe.wait_ge(hidT_ready, g + 1)
                    for j in range(GRP):
                        t = pe.matmul(bm[:, j * E:(j + 1) * E], hT[:, j * P:(j + 1) * P], wg[:], start=(j == 0), stop=True, skip_group_check=True)
                    t.then_inc(logit_acc, 1)
                    pe.wait_ge(r_step, RSTEPS * g + R_MASKS)
                    cum = bq[:, 0:ME]
                    pe.matmul(cum, lowtri_r[:], mask[:], start=True, stop=False, skip_group_check=True)
                    TE = TOPK * E
                    for j in range(GRP - 1):
                        later = cum[:, (j + 1) * TE:ME].rearrange("p (k c) -> p k c", c=TE)
                        pe.matmul(later, ones_r[:], mask[:, j * TE:(j + 1) * TE].unsqueeze(1).broadcast_to([P, GRP - 1 - j, TE]),
                                  start=False, stop=False, skip_group_check=True)
                    for j in range(GRP):
                        t = pe.matmul(bq[:, ME:ME + TE], ones_r[:], mask[:, j * TE:(j + 1) * TE], start=False, stop=(j == GRP - 1), skip_group_check=True)
                    t.then_inc(rank_acc, 1)

            @block.scalar
            def _(act):
                def turn(g):
                    act.wait_ge(q_acc, g + 1)
                    act.activation(qT[:], bq[:], ACT.Identity, bias=vecT[:, R_BQ2:R_BQ2 + 1]).then_inc(q_ready, 1)
                    act.wait_ge(k_acc, g + 1)
                    act.activation(kT[:], bk[:], ACT.Identity, bias=vecT[:, R_BK2:R_BK2 + 1]).then_inc(k_ready, 1)
                    act.wait_ge(smax_ready, 2 * (g + 1))
                    for j in range(GRP):
                        js = slice(j * P, (j + 1) * P)
                        act.activation(pr[:, js], bs[:, js], ACT.Exp, bias=nsmax[:, j:j + 1], scale=SCALE, accum_out=rs[:, j:j + 1]).then_inc(p_ready, 1)
                    act.wait_ge(aT_acc, g + 1)
                    act.activation(amT[:], ba[:], ACT.Copy).then_inc(aT_ready, 1)
                    act.wait_ge(hid_acc, g + 1)
                    atleast(act, sent0, 16 * GRP * g)
                    act.activation(hg3[:, :, 0:P], bh[:].rearrange("p (b c) -> p b c", c=P), ACT.Copy).then_inc(hid_copied, 1)
                    act.wait_ge(hidT_acc, g + 1)
                    act.activation(hT[:], ba[:], ACT.Copy).then_inc(hidT_ready, 1)
                    act.wait_ge(r_step, RSTEPS * g + R_SHIFTED)
                    act.activation(lex[:], lsh[:], ACT.Exp).then_inc(l_exp, 1)

                turn(0)
                with act.Fori(1, NG) as g:
                    turn(g)

            @block.vector
            def _(dve):
                dve.memset(run[:], 0.0).then_inc(w_step, 1)
                dve.wait_ge(const_step, 2)
                dve.tensor_copy(lowtri_r[:], lowtri[:]).then_inc(w_conv, 1)
                dve.tensor_scalar(ones_r[:], lowtri[:], 0.0, 1.0, ALU.mult, ALU.add).then_inc(w_conv, 1)
                dve.wait_ge(att_in, 16 * LOADS)
                dve.tensor_copy(w_hi[:, 0:3 * P], raw[0][:, 0:3 * P]).then_inc(w_conv, 1)
                dve.wait_ge(w_conv, 3)
                dve.tensor_tensor(w_lo[:, 0:3 * P], raw[0][:, 0:3 * P], w_hi[:, 0:3 * P], ALU.subtract).then_inc(w_conv, 1)
                dve.wait_ge(id_step, 2)
                dve.wait_ge(w_step, 1)
                def turn(g):
                    n = RSTEPS * g
                    cols = bass.ds(g * GT, GT)
                    atleast(dve, rank_acc, g)
                    dve.tensor_scalar(xg_hi[:], x1T[:, cols], 1.0, None, ALU.mult).then_inc(x_ready, 1)
                    dve.tensor_scalar(xg[:], x1T[:, cols], 1.0, None, ALU.mult).then_inc(x_ready, 1)
                    dve.tensor_scalar(condg[:], condT[:, bass.ds(g * GRP, GRP)], 1.0, None, ALU.mult).then_inc(cond_ready, 1)
                    dve.wait_ge(x_ready, 3 * g + 1)
                    dve.tensor_tensor(xg_lo[:], x1T[:, cols], xg_hi[:], ALU.subtract).then_inc(x_ready, 1)
                    dve.wait_ge(v_acc, g + 1)
                    dve.tensor_tensor(v3(v, P), bv_[:].rearrange("p (k c) -> p k c", c=P), bvb[:].unsqueeze(1).broadcast_to([P, GRP, P]), ALU.add).then_inc(v_ready, 1)
                    dve.wait_ge(s_acc, g + 1)
                    dve.tensor_reduce(smax[:], bs[:].rearrange("p (k c) -> p k c", c=P), AX.X, ALU.max).then_inc(smax_ready, 1)
                    dve.wait_ge(smax_ready, 2 * g + 1)
                    dve.tensor_scalar(nsmax[:], smax[:], -SCALE, None, ALU.mult).then_inc(smax_ready, 1)
                    dve.wait_ge(rows_acc, g + 1)
                    dve.tensor_scalar(x1rows[:, cols], br[:], 1.0, None, ALU.mult).then_inc(rows_done, 1)
                    dve.wait_ge(p_ready, GRP * (g + 1))
                    dve.reciprocal(rinv[:], rs[:]).then_inc(a_step, 1)
                    dve.wait_ge(a_step, g + 1)
                    for j in range(GRP):
                        js = slice(j * P, (j + 1) * P)
                        dve.tensor_scalar(am[:, js], pr[:, js], rinv[:, j:j + 1], alphaT[:, bass.ds(g * GRP + j, 1)], ALU.mult, ALU.subtract).then_inc(a_ready, 1)
                    dve.wait_ge(hid_copied, g + 1)
                    dve.tensor_scalar(hid3[:, bass.ds(g * GRP, GRP), 0:P], hg3[:, :, 0:P], 1.0, None, ALU.mult).then_inc(hid_kept, 1)
                    dve.tensor_scalar(hg3[:, :, P:ROWW], hg3[:, :, P:ROWW], float(GT), None, ALU.add).then_inc(hid_kept, 1)

                    step = [0]

                    def did(ins):
                        step[0] += 1
                        ins.then_inc(r_step, 1)
                        return step[0]

                    def after(k):
                        dve.wait_ge(r_step, n + k)

                    lg = bm[:, 0:GRP * E].rearrange("p (k e) -> p k e", e=E)
                    dve.wait_ge(logit_acc, g + 1)
                    k = did(dve.tensor_reduce(lmax[:], lg, AX.X, ALU.max))
                    after(k)
                    k = did(dve.tensor_tensor(v3(lsh, E), lg, lmax[:].unsqueeze(2).broadcast_to([P, GRP, E]), ALU.subtract))
                    assert k == R_SHIFTED
                    dve.wait_ge(l_exp, g + 1)
                    k = did(dve.tensor_reduce(lsum[:], v3(lex, E), AX.X, ALU.add))
                    after(k)
                    k = did(dve.reciprocal(lrec[:], lsum[:]))
                    after(k)
                    k = did(dve.tensor_tensor(v3(sc, E), v3(lex, E), lrec[:].unsqueeze(2).broadcast_to([P, GRP, E]), ALU.mult))
                    after(k)
                    k = did(dve.tensor_scalar(lmax[:], v3(sc, E)[:, :, 0], 1.0, None, ALU.mult))
                    for j in range(GRP):
                        k = did(dve.max(mx[:, j * 8:(j + 1) * 8], sc[:, j * E:(j + 1) * E]))
                    after(k)
                    k0 = did(dve.tensor_tensor(den[:].unsqueeze(2), v3(mx, 8)[:, :, 0:1], v3(mx, 8)[:, :, 1:2], ALU.add))
                    for j in range(GRP):
                        k = did(dve.max_index(ix[:, j * 8:(j + 1) * 8], mx[:, j * 8:(j + 1) * 8], sc[:, j * E:(j + 1) * E]))
                    after(k)
                    k = did(dve.tensor_scalar(v3(ixf, TOPK), v3(ix, 8)[:, :, 0:TOPK], 1.0, None, ALU.mult))
                    kd = did(dve.tensor_scalar(den[:], den[:], EPS_GATE, None, ALU.max))
                    after(kd)
                    for q in range(TOPK):
                        k = did(dve.tensor_tensor(mask4[:, :, q, :], iota8[:].unsqueeze(1).broadcast_to([P, GRP, E]),
                                                  v3(ixf, TOPK)[:, :, q:q + 1].broadcast_to([P, GRP, E]), ALU.is_equal))
                    assert k == R_MASKS
                    kr = did(dve.reciprocal(dinv[:], den[:]))
                    after(kr)
                    kg = did(dve.tensor_tensor(v3(gt, TOPK), v3(mx, 8)[:, :, 0:TOPK], dinv[:].unsqueeze(2).broadcast_to([P, GRP, TOPK]), ALU.mult))
                    dve.wait_ge(rank_acc, g + 1)
                    cum = bq[:, 0:ME].rearrange("p (k c) -> p k c", c=TOPK * E)
                    kl = did(dve.tensor_tensor(v3(loc, TOPK * E), cum, run[:].unsqueeze(1).broadcast_to([P, GRP, TOPK * E]), ALU.add))
                    after(kl)
                    k = did(dve.tensor_tensor(run[:], run[:], bq[:, ME:ME + TOPK * E], ALU.add))
                    k = did(dve.tensor_tensor(sel[:], loc[:], mask[:], ALU.mult))
                    after(k)
                    k = did(dve.tensor_reduce(rank[:].rearrange("p (k q) -> p k q", q=TOPK), sel[:].rearrange("p (k q e) -> p k q e", q=TOPK, e=E), AX.X, ALU.add))
                    after(k)
                    r0 = v3(rank, TOPK)[:, :, 0]
                    e0 = v3(ixf, TOPK)[:, :, 0]
                    ka = did(dve.tensor_scalar(over[:], r0, float(CAP), FAR, ALU.is_gt, ALU.mult))
                    kb = did(dve.scalar_tensor_tensor(out=pos[:], in0=e0, scalar=float(CAP), in1=r0, op0=ALU.mult, op1=ALU.add))
                    kc = did(dve.tensor_scalar(keep[:], r0, float(CAP), None, ALU.is_le))
                    after(kb)
                    atleast(dve, sent0, 16 * GRP * g)
                    atleast(dve, touch, g)
                    dve.scalar_tensor_tensor(out=posi[:], in0=pos[:], scalar=-1.0, in1=over[:], op0=ALU.add, op1=ALU.add).then_inc(pos_ready, 1)
                    after(kc)
                    ga = gates_all[:].rearrange("p (k q) -> p k q", q=TOPK)
                    did(dve.tensor_tensor(ga[:, bass.ds(g * GRP, GRP), 0:1], v3(gt, TOPK)[:, :, 0:1], keep[:].unsqueeze(2), ALU.mult))
                    did(dve.tensor_scalar(ga[:, bass.ds(g * GRP, GRP), 1:2], v3(gt, TOPK)[:, :, 1:2], 1.0, None, ALU.mult))
                    did(dve.tensor_scalar(rank1[:, bass.ds(g * GRP, GRP)], v3(rank, TOPK)[:, :, 1], 1.0, None, ALU.mult))
                    did(dve.tensor_scalar(ex1[:, bass.ds(g * GRP, GRP)], v3(ixf, TOPK)[:, :, 1], 1.0, None, ALU.mult))
                    did(dve.tensor_scalar(mask1[:].rearrange("p (k e) -> p k e", e=E)[:, bass.ds(g * GRP, GRP), :], mask4[:, :, 1, :], 1.0, None, ALU.mult))
                    assert step[0] == RSTEPS, step[0]

                turn(0)
                with dve.Fori(1, NG) as g:
                    turn(g)

                dve.wait_ge(r_step, RSTEPS * NG)
                dve.tensor_tensor(v3(sel1, E), v3(mask1, E), run[:, 0:E].unsqueeze(1).broadcast_to([P, B, E]), ALU.mult).then_inc(f_step, 1)
                dve.wait_ge(f_step, 1)
                dve.tensor_reduce(pos1[:], v3(sel1, E), AX.X, ALU.add).then_inc(f_step, 1)
                dve.wait_ge(f_step, 2)
                dve.tensor_tensor(rank1[:], rank1[:], pos1[:], ALU.add).then_inc(f_step, 1)
                dve.wait_ge(f_step, 3)
                dve.tensor_scalar(over1[:], rank1[:], float(CAP), FAR, ALU.is_gt, ALU.mult).then_inc(f_step, 1)
                dve.scalar_tensor_tensor(out=pos1[:], in0=ex1[:], scalar=float(CAP), in1=rank1[:], op0=ALU.mult, op1=ALU.add).then_inc(f_step, 1)
                dve.tensor_scalar(keep1[:], rank1[:], float(CAP), None, ALU.is_le).then_inc(f_step, 1)
                dve.wait_ge(f_step, 6)
                dve.scalar_tensor_tensor(out=pos1i[:], in0=pos1[:], scalar=-1.0, in1=over1[:], op0=ALU.add, op1=ALU.add).then_inc(f_step, 1)
                ga = gates_all[:].rearrange("p (k q) -> p k q", q=TOPK)
                dve.tensor_tensor(ga[:, :, 1:2], ga[:, :, 1:2], keep1[:].unsqueeze(2), ALU.mult).then_inc(f_step, 1)


R_SHIFTED, R_MASKS, RSTEPS = 2, 19, 33
FSTEPS = 8


def phase_experts(nc, d, m):
    bank, ident, vecT = m["bank"], m["ident"], m["vecT"]
    w_hi, w_lo, raw = m["w_hi"], m["w_lo"], m["raw"]
    slots, results = m["slots"], m["results"]
    g_f, g_hi, g_lo = m["g_f"], m["g_hi"], m["g_lo"]
    NCK = [(0, 512), (512, 512), (1024, 256)]
    XP = CAP
    WB = [0, 2 * H]
    XB = [4 * H, 4 * H + XP]
    UN = [(s, hb) for s in range(3) for hb in range(HB)]
    NU = len(UN)
    NY = 3

    with ExitStack() as ctx:
        def sb(name, shape, dt=F32):
            return ctx.enter_context(nc.sbuf_tensor(name, shape, dt))

        def sem(name):
            return ctx.enter_context(nc.semaphore(name))

        rows = [sb(f"slotrows{i}", [P, ST * ROWW]) for i in range(2)]
        iota8 = m["iota8"]
        touched = sb("touched3", [P, 6])
        TOUCH = [0, 3]
        touch = sem("touch3")
        dest = [sb(f"dest{i}", [P, ST], U32) for i in range(2)]
        yT = [sb(f"yT{i}", [P, 512]) for i in range(2)]
        yrow = [sb(f"yrow{i}", [P, ST * P]) for i in range(2)]
        b1c = [sb(f"b1c{i}", [P, HB + 1]) for i in range(2)]

        rows_in = [sem("rows_in0"), sem("rows_in1")]
        wts_in = [sem("wts_in0"), sem("wts_in1")]
        dest_ready = sem("dest_ready"); xe_acc = sem("xe_acc"); xe_ready = sem("xe_ready"); fc1_acc = sem("fc1_acc")
        fc1_ready = sem("fc1_ready"); fc2_ready = sem("fc2_ready"); bias_ready = sem("bias_ready")
        h1_done = sem("h1_done"); silu_done = sem("silu_done"); lo_done = sem("lo_done"); y_done = sem("y_done")
        yT_ready = sem("yT_ready"); yr_acc = sem("yr_acc"); yr_ready = sem("yr_ready"); sent = [sem("sent_even"), sem("sent_odd")]

        xbank = [bank[0], bank[1]]
        hbank = [bank[2], bank[3], bank[4]]
        ybank = [bank[5], bank[6]]
        rbank = bank[7]
        XT = 3
        TILES = [(0, 4), (4, 4), (8, 2)]

        with nc.Block() as block:
            @block.sync
            def _(sp):
                def turn(e, q, pair):
                    atleast(sp, fc2_ready, 2 * max_expr(e, q))
                    if not isinstance(e, int):
                        sp.wait_ge(fc2_ready, 2)
                    sp.dma_start(raw[q][:, 0:H].rearrange("p (m n) -> p m n", m=HB), d["L1_ffn_fc1_w"][bass.ds(e, 1)].rearrange("a (m p) n -> p (a m) n", p=P)).then_inc(wts_in[q], 16)
                    sp.dma_start(raw[q][:, H:2 * H].rearrange("p (m n) -> p m n", m=HB), d["L1_ffn_fc2_w"][bass.ds(e, 1)].rearrange("a (m p) n -> p (a m) n", p=P)).then_inc(wts_in[q], 16)
                    sp.dma_start(rows[q][:].rearrange("p (n c) -> p n c", c=ROWW), slots[bass.ds(e * CAP, CAP), :].rearrange("(n p) c -> p n c", p=P)).then_inc(rows_in[q], 16)
                loop_pairs(sp, turn)

            @block.gpsimd
            def _(gp):
                last_result = gp.to_reg(TOPK * N - 1)

                def turn(e, q, pair):
                    for i, (t0, nt) in enumerate(TILES):
                        atleast(gp, yr_ready, NY * e + i + 1)
                        if i == 0:
                            atleast(gp, dest_ready, e + 1)
                        gp.tensor_tensor(touched[:, TOUCH[q] + i:TOUCH[q] + i + 1], iota8[:, 0:1], iota8[:, 0:1], ALU.add).then_inc(touch, 1)
                        for j in range(t0, t0 + nt):
                            gp.indirect_dma_start(out=results, out_offset=bass.IndirectOffsetOnAxis(ap=dest[q][:, j:j + 1], axis=0),
                                                  in_=yrow[q][:, j * P:(j + 1) * P], in_offset=None,
                                                  bounds_check=last_result, oob_is_err=False).then_inc(sent[q], 16)
                loop_pairs(gp, turn)
                gp.wait_ge(sent[0], 16 * ST * E // 2)
                gp.wait_ge(sent[1], 16 * ST * E // 2)

            @block.tensor
            def _(pe):
                def prepare(e, q, pair):
                    atleast(pe, rows_in[q], 16 * (pair + 1))
                    for i, (t0, nt) in enumerate(TILES):
                        if i >= 2:
                            atleast(pe, xe_ready, 6 * e + 2 * (i - 1))
                        else:
                            atleast(pe, fc1_ready, 2 * e) if i == 1 else atleast(pe, xe_ready, 6 * e)
                        for j in range(nt):
                            t = pe.transpose(xbank[i % 2][:, j * P:(j + 1) * P], rows[q][:, (t0 + j) * ROWW:(t0 + j) * ROWW + P], ident[:])
                        t.then_inc(xe_acc, 1)
                    atleast(pe, wts_in[q], 32 * (pair + 1))
                    atleast(pe, xe_ready, 6 * e + 4)
                    for j in range(HB):
                        t = pe.transpose(xbank[1][:, j * P:(j + 1) * P], raw[q][:, j * P:(j + 1) * P], ident[:])
                    t.then_inc(fc1_acc, 1)

                def first(e, q, u):
                    s, hb = UN[u]
                    c0, w = NCK[s]
                    if u == 0:
                        atleast(pe, xe_ready, 6 * (e + 1))
                        atleast(pe, fc1_ready, 2 * (e + 1))
                    atleast(pe, silu_done, 2 * (NU * e + max(u - 2, 0)))
                    a = slice(WB[q] + hb * P, WB[q] + (hb + 1) * P)
                    b_ = slice(XB[q] + c0, XB[q] + c0 + w)
                    mm3(pe, hbank[u % 3][:, 0:w], w_hi[:, a], w_lo[:, a], w_hi[:, b_], w_lo[:, b_], True, True).then_inc(h1_done, 1)

                def second(e, q, u):
                    s, hb = UN[u]
                    c0, w = NCK[s]
                    if u == 0:
                        atleast(pe, fc2_ready, 2 * (e + 1))
                    if hb == 0:
                        atleast(pe, yT_ready, NY * e + max(s - 1, 0))
                    atleast(pe, lo_done, NU * e + u + 1)
                    a = slice(WB[q] + H + hb * P, WB[q] + H + (hb + 1) * P)
                    mm3(pe, ybank[s % 2][:, 0:w], w_hi[:, a], w_lo[:, a], g_hi[u % 4][:, 0:w], g_lo[u % 4][:, 0:w], hb == 0, hb == HB - 1).then_inc(y_done, 1)

                def back(e, q, s):
                    t0, nt = TILES[s]
                    atleast(pe, yT_ready, NY * e + s + 1)
                    atleast(pe, yr_ready, NY * e + s)
                    for j in range(nt):
                        t = pe.transpose(rbank[:, j * P:(j + 1) * P], yT[s % 2][:, j * P:(j + 1) * P], ident[:])
                    t.then_inc(yr_acc, 1)

                def turn(e, q, pair):
                    prepare(e, q, pair)
                    for u in range(NU + 2):
                        if u < NU:
                            first(e, q, u)
                        if u >= 2:
                            second(e, q, u - 2)
                        if u in (6, 10):
                            back(e, q, (u - 6) // 4)
                    back(e, q, 2)

                loop_pairs(pe, turn)

            @block.scalar
            def _(act):
                def turn(e, q, pair):
                    atleast(act, fc1_acc, e + 1)
                    atleast(act, y_done, NU * max_expr(e, q))
                    act.activation(w_hi[:, WB[q]:WB[q] + H], xbank[1][:], ACT.Copy).then_inc(fc1_ready, 1)
                    for u in range(NU + 3):
                        if u < NU:
                            s, hb = UN[u]
                            w = NCK[s][1]
                            atleast(act, h1_done, NU * e + u + 1)
                            atleast(act, bias_ready, e + 1)
                            atleast(act, lo_done, NU * e + max(u - 1, 0))
                            atleast(act, y_done, NU * e + max(u - 3, 0))
                            b_ = b1c[q][:, hb:hb + 1]
                            act.activation(g_f[u % 2][:, 0:w], hbank[u % 3][:, 0:w], ACT.Silu, bias=b_).then_inc(silu_done, 1)
                            act.activation(g_hi[u % 4][:, 0:w], hbank[u % 3][:, 0:w], ACT.Silu, bias=b_).then_inc(silu_done, 1)
                        if u in (6, 10, 14):
                            s = (u - 6) // 4
                            w = NCK[s][1]
                            atleast(act, y_done, NU * e + 4 * (s + 1))
                            atleast(act, yr_acc, NY * e + max(s - 1, 0))
                            act.activation(yT[s % 2][:, 0:w], ybank[s % 2][:, 0:w], ACT.Identity, bias=b1c[q][:, HB:HB + 1]).then_inc(yT_ready, 1)

                loop_pairs(act, turn)

            @block.vector
            def _(dve):
                def turn(e, q, pair):
                    atleast(dve, yT_ready, NY * max_expr(e, q))
                    atleast(dve, sent[q], 16 * ST * pair)
                    atleast(dve, touch, NY * max_expr(e, q))
                    dve.tensor_scalar(b1c[q][:, 0:HB], vecT[:, bass.ds(R_FB1 + HB * e, HB)], 1.0, None, ALU.mult)
                    dve.tensor_scalar(b1c[q][:, HB:HB + 1], vecT[:, bass.ds(R_FB2 + e, 1)], 1.0, None, ALU.mult).then_inc(bias_ready, 1)
                    atleast(dve, rows_in[q], 16 * (pair + 1))
                    dve.tensor_scalar(dest[q][:].unsqueeze(2), rows[q][:].rearrange("p (n c) -> p n c", c=ROWW)[:, :, P:ROWW], 1.0, None, ALU.mult).then_inc(dest_ready, 1)
                    atleast(dve, y_done, NU * max_expr(e, q))
                    for i, (t0, nt) in enumerate(TILES):
                        atleast(dve, xe_acc, 3 * e + i + 1)
                        o = slice(XB[q] + t0 * P, XB[q] + (t0 + nt) * P)
                        dve.tensor_copy(w_hi[:, o], xbank[i % 2][:, 0:nt * P]).then_inc(xe_ready, 1)
                        atleast(dve, xe_ready, 6 * e + 2 * i + 1)
                        dve.tensor_tensor(w_lo[:, o], xbank[i % 2][:, 0:nt * P], w_hi[:, o], ALU.subtract).then_inc(xe_ready, 1)
                    atleast(dve, fc1_ready, 2 * e + 1)
                    dve.tensor_tensor(w_lo[:, WB[q]:WB[q] + H], xbank[1][:], w_hi[:, WB[q]:WB[q] + H], ALU.subtract).then_inc(fc1_ready, 1)
                    dve.tensor_copy(w_hi[:, WB[q] + H:WB[q] + 2 * H], raw[q][:, H:2 * H]).then_inc(fc2_ready, 1)
                    atleast(dve, fc2_ready, 2 * e + 1)
                    dve.tensor_tensor(w_lo[:, WB[q] + H:WB[q] + 2 * H], raw[q][:, H:2 * H], w_hi[:, WB[q] + H:WB[q] + 2 * H], ALU.subtract).then_inc(fc2_ready, 1)
                    for u in range(NU + 3):
                        if u < NU:
                            s, hb = UN[u]
                            w = NCK[s][1]
                            atleast(dve, silu_done, 2 * (NU * e + u + 1))
                            atleast(dve, y_done, NU * e + max(u - 3, 0))
                            dve.tensor_tensor(g_lo[u % 4][:, 0:w], g_f[u % 2][:, 0:w], g_hi[u % 4][:, 0:w], ALU.subtract).then_inc(lo_done, 1)
                        if u in (6, 10, 14):
                            s = (u - 6) // 4
                            t0, nt = TILES[s]
                            atleast(dve, yr_acc, NY * e + s + 1)
                            dve.tensor_copy(yrow[q][:, t0 * P:(t0 + nt) * P], rbank[:, 0:nt * P]).then_inc(yr_ready, 1)

                loop_pairs(dve, turn)


def loop_pairs(eng, turn):
    turn(0, 0, 0)
    turn(1, 1, 0)
    with eng.Fori(1, E // 2) as pair:
        turn(pair * 2, 0, pair)
        turn(pair * 2 + 1, 1, pair)


def max_expr(e, q):
    return max(e - 1, 0) if isinstance(e, int) else e - 1


def phase_norm(nc, d, m, out):
    xT, wide, results, gates_all = m["xT"], m["wide"], m["results"], m["gates_all"]
    x1rows = xT
    hid3 = wide[:].rearrange("p (b c) -> p b c", c=ROWW)
    with ExitStack() as ctx:
        def sb(name, shape, dt=F32):
            return ctx.enter_context(nc.sbuf_tensor(name, shape, dt))

        def sem(name):
            return ctx.enter_context(nc.semaphore(name))

        gb = sb("gamma", [P, P]); bb = sb("beta", [P, P]); epsc = sb("epsc", [P, 1])
        yb = [[sb(f"y{q}{i}", [P, GRP * P]) for i in range(2)] for q in range(TOPK)]
        res = [sb(f"res{i}", [P, GRP * P]) for i in range(2)]
        nrm = [sb(f"nrm{i}", [P, GRP * P]) for i in range(2)]
        fin = [sb(f"fin{i}", [P, GRP * P]) for i in range(2)]
        st = sb("stats", [P, GRP * 6]); mv = sb("mv", [P, GRP * 2]); sd = sb("sd", [P, GRP]); rstd = sb("rstd", [P, GRP])
        n_in = sem("n_in"); y_in = [sem("y_in0"), sem("y_in1")]; eps_ready = sem("eps_ready"); c_step = sem("c_step")
        mv_ready = sem("mv_ready"); sd_ready = sem("sd_ready"); nrm_step = sem("nrm_step"); scaled = sem("scaled"); fin_ready = sem("fin_ready"); stored = [sem("stored_even"), sem("stored_odd")]
        CS = GRP * 3 + 1
        y_src = results.rearrange("(q g b p) c -> q g p b c", q=TOPK, b=GRP, p=P)

        def v3(a):
            return a[:].rearrange("p (b c) -> p b c", c=P)

        with nc.Block() as block:
            @block.sync
            def _(sp):
                sp.dma_start(gb[:], d["L1_ffn_ln_gamma"].rearrange("(a p) -> a p", a=1).broadcast_to([P, P])).then_inc(n_in, 16)
                sp.dma_start(bb[:], d["L1_ffn_ln_beta"].rearrange("(a p) -> a p", a=1).broadcast_to([P, P])).then_inc(n_in, 16)
                for g in range(NG):
                    if g >= 2:
                        sp.wait_ge(c_step, CS * (g - 1))
                    for q in range(TOPK):
                        sp.dma_start(v3(yb[q][g % 2]), y_src[q, g]).then_inc(y_in[g % 2], 16)

            @block.scalar
            def _(act):
                for g in range(NG):
                    act.wait_ge(mv_ready, GRP * (g + 1))
                    act.wait_ge(eps_ready, 1)
                    act.activation(sd[:], mv[:].rearrange("p (b c) -> p b c", c=2)[:, :, 1], ACT.Sqrt, bias=epsc[:]).then_inc(sd_ready, 1)
                    if g >= 1:
                        act.wait_ge(fin_ready, g)
                        act.dma_start(out[GRP * (g - 1):GRP * g].rearrange("b t c -> t b c"), v3(fin[(g - 1) % 2])).then_inc(stored[(g - 1) % 2], 16)
                act.wait_ge(fin_ready, NG)
                act.dma_start(out[GRP * (NG - 1):GRP * NG].rearrange("b t c -> t b c"), v3(fin[(NG - 1) % 2])).then_inc(stored[(NG - 1) % 2], 16)
                act.wait_ge(stored[0], 16 * NG // 2)
                act.wait_ge(stored[1], 16 * NG // 2)

            @block.gpsimd
            def _(gp):
                gp.wait_ge(n_in, 32)
                for g in range(NG):
                    f, w = v3(fin[g % 2]), v3(nrm[g % 2])
                    gp.wait_ge(nrm_step, GRP * (g + 1))
                    if g >= 2:
                        gp.wait_ge(stored[g % 2], 16 * (g // 2))
                    gp.tensor_tensor(f, w, gb[:].unsqueeze(1).broadcast_to([P, GRP, P]), ALU.mult).then_inc(scaled, 1)
                    gp.wait_ge(scaled, 2 * g + 1)
                    gp.tensor_tensor(f, f, bb[:].unsqueeze(1).broadcast_to([P, GRP, P]), ALU.add).then_inc(scaled, 1)

            @block.vector
            def _(dve):
                dve.memset(epsc[:], EPS_LN).then_inc(eps_ready, 1)

                def finish(g):
                    dve.wait_ge(scaled, 2 * (g + 1))
                    dve.tensor_tensor(fin[g % 2][:], fin[g % 2][:], x1rows[:, g * GRP * P:(g + 1) * GRP * P], ALU.add).then_inc(fin_ready, 1)

                for g in range(NG):
                    dve.wait_ge(y_in[g % 2], 32 * (g // 2 + 1))
                    n = CS * g
                    k = 0
                    r = res[g % 2]
                    if g >= 2:
                        dve.wait_ge(nrm_step, GRP * (g - 1))
                    for q in range(TOPK):
                        for j in range(GRP):
                            b = g * GRP + j
                            js = slice(j * P, (j + 1) * P)
                            if q:
                                dve.wait_ge(c_step, n + j + 1)
                            dve.scalar_tensor_tensor(out=r[:, js], in0=yb[q][g % 2][:, js], scalar=gates_all[:, TOPK * b + q:TOPK * b + q + 1],
                                                     in1=(r[:, js] if q else hid3[:, b, 0:P]), op0=ALU.mult, op1=ALU.add).then_inc(c_step, 1)
                    for j in range(GRP):
                        dve.wait_ge(c_step, n + GRP + j + 1)
                        dve.bn_stats(st[:, 6 * j:6 * j + 6], r[:, j * P:(j + 1) * P]).then_inc(c_step, 1)
                    if g >= 1:
                        dve.wait_ge(sd_ready, g)
                    for j in range(GRP):
                        dve.wait_ge(c_step, n + 2 * GRP + j + 1)
                        dve.bn_aggr(mv[:, 2 * j:2 * j + 2], st[:, 6 * j:6 * j + 6]).then_inc(mv_ready, 1)
                    if g >= 1:
                        finish(g - 1)
                    dve.wait_ge(sd_ready, g + 1)
                    dve.reciprocal(rstd[:], sd[:]).then_inc(c_step, 1)
                    dve.wait_ge(c_step, n + 3 * GRP + 1)
                    dve.wait_ge(mv_ready, GRP * (g + 1))
                    if g >= 2:
                        dve.wait_ge(scaled, 2 * g - 3)
                    for j in range(GRP):
                        js = slice(j * P, (j + 1) * P)
                        dve.tensor_scalar(nrm[g % 2][:, js], r[:, js], mv[:, 2 * j:2 * j + 1], rstd[:, j:j + 1], ALU.subtract, ALU.mult).then_inc(nrm_step, 1)
                finish(NG - 1)


NAMES = ['x', 'cond_1024', 'L0_cond_W_z', 'L0_cond_U_z', 'L0_cond_C_z', 'L0_cond_b_z', 'L0_cond_W_r', 'L0_cond_U_r',
         'L0_cond_C_r', 'L0_cond_b_r', 'L0_cond_W', 'L0_cond_U', 'L0_cond_C', 'L0_cond_b', 'L0_ffn_rW', 'L0_ffn_rb',
         'L0_ffn_W1', 'L0_ffn_b1', 'L0_ffn_W2', 'L0_ffn_b2', 'L0_ffn_sW1', 'L0_ffn_sb1', 'L0_ffn_sW2', 'L0_ffn_sb2',
         'L1_cond_Wq1', 'L1_cond_bq1', 'L1_cond_Wq2', 'L1_cond_bq2', 'L1_cond_Wk1', 'L1_cond_bk1', 'L1_cond_Wk2',
         'L1_cond_bk2', 'L1_cond_Wv', 'L1_cond_bv', 'L1_cond_alpha', 'L1_ffn_wg', 'L1_ffn_fc1_w', 'L1_ffn_fc1_b',
         'L1_ffn_fc2_w', 'L1_ffn_fc2_b', 'L1_ffn_ln_gamma', 'L1_ffn_ln_beta']


def kernel(**inputs):
    from concourse import bacc
    from concourse.bass_utils import run_bass_kernel_spmd

    nc = bacc.Bacc("TRN2", target_bir_lowering=False, num_devices=1)
    arrays, d = {}, {}
    for name in NAMES:
        a = np.ascontiguousarray(inputs[name])
        arrays[f"in_{name}"] = a
        d[name] = nc.dram_tensor(f"in_{name}", a.shape, F32, kind="ExternalInput").ap()
    out = nc.dram_tensor("out", (B, T, P), F32, kind="ExternalOutput").ap()
    build(nc, d, out)
    return run_bass_kernel_spmd(nc, [arrays], core_ids=[0]).results[0]["out"]
```

```python
from contextlib import ExitStack

import numpy as np
import concourse.bass as bass
from concourse import mybir

F32 = mybir.dt.float32
F32R = mybir.dt.float32r
U32 = mybir.dt.uint32
ALU = mybir.AluOpType
ACT = mybir.ActivationFunctionType
AX = mybir.AxisListType

P = 128
B, T = 32, 128
N = B * T
H = 512
HB = H // P
E = 8
NSH = 2
NE0 = E + NSH
TOPK = 2
STEPS = 16
CH = STEPS * B
NCH = N // CH
UNITS = NE0 * HB
SG = 4
GRP = 4
NG = B // GRP
CAP = TOPK * int(1.25 * ((N + E - 1) // E))
ST = CAP // P
ROWW = P + 1
SECOND = E * 2 * CAP
SLOT_ROWS = SECOND + E * CAP
FAR = 60000.0
SCALE = 1.0 / float(np.sqrt(np.float32(P)))
EPS_GATE = 1.1920929e-07
EPS_LN = 1e-05

R_SB1, R_B1, R_BZ, R_BR, R_BH = 0, 8, 40, 41, 42
R_SB2, R_B2, R_BQ2, R_BK2, R_FB1, R_FB2, NVEC = 43, 45, 53, 54, 55, 87, 95


def atleast(eng, sem, value):
    if isinstance(value, int) and value <= 0:
        return
    eng.wait_ge(sem, value)


def part_slot(p):
    return (p * UNITS) // (2 * STEPS)


PART_OF_SLOT = {part_slot(p): p for p in range(2 * STEPS)}
NGRP = 1 + E


def group_of(u):
    if u < NSH * HB:
        return 0, u == 0, u == NSH * HB - 1
    k = u // HB - 1
    return k, u % HB == 0, u % HB == HB - 1


def build(nc, d, out):
    with ExitStack() as ctx:
        def sb(name, shape, dt=F32):
            return ctx.enter_context(nc.sbuf_tensor(name, shape, dt))

        def sem(name):
            return ctx.enter_context(nc.semaphore(name))

        bank = [ctx.enter_context(nc.psum_tensor(f"bank{i}", [P, 512], F32)) for i in range(8)]

        w_dram = nc.dram_tensor("w_dram", (E, CH), F32, kind="Internal").ap()
        slots = nc.dram_tensor("slot_rows", (SLOT_ROWS, ROWW), F32, kind="Internal").ap()
        results = nc.dram_tensor("result_rows", (TOPK * N, P), F32, kind="Internal").ap()

        ident = sb("ident", [P, P])
        identr = sb("identr", [P, P], F32R)
        vecs = sb("vecs", [P, P])
        vecT = sb("vecT", [P, NVEC])
        iota8 = sb("iota8", [P, E])
        condT = sb("condT", [P, B])
        xT = sb("xT", [P, N])
        x1T = sb("x1T", [P, N])
        wide = sb("wide", [P, B * ROWW])
        w_hi = sb("w_hi", [P, NE0 * 2 * H], F32R)
        w_lo = sb("w_lo", [P, NE0 * 2 * H], F32R)
        raw = [sb(f"raw{i}", [P, 2 * H]) for i in range(2)]
        alphaT = sb("alphaT", [P, B])
        firsts = sb("firsts", [P, E])
        firsts_u = sb("firsts_u", [1, E], U32)
        gates_all = sb("gates_all", [P, B * TOPK])
        zt = sb("zt", [P, ST * ROWW])
        g_f = [sb(f"g_f{i}", [P, CH]) for i in range(2)]
        g_hi = [sb(f"g_hi{i}", [P, CH], F32R) for i in range(4)]
        g_lo = [sb(f"g_lo{i}", [P, CH], F32R) for i in range(4)]

        hs = [sb(f"hs{i}", [P, GRP * ROWW]) for i in range(2)]
        posi = [sb(f"posi{i}", [P, GRP * TOPK], U32) for i in range(2)]
        hs_ready = sem("hs_ready"); hs_free = sem("hs_free"); pos_ready = sem("pos_ready"); hid_kept = sem("hid_kept")
        sent_rows = [sem("sent_rows_even"), sem("sent_rows_odd")]; touch = sem("touch")
        touched = sb("touched", [P, 3])
        wts_in = [sem("wts_in0"), sem("wts_in1")]

        def dispatch(gp, last_slot, g, par, before):
            gp.wait_ge(hs_ready, (g + 1) * 16)
            gp.wait_ge(pos_ready, g + 1)
            gp.tensor_tensor(touched[:, par:par + 1], iota8[:, 0:1], iota8[:, 0:1], ALU.add).then_inc(touch, 1)
            for j in range(GRP):
                if j == GRP // 2 and not (isinstance(g, int) and g == NG - 1):
                    atleast(gp, sent_rows[1 - par], 16 * GRP * TOPK * before)
                    gp.wait_ge(hid_kept, (g + 2) * 16)
                    gp.tensor_tensor(touched[:, 2:3], iota8[:, 0:1], iota8[:, 0:1], ALU.add).then_inc(hs_free, 1)
                for q in range(TOPK):
                    k = j * TOPK + q
                    gp.indirect_dma_start(out=slots, out_offset=bass.IndirectOffsetOnAxis(ap=posi[par][:, k:k + 1], axis=0),
                                          in_=hs[par][:, j * ROWW:(j + 1) * ROWW], in_offset=None,
                                          bounds_check=last_slot, oob_is_err=False).then_inc(sent_rows[par], 16)

        phase_scan(nc, d, locals())
        phase_attention(nc, d, locals())
        phase_experts(nc, d, locals())
        phase_norm(nc, d, locals(), out)


def load_expert_weights(sp, d, raw, wts_in, e):
    q = e % 2
    sp.dma_start(raw[q][:, 0:H].rearrange("p (m n) -> p m n", m=HB), d["L1_ffn_fc1_w"][e].rearrange("(m p) n -> p m n", p=P)).then_inc(wts_in[q], 16)
    sp.dma_start(raw[q][:, H:2 * H].rearrange("p (m n) -> p m n", m=HB), d["L1_ffn_fc2_w"][e].rearrange("(m p) n -> p m n", p=P)).then_inc(wts_in[q], 16)


def mm3(pe, out, a_hi, a_lo, b_hi, b_lo, start, stop):
    pe.matmul(out, a_hi, b_hi, start=start, stop=False, skip_group_check=True)
    pe.matmul(out, a_hi, b_lo, start=False, stop=False, skip_group_check=True)
    return pe.matmul(out, a_lo, b_hi, start=False, stop=stop, skip_group_check=True)


def phase_scan(nc, d, m):
    bank, ident, identr, vecs, vecT = m["bank"], m["ident"], m["identr"], m["vecs"], m["vecT"]
    condT, xT, x1T, wide, w_hi, w_lo, raw = (m[k] for k in ("condT", "xT", "x1T", "wide", "w_hi", "w_lo", "raw"))
    iota8, zt, g_f, g_hi, g_lo, alphaT = (m[k] for k in ("iota8", "zt", "g_f", "g_hi", "g_lo", "alphaT"))
    w_dram, slots, results = m["w_dram"], m["slots"], m["results"]
    wb = wide[:, 0:E * CH]

    with ExitStack() as ctx:
        def sb(name, shape, dt=F32):
            return ctx.enter_context(nc.sbuf_tensor(name, shape, dt))

        def sem(name):
            return ctx.enter_context(nc.semaphore(name))

        xrows = [sb(f"xrows{i}", [P, 4 * P]) for i in range(2)]
        condr = sb("condr", [B, P])
        wx = sb("wx", [P, 3 * P])
        wx_hi = sb("wx_hi", [P, 3 * P], F32R)
        wx_lo = sb("wx_lo", [P, 3 * P], F32R)
        uh = sb("uh", [P, 3 * P])
        cv = sb("cv", [P, 3 * P])
        vb = sb("vb", [P, 3 * B])
        vb_hi = sb("vb_hi", [P, 3 * B], F32R)
        vb_lo = sb("vb_lo", [P, 3 * B], F32R)
        x_hi = sb("x_hi", [P, CH], F32R)
        x_lo = sb("x_lo", [P, CH], F32R)
        h = sb("h", [P, CH])
        h_hi = sb("h_hi", [P, CH], F32R)
        h_lo = sb("h_lo", [P, CH], F32R)
        tzr = sb("tzr", [P, 2 * B])
        rh = sb("rh", [P, B])
        z = sb("z", [P, B])
        kept = sb("kept", [P, B])
        hh = sb("hh", [P, B])
        zhh = sb("zhh", [P, B])
        acc = sb("acc", [P, CH])
        tmp = sb("tmp", [P, CH])
        sbias = sb("sbias", [P, 1])
        rw = sb("rw", [P, E])
        rbb = sb("rbb", [P, E])
        lg = sb("lg", [P, 4 * E])
        mx = sb("mx", [P, 4 * 8])
        ix = sb("ix", [P, 4 * 8], U32)
        ixf = sb("ixf", [P, 4 * 2])
        lgmax = sb("lgmax", [P, 1])
        dlt = sb("dlt", [P, 4])
        th = sb("th", [P, 4])
        p0 = sb("p0", [P, 4])
        p1 = sb("p1", [P, 4])
        oh0 = sb("oh0", [P, 4 * E])
        oh1 = sb("oh1", [P, 4 * E])
        wt = sb("wt", [P, 4 * E])
        wT = sb("wT", [E, CH])
        wq1 = sb("wq1", [P, P])
        wk1 = sb("wk1", [P, P])
        bq1 = sb("bq1", [B, P])
        bk1 = sb("bk1", [B, P])
        alph = sb("alph", [B, 1])
        q1 = sb("q1", [B, P])
        k1 = sb("k1", [B, P])
        s1 = sb("s1", [B, 4])
        a1 = sb("a1", [B, P])
        e1 = sb("e1", [B, P])

        small_in = sem("small_in"); x_in = [sem("x_in0"), sem("x_in1")]; w_in = [sem("w_in0"), sem("w_in1")]
        a1_in = sem("a1_in")
        zeroed = sem("zeroed")
        ident_ready = sem("ident_ready"); setup_pe = sem("setup_pe"); setup_dve = sem("setup_dve")
        xt_pe = sem("xt_pe"); xt_done = sem("xt_done"); w_split = sem("w_split"); w_step = sem("w_step")
        zt_ready = sem("zt_ready"); a1_pe = sem("a1_pe"); a1_dve = sem("a1_dve"); a1_act = sem("a1_act")
        x_split = sem("x_split"); prefilled = sem("prefilled")
        zr_acc = sem("zr_acc"); zr_tanh = sem("zr_tanh"); rh_ready = sem("rh_ready"); z_ready = sem("z_ready")
        kept_ready = sem("kept_ready"); hh_acc = sem("hh_acc"); hh_tanh = sem("hh_tanh"); zhh_ready = sem("zhh_ready")
        h_ready = sem("h_ready")
        h_split = sem("h_split"); w1_done = sem("w1_done"); gelu_done = sem("gelu_done"); lo_ready = sem("lo_ready")
        w2_done = sem("w2_done"); y_read = sem("y_read"); acc_ready = sem("acc_ready")
        gate_acc = sem("gate_acc"); gate_step = sem("gate_step"); gate_tanh = sem("gate_tanh"); wT_acc = sem("wT_acc")
        wT_ready = sem("wT_ready"); w_out = sem("w_out"); wb_ready = sem("wb_ready")

        scan_bank = [bank[0], bank[1]]
        w1_bank = [bank[2], bank[3], bank[4]]
        y_bank = [bank[5], bank[6]]
        gate_bank = bank[7]
        x1T_tb = x1T[:].rearrange("p (b t) -> p t b", b=B)
        xT_tb = xT[:].rearrange("p (t b) -> p t b", b=B)
        GSTEPS = 18

        SMALL = 0

        def w1(part, e, hb):
            return part[:, e * 2 * H + hb * P:e * 2 * H + (hb + 1) * P]

        def w2(part, e, hb):
            return part[:, e * 2 * H + H + hb * P:e * 2 * H + H + (hb + 1) * P]

        with nc.Block() as block:
            @block.sync
            def _(sp):
                n = 0
                for dst, src in (
                    (condr[:], d["cond_1024"]),
                    (vecs[R_SB1:R_SB1 + 8, :], d["L0_ffn_sb1"].rearrange("s (m p) -> (s m) p", p=P)),
                    (vecs[R_B1:R_B1 + 32, :], d["L0_ffn_b1"].rearrange("s (m p) -> (s m) p", p=P)),
                    (vecs[R_BZ:R_BZ + 1, :], d["L0_cond_b_z"].rearrange("(a p) -> a p", a=1)),
                    (vecs[R_BR:R_BR + 1, :], d["L0_cond_b_r"].rearrange("(a p) -> a p", a=1)),
                    (vecs[R_BH:R_BH + 1, :], d["L0_cond_b"].rearrange("(a p) -> a p", a=1)),
                    (vecs[R_SB2:R_SB2 + 2, :], d["L0_ffn_sb2"]),
                    (vecs[R_B2:R_B2 + 8, :], d["L0_ffn_b2"]),
                    (vecs[R_BQ2:R_BQ2 + 1, :], d["L1_cond_bq2"].rearrange("(a p) -> a p", a=1)),
                    (vecs[R_BK2:R_BK2 + 1, :], d["L1_cond_bk2"].rearrange("(a p) -> a p", a=1)),
                    (vecs[R_FB1:R_FB1 + 32, :], d["L1_ffn_fc1_b"].rearrange("s (m p) -> (s m) p", p=P)),
                    (vecs[R_FB2:R_FB2 + 8, :], d["L1_ffn_fc2_b"]),
                    (wx[:, 0:P], d["L0_cond_W_z"]), (wx[:, P:2 * P], d["L0_cond_W_r"]), (wx[:, 2 * P:3 * P], d["L0_cond_W"]),
                    (cv[:, 0:P], d["L0_cond_C_z"]), (cv[:, P:2 * P], d["L0_cond_C_r"]), (cv[:, 2 * P:3 * P], d["L0_cond_C"]),
                    (uh[:, 0:P], d["L0_cond_U_z"]), (uh[:, P:2 * P], d["L0_cond_U_r"]), (uh[:, 2 * P:3 * P], d["L0_cond_U"]),
                    (rw[:], d["L0_ffn_rW"]),
                    (rbb[:], d["L0_ffn_rb"].rearrange("(a p) -> a p", a=1).broadcast_to([P, E])),
                ):
                    sp.dma_start(dst, src).then_inc(small_in, 16)
                    n += 16
                assert n == NSMALL
                for dst, src in (
                    (wq1[:], d["L1_cond_Wq1"]), (wk1[:], d["L1_cond_Wk1"]),
                    (bq1[:], d["L1_cond_bq1"].rearrange("(a p) -> a p", a=1).broadcast_to([B, P])),
                    (bk1[:], d["L1_cond_bk1"].rearrange("(a p) -> a p", a=1).broadcast_to([B, P])),
                    (alph[:], d["L1_cond_alpha"].rearrange("(a p) -> a p", a=1).broadcast_to([B, 1])),
                ):
                    sp.dma_start(dst, src).then_inc(a1_in, 16)
                for e in range(NE0):
                    if e >= 2:
                        sp.wait_ge(w_split, 2 * (e - 1))
                    a, b_ = (d["L0_ffn_sW1"][e], d["L0_ffn_sW2"][e]) if e < NSH else (d["L0_ffn_W1"][e - NSH], d["L0_ffn_W2"][e - NSH])
                    sp.dma_start(raw[e % 2][:, 0:H], a).then_inc(w_in[e % 2], 16)
                    sp.dma_start(raw[e % 2][:, H:2 * H].rearrange("p (m n) -> p m n", m=HB), b_.rearrange("(m p) n -> p m n", p=P)).then_inc(w_in[e % 2], 16)
                sp.wait_ge(zt_ready, 2)
                for e in range(E):
                    sp.dma_start(slots[SECOND + e * CAP:SECOND + (e + 1) * CAP, :].rearrange("(p n) c -> p (n c)", p=P), zt[:]).then_inc(zeroed, 16)
                rows = TOPK * N // E
                for e in range(E):
                    sp.dma_start(results[e * rows:(e + 1) * rows, :].rearrange("(p n) c -> p n c", p=P),
                                 zt[:].rearrange("p (n c) -> p n c", c=ROWW)[:, 0:rows // P, 0:P]).then_inc(zeroed, 16)

                def routing(c):
                    sp.wait_ge(wT_ready, c + 1)
                    sp.dma_start(w_dram, wT[:]).then_inc(w_out, 16)
                    sp.wait_ge(w_out, (c + 1) * 16)
                    sp.dma_start(wb, w_dram.rearrange("e n -> (e n)").rearrange("(a n) -> a n", a=1).broadcast_to([P, E * CH])).then_inc(wb_ready, 16)

                with sp.Fori(0, NCH) as c:
                    routing(c)
                sp.wait_ge(zeroed, 16 * 2 * E)

            @block.gpsimd
            def _(gp):
                gp.memset(ident[:], 0.0).then_inc(ident_ready, 1)
                gp.wait_ge(ident_ready, 1)
                gp.affine_select(out=ident[:], in_=ident[:], compare_op=ALU.not_equal, fill=1.0, base=0,
                                 pattern=[[-1, P]], channel_multiplier=1).then_inc(ident_ready, 1)
                gp.iota(iota8[:], pattern=[[1, E]], base=0, channel_multiplier=0, allow_small_or_imprecise_dtypes=True).then_inc(ident_ready, 1)
                gp.memset(zt[:], 0.0).then_inc(zt_ready, 1)
                gp.wait_ge(zt_ready, 1)
                gp.memset(zt[:].rearrange("p (n c) -> p n c", c=ROWW)[:, :, P:ROWW], FAR).then_inc(zt_ready, 1)
                for e in range(NE0):
                    gp.wait_ge(w_in[e % 2], 32 * (e // 2 + 1))
                    o = slice(e * 2 * H, (e + 1) * 2 * H)
                    gp.tensor_copy(w_hi[:, o], raw[e % 2][:]).then_inc(w_split, 1)
                    gp.wait_ge(w_split, 2 * e + 1)
                    gp.tensor_tensor(w_lo[:, o], raw[e % 2][:], w_hi[:, o], ALU.subtract).then_inc(w_split, 1)

            @block.tensor
            def _(pe):
                pe.wait_ge(ident_ready, 2)
                for k in range(B // 4):
                    pe.wait_ge(x_in[k % 2], 16 * (k // 2 + 1))
                    if k >= 2:
                        pe.wait_ge(xt_done, k - 1)
                    for j in range(4):
                        t = pe.transpose(w1_bank[k % 2][:, j * P:(j + 1) * P], xrows[k % 2][:, j * P:(j + 1) * P], ident[:])
                    t.then_inc(xt_pe, 1)
                pe.wait_ge(small_in, NSMALL)
                pe.transpose(gate_bank[:, 0:B], condr[:], ident[0:B, 0:B])
                pe.transpose(gate_bank[:, B:B + NVEC], vecs[0:NVEC, :], ident[0:NVEC, 0:NVEC]).then_inc(setup_pe, 1)
                pe.wait_ge(setup_dve, 2)
                for g in range(3):
                    t = pe.matmul(y_bank[0][:, g * B:(g + 1) * B], cv[:, g * P:(g + 1) * P], condT[:], start=(g == 0), stop=(g == 2), skip_group_check=True)
                t.then_inc(setup_pe, 1)
                pe.wait_ge(a1_in, 80)
                pe.matmul(y_bank[1][0:B, 0:P], condT[:], wq1[:], start=True, stop=True, skip_group_check=True)
                pe.matmul(y_bank[1][0:B, P:2 * P], condT[:], wk1[:], start=False, stop=True, skip_group_check=True).then_inc(a1_pe, 1)

                def prefill(g):
                    o = scan_bank[g % 2][:, 0:SG * 3 * B].rearrange("p (s c) -> p s c", s=SG)
                    xs = slice(g * SG * B, (g + 1) * SG * B)
                    for q in range(3):
                        dst = o[:, :, q * B:(q + 1) * B]
                        mm3(pe, dst, wx_hi[:, q * P:(q + 1) * P], wx_lo[:, q * P:(q + 1) * P],
                            x_hi[:, xs].rearrange("p (s b) -> p s b", b=B), x_lo[:, xs].rearrange("p (s b) -> p s b", b=B), q == 0, False)
                        for v in (vb_hi, vb_lo):
                            r = v[:, q * B:(q + 1) * B].unsqueeze(1).broadcast_to([P, SG, B])
                            t = pe.matmul(dst, identr[:], r, start=False, stop=False, skip_group_check=True)
                    t.then_inc(prefilled, 1)

                def scan_part(i, p):
                    t, half = p // 2, p % 2
                    o = scan_bank[(t // SG) % 2][:, (t % SG) * 3 * B:(t % SG + 1) * 3 * B]
                    if half == 0:
                        hp = h[:, ((t - 1) % STEPS) * B:((t - 1) % STEPS + 1) * B]
                        atleast(pe, h_ready, STEPS * i + t + 1)
                        pe.matmul(o[:, B:2 * B], uh[:, P:2 * P], hp, start=False, stop=False, skip_group_check=True)
                        pe.matmul(o[:, 0:B], uh[:, 0:P], hp, start=False, stop=False, skip_group_check=True).then_inc(zr_acc, 1)
                        if t % SG == 0 and t + SG < STEPS:
                            prefill(t // SG + 1)
                    else:
                        atleast(pe, rh_ready, STEPS * i + t + 1)
                        pe.matmul(o[:, 2 * B:3 * B], uh[:, 2 * P:3 * P], rh[:], start=False, stop=False, skip_group_check=True).then_inc(hh_acc, 1)

                def first_layer(c, u):
                    e, hb = u // HB, u % HB
                    if u >= 3:
                        atleast(pe, gelu_done, 2 * (UNITS * c + u - 2))
                    mm3(pe, w1_bank[u % 3][:], w1(w_hi, e, hb), w1(w_lo, e, hb), h_hi[:], h_lo[:], True, True).then_inc(w1_done, 1)

                def second_layer(c, u):
                    e, hb = u // HB, u % HB
                    k, first, last = group_of(u)
                    if first:
                        atleast(pe, y_read, NGRP * c + max(k - 1, 0))
                    pe.wait_ge(lo_ready, UNITS * c + u + 1)
                    mm3(pe, y_bank[k % 2][:], w2(w_hi, e, hb), w2(w_lo, e, hb), g_hi[u % 4][:], g_lo[u % 4][:], first, last).then_inc(w2_done, 1)

                def gates(i):
                    pe.wait_ge(h_ready, STEPS * (i + 1) + 1)
                    atleast(pe, wT_ready, i)
                    for k in range(4):
                        t = pe.matmul(gate_bank[:, k * E:(k + 1) * E], h[:, k * P:(k + 1) * P], rw[:], start=(k == 0), stop=(k == 3), skip_group_check=True)
                    t.then_inc(gate_acc, 1)

                def body(i, c, scan, ffn, more):
                    if ffn:
                        pe.wait_ge(h_split, 2 * (c + 1))
                    for u in range(UNITS):
                        if scan and u in PART_OF_SLOT:
                            scan_part(i, PART_OF_SLOT[u])
                        if ffn:
                            first_layer(c, u)
                            if u >= 2:
                                second_layer(c, u - 2)
                            if u == 4:
                                pe.wait_ge(gate_step, GSTEPS * (c + 1))
                                for k in range(4):
                                    t = pe.transpose(gate_bank[0:E, k * P:(k + 1) * P], wt[:, k * E:(k + 1) * E], ident[:])
                                t.then_inc(wT_acc, 1)
                    if ffn:
                        second_layer(c, UNITS - 2)
                    if more:
                        pe.wait_ge(x_split, 2 * (i + 2))
                        prefill(0)
                    if scan:
                        gates(i)
                    if ffn:
                        second_layer(c, UNITS - 1)

                pe.wait_ge(setup_dve, SETUP_DVE)
                pe.wait_ge(x_split, 2)
                prefill(0)
                body(0, None, True, False, True)
                pe.wait_ge(w_split, 2 * NE0)
                body(1, 0, True, True, True)
                with pe.Fori(2, NCH - 1) as i:
                    body(i, i - 1, True, True, True)
                body(NCH - 1, NCH - 2, True, True, False)
                body(None, NCH - 1, False, True, False)
                pe.wait_ge(a1_dve, A1_DVE)
                pe.transpose(gate_bank[:, 0:B], a1[:], ident[0:B, 0:B]).then_inc(a1_pe, 1)

            @block.scalar
            def _(act):
                act.wait_ge(ident_ready, 3)
                act.activation(th[:, 0:1], iota8[:, 0:1], ACT.Gelu).then_inc(gate_tanh, 1)
                for k in range(B // 4):
                    if k >= 2:
                        act.wait_ge(xt_pe, k - 1)
                    act.dma_start(xrows[k % 2][:].rearrange("p (b c) -> p b c", b=4),
                                  d["x"][4 * k:4 * k + 4].rearrange("b t c -> t b c")).then_inc(x_in[k % 2], 16)

                def scan_part(i, p):
                    t, half = p // 2, p % 2
                    o = scan_bank[(t // SG) % 2][:, (t % SG) * 3 * B:(t % SG + 1) * 3 * B]
                    if half == 0:
                        act.wait_ge(zr_acc, STEPS * i + t + 1)
                        act.activation(tzr[:], o[:, 0:2 * B], ACT.Tanh, scale=0.5).then_inc(zr_tanh, 1)
                    else:
                        act.wait_ge(hh_acc, STEPS * i + t + 1)
                        act.activation(hh[:], o[:, 2 * B:3 * B], ACT.Tanh).then_inc(hh_tanh, 1)

                def gelu(c, u):
                    act.wait_ge(w1_done, UNITS * c + u + 1)
                    atleast(act, lo_ready, UNITS * c + max(u - 1, 0))
                    atleast(act, w2_done, UNITS * c + max(u - 3, 0))
                    bias = vecT[:, R_SB1 + u:R_SB1 + u + 1]
                    act.activation(g_f[u % 2][:], w1_bank[u % 3][:], ACT.Gelu, bias=bias).then_inc(gelu_done, 1)
                    act.activation(g_hi[u % 4][:], w1_bank[u % 3][:], ACT.Gelu, bias=bias).then_inc(gelu_done, 1)

                def body(i, c, scan, ffn):
                    for u in range(UNITS + 1):
                        if scan and u in PART_OF_SLOT:
                            scan_part(i, PART_OF_SLOT[u])
                        if ffn and u >= 1:
                            gelu(c, u - 1)
                        if ffn and u == 1:
                            act.wait_ge(gate_step, GSTEPS * c + 6)
                            act.activation(th[:], dlt[:], ACT.Tanh, scale=0.5).then_inc(gate_tanh, 1)
                        if ffn and u == 5:
                            act.wait_ge(wT_acc, c + 1)
                            act.activation(wT[:], gate_bank[0:E, :], ACT.Copy).then_inc(wT_ready, 1)

                body(0, None, True, False)
                body(1, 0, True, True)
                with act.Fori(2, NCH - 1) as i:
                    body(i, i - 1, True, True)
                body(NCH - 1, NCH - 2, True, True)
                body(None, NCH - 1, False, True)
                act.wait_ge(a1_dve, 5)
                act.activation(e1[:], a1[:], ACT.Exp, bias=s1[:, 1:2], accum_out=s1[:, 2:3]).then_inc(a1_act, 1)

            @block.vector
            def _(dve):
                dve.memset(h[:, CH - B:CH], 0.0).then_inc(h_ready, 1)
                for k in range(B // 4):
                    dve.wait_ge(xt_pe, k + 1)
                    dve.tensor_copy(xT_tb[:, :, 4 * k:4 * k + 4], w1_bank[k % 2][:].rearrange("p (b t) -> p t b", b=4)).then_inc(xt_done, 1)
                dve.wait_ge(setup_pe, 1)
                dve.tensor_copy(condT[:], gate_bank[:, 0:B]).then_inc(setup_dve, 1)
                dve.tensor_copy(vecT[:], gate_bank[:, B:B + NVEC]).then_inc(setup_dve, 1)
                dve.tensor_scalar(uh[:, 2 * P:3 * P], uh[:, 2 * P:3 * P], 0.5, None, ALU.mult).then_inc(setup_dve, 1)
                dve.tensor_copy(wx_hi[:], wx[:]).then_inc(setup_dve, 1)
                dve.wait_ge(ident_ready, 3)
                dve.tensor_copy(identr[:], ident[:]).then_inc(setup_dve, 1)
                dve.wait_ge(setup_dve, 5)
                dve.tensor_tensor(wx_lo[:], wx[:], wx_hi[:], ALU.subtract).then_inc(setup_dve, 1)
                dve.tensor_tensor(sbias[:], vecT[:, R_SB2:R_SB2 + 1], vecT[:, R_SB2 + 1:R_SB2 + 2], ALU.add).then_inc(setup_dve, 1)
                dve.wait_ge(setup_dve, 7)
                dve.tensor_scalar(sbias[:], sbias[:], 0.5, None, ALU.mult).then_inc(setup_dve, 1)
                dve.wait_ge(setup_pe, 2)
                for g, r in enumerate((R_BZ, R_BR, R_BH)):
                    dve.tensor_scalar(vb[:, g * B:(g + 1) * B], y_bank[0][:, g * B:(g + 1) * B], vecT[:, r:r + 1], None, ALU.add).then_inc(setup_dve, 1)
                dve.wait_ge(setup_dve, 11)
                dve.tensor_copy(vb_hi[:], vb[:]).then_inc(setup_dve, 1)
                dve.wait_ge(setup_dve, 12)
                dve.tensor_tensor(vb_lo[:], vb[:], vb_hi[:], ALU.subtract).then_inc(setup_dve, 1)
                dve.wait_ge(a1_pe, 1)
                dve.tensor_tensor(q1[:], y_bank[1][0:B, 0:P], bq1[:], ALU.add).then_inc(a1_dve, 1)
                dve.tensor_tensor(k1[:], y_bank[1][0:B, P:2 * P], bk1[:], ALU.add).then_inc(a1_dve, 1)
                dve.wait_ge(a1_dve, 2)
                dve.tensor_tensor_reduce(out=e1[:], in0=q1[:], in1=k1[:], scale=1.0, scalar=0.0, op0=ALU.mult, op1=ALU.add,
                                         accum_out=s1[:, 0:1]).then_inc(a1_dve, 1)
                dve.wait_ge(a1_dve, 3)
                dve.tensor_scalar(a1[:], s1[:, 0:1].broadcast_to([B, P]), SCALE, None, ALU.mult).then_inc(a1_dve, 1)
                dve.wait_ge(a1_dve, 4)
                dve.tensor_reduce(s1[:, 1:2], a1[:], AX.X, ALU.max, negate=True).then_inc(a1_dve, 1)

                def split_x(i):
                    atleast(dve, prefilled, SG * i)
                    src = xT[:, bass.ds(i * CH, CH)]
                    dve.tensor_scalar(x_hi[:], src, 1.0, None, ALU.mult).then_inc(x_split, 1)
                    dve.wait_ge(x_split, 2 * i + 1)
                    dve.tensor_tensor(x_lo[:], src, x_hi[:], ALU.subtract).then_inc(x_split, 1)

                def scan_part(i, p):
                    t, half = p // 2, p % 2
                    n = STEPS * i + t + 1
                    hp = h[:, ((t - 1) % STEPS) * B:((t - 1) % STEPS + 1) * B]
                    if half == 0:
                        dve.wait_ge(zr_tanh, n)
                        dve.scalar_tensor_tensor(out=rh[:], in0=tzr[:, B:2 * B], scalar=1.0, in1=hp, op0=ALU.add, op1=ALU.mult).then_inc(rh_ready, 1)
                        dve.tensor_scalar(z[:], tzr[:, 0:B], 0.5, 0.5, ALU.mult, ALU.add).then_inc(z_ready, 1)
                        dve.wait_ge(z_ready, n)
                        dve.scalar_tensor_tensor(out=kept[:], in0=z[:], scalar=-1.0, in1=hp, op0=ALU.add, op1=ALU.mult).then_inc(kept_ready, 1)
                    else:
                        dve.wait_ge(hh_tanh, n)
                        dve.tensor_tensor(zhh[:], z[:], hh[:], ALU.mult).then_inc(zhh_ready, 1)
                        dve.wait_ge(zhh_ready, n)
                        dve.wait_ge(kept_ready, n)
                        dve.tensor_tensor(h[:, t * B:(t + 1) * B], zhh[:], kept[:], ALU.subtract).then_inc(h_ready, 1)

                def low_part(c, u):
                    dve.wait_ge(gelu_done, 2 * (UNITS * c + u + 1))
                    atleast(dve, w2_done, UNITS * c + max(u - 3, 0))
                    dve.tensor_tensor(g_lo[u % 4][:], g_f[u % 2][:], g_hi[u % 4][:], ALU.subtract).then_inc(lo_ready, 1)

                def combine(c, k):
                    last = NSH * HB + k * HB
                    dve.wait_ge(w2_done, UNITS * c + last)
                    src = xT[:, bass.ds(c * CH, CH)]
                    y = y_bank[k % 2][:]
                    atleast(dve, acc_ready, NGRP * c + k)
                    if k == 0:
                        dve.scalar_tensor_tensor(out=acc[:], in0=y, scalar=0.5, in1=src, op0=ALU.mult, op1=ALU.add).then_inc(y_read, 1)
                        dve.wait_ge(y_read, NGRP * c + 1)
                        dve.tensor_scalar(acc[:], acc[:], sbias[:], None, ALU.add).then_inc(acc_ready, 1)
                        return
                    if k == 1:
                        dve.wait_ge(wb_ready, 16 * (c + 1))
                    dve.scalar_tensor_tensor(out=tmp[:], in0=y, scalar=vecT[:, R_B2 + k - 1:R_B2 + k], in1=wb[:, (k - 1) * CH:k * CH],
                                             op0=ALU.add, op1=ALU.mult).then_inc(y_read, 1)
                    dve.wait_ge(y_read, NGRP * c + k + 1)
                    if k < E:
                        dve.tensor_tensor(acc[:], acc[:], tmp[:], ALU.add).then_inc(acc_ready, 1)
                    else:
                        dve.tensor_tensor(x1T_tb[:, bass.ds(c * STEPS, STEPS), :], acc[:].rearrange("p (t b) -> p t b", b=B),
                                          tmp[:].rearrange("p (t b) -> p t b", b=B), ALU.add).then_inc(acc_ready, 1)

                def v3(a, w):
                    return a[:].rearrange("p (k e) -> p k e", e=w)

                def gate_a(c):
                    n = GSTEPS * c
                    dve.wait_ge(gate_acc, c + 1)
                    dve.tensor_tensor(v3(lg, E), gate_bank[:, 0:4 * E].rearrange("p (k e) -> p k e", e=E),
                                      rbb[:].unsqueeze(1).broadcast_to([P, 4, E]), ALU.add).then_inc(gate_step, 1)
                    dve.wait_ge(gate_step, n + 1)
                    dve.tensor_scalar(lgmax[:], lg[:, 0:1], 1.0, None, ALU.mult)
                    for k in range(4):
                        dve.max(mx[:, k * 8:(k + 1) * 8], lg[:, k * E:(k + 1) * E]).then_inc(gate_step, 1)
                    dve.wait_ge(gate_step, n + 5)
                    dve.tensor_tensor(dlt[:].unsqueeze(2), v3(mx, 8)[:, :, 0:1], v3(mx, 8)[:, :, 1:2], ALU.subtract).then_inc(gate_step, 1)
                    for k in range(4):
                        dve.max_index(ix[:, k * 8:(k + 1) * 8], mx[:, k * 8:(k + 1) * 8], lg[:, k * E:(k + 1) * E]).then_inc(gate_step, 1)
                    dve.wait_ge(gate_step, n + 10)
                    dve.tensor_scalar(v3(ixf, 2), v3(ix, 8)[:, :, 0:2], 1.0, None, ALU.mult).then_inc(gate_step, 1)

                def gate_b(c):
                    n = GSTEPS * c
                    dve.wait_ge(gate_tanh, c + 2)
                    dve.tensor_scalar(p0[:], th[:], 0.5, 0.5, ALU.mult, ALU.add).then_inc(gate_step, 1)
                    dve.tensor_scalar(p1[:], th[:], -0.5, 0.5, ALU.mult, ALU.add).then_inc(gate_step, 1)
                    dve.wait_ge(gate_step, n + 11)
                    io = iota8[:].unsqueeze(1).broadcast_to([P, 4, E])
                    for q, oh in enumerate((oh0, oh1)):
                        dve.tensor_tensor(v3(oh, E), io, v3(ixf, 2)[:, :, q:q + 1].broadcast_to([P, 4, E]), ALU.is_equal).then_inc(gate_step, 1)
                    dve.wait_ge(gate_step, n + 15)
                    for oh, p in ((oh0, p0), (oh1, p1)):
                        dve.tensor_tensor(v3(oh, E), v3(oh, E), p[:].unsqueeze(2).broadcast_to([P, 4, E]), ALU.mult).then_inc(gate_step, 1)
                    dve.wait_ge(gate_step, n + 17)
                    dve.tensor_tensor(wt[:], oh0[:], oh1[:], ALU.add).then_inc(gate_step, 1)

                def split_h(i, c):
                    dve.wait_ge(h_ready, STEPS * (i + 1) + 1)
                    if c is not None:
                        dve.wait_ge(w1_done, UNITS * (c + 1))
                    dve.tensor_copy(h_hi[:], h[:]).then_inc(h_split, 1)
                    dve.wait_ge(h_split, 2 * i + 1)
                    dve.tensor_tensor(h_lo[:], h[:], h_hi[:], ALU.subtract).then_inc(h_split, 1)

                def body(i, c, scan, ffn, more):
                    for u in range(UNITS + 1):
                        if scan and u in PART_OF_SLOT:
                            scan_part(i, PART_OF_SLOT[u])
                        if ffn and u >= 1:
                            low_part(c, u - 1)
                        if ffn and u == 1:
                            gate_a(c)
                        if ffn and u == 3:
                            gate_b(c)
                        if ffn:
                            for k in range(NGRP - 1):
                                if u == NSH * HB + k * HB + 2:
                                    combine(c, k)
                        if more and u == part_slot(2 * (STEPS - SG)) + 2:
                            split_x(i + 1)
                    if scan:
                        split_h(i, c)
                    if ffn:
                        combine(c, NGRP - 1)

                split_x(0)
                body(0, None, True, False, True)
                body(1, 0, True, True, True)
                with dve.Fori(2, NCH - 1) as i:
                    body(i, i - 1, True, True, True)
                body(NCH - 1, NCH - 2, True, True, False)
                body(None, NCH - 1, False, True, False)
                dve.wait_ge(a1_act, 1)
                dve.reciprocal(s1[:, 3:4], s1[:, 2:3]).then_inc(a1_dve, 1)
                dve.wait_ge(a1_dve, 6)
                dve.tensor_scalar(a1[:], e1[:], s1[:, 3:4], alph[:], ALU.mult, ALU.mult).then_inc(a1_dve, 1)
                dve.wait_ge(a1_pe, 2)
                dve.tensor_copy(alphaT[:], gate_bank[:, 0:B])


NSMALL = 23 * 16
SETUP_DVE = 13
A1_DVE = 7


def phase_attention(nc, d, m):
    bank, ident, identr, vecT = m["bank"], m["ident"], m["identr"], m["vecT"]
    condT, xT, x1T, wide, alphaT, iota8 = (m[k] for k in ("condT", "xT", "x1T", "wide", "alphaT", "iota8"))
    w_hi, w_lo, raw, slots = m["w_hi"], m["w_lo"], m["raw"], m["slots"]
    gates_all, firsts, firsts_u = m["gates_all"], m["firsts"], m["firsts_u"]
    hs, dispatch, hs_ready, hs_free, pos_ready, posi, hid_kept, wts_in = (m[k] for k in ("hs", "dispatch", "hs_ready", "hs_free", "pos_ready", "posi", "hid_kept", "wts_in"))
    x1rows, hid = xT, wide
    hid3 = hid[:].rearrange("p (b c) -> p b c", c=ROWW)
    GT = GRP * P
    TE = TOPK * E
    ME = GRP * TE
    BF16 = mybir.dt.bfloat16

    with ExitStack() as ctx:
        def sb(name, shape, dt=F32):
            return ctx.enter_context(nc.sbuf_tensor(name, shape, dt))

        def sem(name):
            return ctx.enter_context(nc.semaphore(name))

        wv1 = sb("wv1", [P, P])
        bvc = sb("bvc", [P, 1])
        cvT = sb("cvT", [P, B])
        wg = sb("wg", [P, E])
        lowtri = sb("lowtri", [P, P])
        lowtri_b = sb("lowtri_b", [P, P], BF16)
        ones_b = sb("ones_b", [P, P], BF16)
        xg = sb("xg", [P, GT])
        xg_hi = sb("xg_hi", [P, GT], F32R)
        xg_lo = sb("xg_lo", [P, GT], F32R)
        qT = sb("qT", [P, GT])
        kT = sb("kT", [P, GT])
        vT = sb("vT", [P, GT])
        v = [sb(f"v{i}", [P, GT]) for i in range(2)]
        smax = sb("smax", [P, GRP])
        nsmax = sb("nsmax", [P, GRP])
        pr = sb("pr", [P, GT])
        rs = sb("rs", [P, GRP])
        rinv = sb("rinv", [P, GRP])
        am = sb("am", [P, GT])
        amT = sb("amT", [P, GT])
        hg = sb("hg", [P, GT])
        hT = sb("hT", [P, GT])
        lmax = sb("lmax", [P, GRP]); lsh = sb("lsh", [P, GRP * E]); lex = sb("lex", [P, GRP * E])
        lsum = sb("lsum", [P, GRP]); lrec = sb("lrec", [P, GRP]); sc = sb("sc", [P, GRP * E]); first_sc = sb("first_sc", [P, 1])
        mx = sb("mx8", [P, GRP * 8]); ix = sb("ix8", [P, GRP * 8], U32); ixf = sb("ixf8", [P, GRP * TOPK])
        den = sb("den", [P, GRP]); dinv = sb("dinv", [P, GRP])
        mask = sb("mask", [P, ME], BF16)
        run = sb("run", [P, TE])
        loc = sb("loc", [P, ME]); sel = sb("sel", [P, ME])
        rank = sb("rank", [P, GRP * TOPK])
        cmul = sb("cmul", [P, TOPK]); cadd = sb("cadd", [P, TOPK])
        over = sb("over", [P, GRP * TOPK]); pos = sb("pos", [P, GRP * TOPK])
        mask1 = sb("mask1", [P, B * E]); rank_all = sb("rank_all", [P, B * TOPK])
        sel1 = sb("sel1", [P, B * E]); before1 = sb("before1", [P, B]); keep = sb("keep", [P, B * TOPK])

        att_in = sem("att_in"); w_conv = sem("att_w_ready"); const_step = sem("const_step"); run_zero = sem("run_zero"); cv_acc = sem("cv_acc")
        x_in = sem("xg_in"); x_ready = sem("x_ready"); q_acc = sem("q_acc"); k_acc = sem("k_acc"); v_acc = sem("v_acc")
        q_ready = sem("q_ready"); k_ready = sem("k_ready"); vT_ready = sem("vT_ready"); vt_acc = sem("vt_acc"); v_ready = sem("v_ready")
        rows_acc = sem("rows_acc"); rows_done = sem("rows_done")
        s_acc = sem("s_acc"); smax_ready = sem("smax_ready"); p_ready = sem("p_ready"); rinv_ready = sem("rinv_ready"); a_ready = sem("a_ready")
        aT_acc = sem("aT_acc"); aT_ready = sem("aT_ready"); hid_acc = sem("hid_acc"); hg_ready = sem("hg_ready")
        hidT_acc = sem("hidT_acc"); hidT_ready = sem("hidT_ready"); logit_acc = sem("logit_acc"); 
        r_step = sem("r_step"); l_exp = sem("l_exp"); rank_acc = sem("rank_acc"); id_step = sem("id_step")
        f_step = sem("f_step")

        LOADS = 6
        bq, bk, bv_, br, bs, ba, bh, bm = bank
        WQ, WK, WV = 0, 1, 2

        def v3(a, w):
            return a[:].rearrange("p (k e) -> p k e", e=w)

        mask4 = mask[:].rearrange("p (k q e) -> p k q e", q=TOPK, e=E)

        def pipeline(eng, turn):
            turn(-1, 1, True, False, False, False)
            turn(0, 0, True, True, False, False)
            turn(1, 1, True, True, True, False)
            turn(2, 0, True, True, True, True)
            with eng.Fori(0, (NG - 4) // 2) as k:
                turn(k * 2 + 3, 1, True, True, True, True)
                turn(k * 2 + 4, 0, True, True, True, True)
            turn(NG - 1, 1, False, True, True, True)
            turn(NG, 0, False, False, True, True)
            turn(NG + 1, 1, False, False, False, True)

        with nc.Block() as block:
            @block.sync
            def _(sp):
                for dst, src in ((raw[0][:, 0:P], d["L1_cond_Wq2"]), (raw[0][:, P:2 * P], d["L1_cond_Wk2"]),
                                 (raw[0][:, 2 * P:3 * P], d["L1_cond_Wv"][P:2 * P, :]), (wv1[:], d["L1_cond_Wv"][0:P, :]),
                                 (bvc[:], d["L1_cond_bv"].rearrange("(p a) -> p a", a=1)),
                                 (wg[:], d["L1_ffn_wg"])):
                    sp.dma_start(dst, src).then_inc(att_in, 16)
                sp.dma_start(xg[:], x1T[:, 0:GT]).then_inc(x_in, 16)

                def turn(i, par, attend, load):
                    if load:
                        sp.wait_ge(rows_acc, i + 2)
                        sp.dma_start(xg[:], x1T[:, bass.ds((i + 2) * GT, GT)]).then_inc(x_in, 16)
                    if attend:
                        b = i - 1
                        sp.wait_ge(hg_ready, b + 1)
                        sp.dma_start(hid3[:, bass.ds(b * GRP, GRP), 0:P], v3(hg, P)).then_inc(hid_kept, 16)
                        if isinstance(b, int) and b == 0:
                            sp.wait_ge(hid_kept, 16)
                        else:
                            sp.wait_ge(hs_free, b)
                        sp.dma_start(hs[1 - par][:], hid[:, bass.ds(b * GRP * ROWW, GRP * ROWW)]).then_inc(hs_ready, 16)

                turn(-1, 1, False, True)
                turn(0, 0, False, True)
                turn(1, 1, True, True)
                with sp.Fori(0, (NG - 4) // 2) as k:
                    turn(k * 2 + 2, 0, True, True)
                    turn(k * 2 + 3, 1, True, True)
                sp.wait_ge(w_conv, 4)
                for e in range(2):
                    load_expert_weights(sp, d, raw, wts_in, e)
                turn(NG - 2, 0, True, False)
                turn(NG - 1, 1, True, False)
                turn(NG, 0, True, False)

            @block.gpsimd
            def _(gp):
                gp.memset(lowtri[:], 1.0).then_inc(const_step, 1)
                gp.wait_ge(const_step, 1)
                gp.affine_select(out=lowtri[:], in_=lowtri[:], compare_op=ALU.is_ge, fill=0.0, base=0, pattern=[[1, P]],
                                 channel_multiplier=-1).then_inc(const_step, 1)
                gp.iota(hid3[:, :, P:ROWW], pattern=[[P, B], [1, 1]], base=0, channel_multiplier=1, allow_small_or_imprecise_dtypes=True).then_inc(id_step, 1)
                last_slot = gp.to_reg(SLOT_ROWS - 1)
                dispatch(gp, last_slot, 0, 0, 0)
                with gp.Fori(0, (NG - 4) // 2) as k:
                    dispatch(gp, last_slot, k * 2 + 1, 1, k + 1)
                    dispatch(gp, last_slot, k * 2 + 2, 0, k + 1)
                dispatch(gp, last_slot, NG - 3, 1, (NG - 2) // 2)
                dispatch(gp, last_slot, NG - 2, 0, (NG - 2) // 2)

            @block.tensor
            def _(pe):
                def wpart(t, q):
                    return t[:, q * P:(q + 1) * P]

                def jcols(j, w=P):
                    return slice(j * w, (j + 1) * w)

                pe.wait_ge(att_in, 16 * LOADS)
                pe.matmul(bm[:, 0:B], wv1[:], condT[:], start=True, stop=True).then_inc(cv_acc, 1)
                pe.wait_ge(w_conv, 5)
                pe.wait_ge(id_step, 1)

                def turn(i, par, project, soften, attend, route):
                    a, b, r = i + 1, i - 1, i - 2
                    if soften:
                        pe.wait_ge(q_ready, i + 1)
                        pe.wait_ge(k_ready, i + 1)
                        atleast(pe, p_ready, GRP * i)
                        for j in range(GRP):
                            t = pe.matmul(bs[:, jcols(j)], qT[:, jcols(j)], kT[:, jcols(j)], start=(j == 0), stop=True, skip_group_check=True)
                        t.then_inc(s_acc, 1)
                    if attend:
                        pe.wait_ge(a_ready, (b + 1) * GRP)
                        atleast(pe, hidT_ready, b)
                        for j in range(GRP):
                            t = pe.transpose(ba[:, jcols(j)], am[:, jcols(j)], ident[:])
                        t.then_inc(aT_acc, 1)
                    if project:
                        pe.wait_ge(x_ready, (a + 1) * 2)
                        atleast(pe, q_ready, a)
                        atleast(pe, k_ready, a)
                        atleast(pe, vT_ready, a)
                        if route:
                            atleast(pe, pos_ready, i - 2)
                        mm3(pe, bq[:], wpart(w_hi, WQ), wpart(w_lo, WQ), xg_hi[:], xg_lo[:], True, True).then_inc(q_acc, 1)
                        mm3(pe, bk[:], wpart(w_hi, WK), wpart(w_lo, WK), xg_hi[:], xg_lo[:], True, True).then_inc(k_acc, 1)
                        mm3(pe, bv_[:], wpart(w_hi, WV), wpart(w_lo, WV), xg_hi[:], xg_lo[:], True, True).then_inc(v_acc, 1)
                        atleast(pe, v_ready, a)
                        for j in range(GRP):
                            t = pe.transpose(br[:, jcols(j)], xg[:, jcols(j)], ident[:])
                        t.then_inc(rows_acc, 1)
                    if attend:
                        pe.wait_ge(aT_ready, b + 1)
                        pe.wait_ge(v_ready, b + 1)
                        for j in range(GRP):
                            t = pe.matmul(bh[:, jcols(j)], amT[:, jcols(j)], v[1 - par][:, jcols(j)], start=(j == 0), stop=True, skip_group_check=True)
                        t.then_inc(hid_acc, 1)
                    if project:
                        pe.wait_ge(vT_ready, a + 1)
                        pe.wait_ge(rows_done, a + 1)
                        for j in range(GRP):
                            t = pe.transpose(br[:, jcols(j)], vT[:, jcols(j)], ident[:])
                        t.then_inc(vt_acc, 1)
                    if route:
                        pe.wait_ge(r_step, RSTEPS * r + R_MASKS)
                        if project:
                            pe.wait_ge(k_ready, a + 1)
                        cum = bk[:, 0:ME]
                        pe.matmul(cum, lowtri_b[:], mask[:], start=True, stop=False, skip_group_check=True)
                        for j in range(GRP - 1):
                            later = cum[:, (j + 1) * TE:ME].rearrange("p (k c) -> p k c", c=TE)
                            pe.matmul(later, ones_b[:], mask[:, jcols(j, TE)].unsqueeze(1).broadcast_to([P, GRP - 1 - j, TE]),
                                      start=False, stop=False, skip_group_check=True)
                        for j in range(GRP):
                            t = pe.matmul(bk[:, ME:ME + TE], ones_b[:], mask[:, jcols(j, TE)], start=False, stop=(j == GRP - 1), skip_group_check=True)
                        t.then_inc(rank_acc, 1)
                    if attend:
                        pe.wait_ge(hg_ready, b + 1)
                        for j in range(GRP):
                            t = pe.transpose(ba[:, jcols(j)], hg[:, jcols(j)], ident[:])
                        t.then_inc(hidT_acc, 1)
                        pe.wait_ge(hidT_ready, b + 1)
                        for j in range(GRP):
                            t = pe.matmul(bm[:, jcols(j, E)], hT[:, jcols(j)], wg[:], start=(j == 0), stop=True, skip_group_check=True)
                        t.then_inc(logit_acc, 1)

                pipeline(pe, turn)

            @block.scalar
            def _(act):
                def turn(i, par, project, soften, attend, route):
                    a, b, r = i + 1, i - 1, i - 2
                    if route:
                        act.wait_ge(r_step, RSTEPS * r + R_SHIFTED)
                        act.activation(lex[:], lsh[:], ACT.Exp).then_inc(l_exp, 1)
                    if attend:
                        act.wait_ge(aT_acc, b + 1)
                        atleast(act, hid_acc, b)
                        act.activation(amT[:], ba[:], ACT.Copy).then_inc(aT_ready, 1)
                    if soften:
                        act.wait_ge(smax_ready, (i + 1) * 2)
                        atleast(act, a_ready, GRP * i)
                        for j in range(GRP):
                            c = slice(j * P, (j + 1) * P)
                            act.activation(pr[:, c], bs[:, c], ACT.Exp, bias=nsmax[:, j:j + 1], scale=SCALE, accum_out=rs[:, j:j + 1]).then_inc(p_ready, 1)
                    if project:
                        act.wait_ge(q_acc, a + 1)
                        atleast(act, s_acc, a)
                        act.activation(qT[:], bq[:], ACT.Identity, bias=vecT[:, R_BQ2:R_BQ2 + 1]).then_inc(q_ready, 1)
                        act.wait_ge(k_acc, a + 1)
                        act.activation(kT[:], bk[:], ACT.Identity, bias=vecT[:, R_BK2:R_BK2 + 1]).then_inc(k_ready, 1)
                        act.wait_ge(rows_acc, a + 1)
                        act.activation(x1rows[:, bass.ds(a * GT, GT)], br[:], ACT.Identity).then_inc(rows_done, 1)
                    if attend:
                        act.wait_ge(hid_acc, b + 1)
                        atleast(act, hid_kept, 16 * b)
                        act.activation(hg[:], bh[:], ACT.Copy).then_inc(hg_ready, 1)
                    if project:
                        act.wait_ge(vt_acc, a + 1)
                        atleast(act, hid_acc, i)
                        act.activation(v[1 - par][:], br[:], ACT.Copy).then_inc(v_ready, 1)

                pipeline(act, turn)

            @block.vector
            def _(dve):
                dve.memset(run[:], 0.0).then_inc(run_zero, 1)
                for q in range(TOPK):
                    dve.memset(cmul[:, q:q + 1], float(CAP * (TOPK - q))).then_inc(run_zero, 1)
                    dve.memset(cadd[:, q:q + 1], float(q * E * 2 * CAP - 1)).then_inc(run_zero, 1)
                dve.wait_ge(const_step, 2)
                dve.tensor_copy(lowtri_b[:], lowtri[:]).then_inc(w_conv, 1)
                dve.tensor_scalar(ones_b[:], lowtri[:], 0.0, 1.0, ALU.mult, ALU.add).then_inc(w_conv, 1)
                dve.wait_ge(att_in, 16 * LOADS)
                dve.tensor_copy(w_hi[:, 0:3 * P], raw[0][:, 0:3 * P]).then_inc(w_conv, 1)
                dve.wait_ge(w_conv, 3)
                dve.tensor_tensor(w_lo[:, 0:3 * P], raw[0][:, 0:3 * P], w_hi[:, 0:3 * P], ALU.subtract).then_inc(w_conv, 1)
                dve.wait_ge(cv_acc, 1)
                dve.tensor_scalar(cvT[:], bm[:, 0:B], bvc[:], None, ALU.add).then_inc(w_conv, 1)
                dve.wait_ge(w_conv, 5)
                dve.wait_ge(run_zero, 1 + 2 * TOPK)

                def split(g):
                    dve.wait_ge(x_in, (g + 1) * 16)
                    atleast(dve, v_acc, g)
                    dve.tensor_copy(xg_hi[:], xg[:]).then_inc(x_ready, 1)
                    dve.wait_ge(x_ready, g * 2 + 1)
                    dve.tensor_tensor(xg_lo[:], xg[:], xg_hi[:], ALU.subtract).then_inc(x_ready, 1)

                def turn(i, par, project, soften, attend, route):
                    a, b, r = i + 1, i - 1, i - 2
                    n = RSTEPS * r
                    step = [0]

                    def did(ins):
                        step[0] += 1
                        ins.then_inc(r_step, 1)
                        return step[0]

                    def after(k):
                        dve.wait_ge(r_step, n + k)

                    lg = bm[:, 0:GRP * E].rearrange("p (k e) -> p k e", e=E)
                    if route:
                        dve.wait_ge(logit_acc, r + 1)
                        k = did(dve.tensor_reduce(lmax[:], lg, AX.X, ALU.max))
                        after(k)
                        k = did(dve.tensor_tensor(v3(lsh, E), lg, lmax[:].unsqueeze(2).broadcast_to([P, GRP, E]), ALU.subtract))
                        assert k == R_SHIFTED
                    if soften:
                        dve.wait_ge(s_acc, i + 1)
                        dve.tensor_reduce(smax[:], bs[:].rearrange("p (k c) -> p k c", c=P), AX.X, ALU.max).then_inc(smax_ready, 1)
                        dve.wait_ge(smax_ready, i * 2 + 1)
                        dve.tensor_scalar(nsmax[:], smax[:], -SCALE, None, ALU.mult).then_inc(smax_ready, 1)
                    if route:
                        dve.wait_ge(l_exp, r + 1)
                        k = did(dve.tensor_reduce(lsum[:], v3(lex, E), AX.X, ALU.add))
                        after(k)
                        k = did(dve.reciprocal(lrec[:], lsum[:]))
                        after(k)
                        k = did(dve.tensor_tensor(v3(sc, E), v3(lex, E), lrec[:].unsqueeze(2).broadcast_to([P, GRP, E]), ALU.mult))
                        after(k)
                        did(dve.tensor_scalar(first_sc[:], sc[:, 0:1], 1.0, None, ALU.mult))
                        for j in range(GRP):
                            k = did(dve.max(mx[:, j * 8:(j + 1) * 8], sc[:, j * E:(j + 1) * E]))
                        after(k)
                        did(dve.tensor_tensor(den[:].unsqueeze(2), v3(mx, 8)[:, :, 0:1], v3(mx, 8)[:, :, 1:2], ALU.add))
                        for j in range(GRP):
                            k = did(dve.max_index(ix[:, j * 8:(j + 1) * 8], mx[:, j * 8:(j + 1) * 8], sc[:, j * E:(j + 1) * E]))
                        after(k)
                        k = did(dve.tensor_scalar(v3(ixf, TOPK), v3(ix, 8)[:, :, 0:TOPK], 1.0, None, ALU.mult))
                        kd = did(dve.tensor_scalar(den[:], den[:], EPS_GATE, None, ALU.max))
                        after(k)
                        for q in range(TOPK):
                            k = did(dve.tensor_tensor(mask4[:, :, q, :], iota8[:].unsqueeze(1).broadcast_to([P, GRP, E]),
                                                      v3(ixf, TOPK)[:, :, q:q + 1].broadcast_to([P, GRP, E]), ALU.is_equal))
                        assert k == R_MASKS
                        after(kd)
                        kr = did(dve.reciprocal(dinv[:], den[:]))
                    if soften:
                        dve.wait_ge(p_ready, (i + 1) * GRP)
                        dve.reciprocal(rinv[:], rs[:]).then_inc(rinv_ready, 1)
                        dve.wait_ge(rinv_ready, i + 1)
                        atleast(dve, aT_acc, i)
                        for j in range(GRP):
                            js = slice(j * P, (j + 1) * P)
                            dve.tensor_scalar(am[:, js], pr[:, js], rinv[:, j:j + 1], alphaT[:, bass.ds(i * GRP + j, 1)], ALU.mult, ALU.subtract).then_inc(a_ready, 1)
                    if project:
                        dve.wait_ge(v_acc, a + 1)
                        atleast(dve, vt_acc, a)
                        dve.tensor_tensor(v3(vT, P), bv_[:].rearrange("p (k c) -> p k c", c=P),
                                          cvT[:, bass.ds(a * GRP, GRP)].unsqueeze(2).broadcast_to([P, GRP, P]), ALU.add).then_inc(vT_ready, 1)
                    if route:
                        after(kr)
                        ga = gates_all[:].rearrange("p (k q) -> p k q", q=TOPK)
                        did(dve.tensor_tensor(ga[:, bass.ds(r * GRP, GRP), :], v3(mx, 8)[:, :, 0:TOPK], dinv[:].unsqueeze(2).broadcast_to([P, GRP, TOPK]), ALU.mult))
                        did(dve.tensor_scalar(mask1[:].rearrange("p (k e) -> p k e", e=E)[:, bass.ds(r * GRP, GRP), :], mask4[:, :, 1, :], 1.0, None, ALU.mult))
                        dve.wait_ge(rank_acc, r + 1)
                        cum = bk[:, 0:ME].rearrange("p (k c) -> p k c", c=TE)
                        kl = did(dve.tensor_tensor(v3(loc, TE), cum, run[:].unsqueeze(1).broadcast_to([P, GRP, TE]), ALU.add))
                        kp = did(dve.tensor_tensor(v3(pos, TOPK), v3(ixf, TOPK), cmul[:].unsqueeze(1).broadcast_to([P, GRP, TOPK]), ALU.mult))
                        after(kl)
                        k = did(dve.tensor_tensor(sel[:], loc[:], mask[:], ALU.mult))
                        did(dve.tensor_tensor(run[:], run[:], bk[:, ME:ME + TE], ALU.add))
                        after(k)
                        k = did(dve.tensor_reduce(rank[:].rearrange("p (k q) -> p k q", q=TOPK), sel[:].rearrange("p (k q e) -> p k q e", q=TOPK, e=E), AX.X, ALU.add))
                    if attend:
                        dve.wait_ge(hidT_acc, b + 1)
                        dve.tensor_copy(hT[:], ba[:]).then_inc(hidT_ready, 1)
                    if route:
                        kq = did(dve.tensor_tensor(v3(pos, TOPK), v3(pos, TOPK), cadd[:].unsqueeze(1).broadcast_to([P, GRP, TOPK]), ALU.add))
                        after(k)
                        ko = did(dve.tensor_scalar(over[:], rank[:], float(CAP), FAR, ALU.is_gt, ALU.mult))
                        did(dve.tensor_scalar(rank_all[:, bass.ds(r * GRP * TOPK, GRP * TOPK)], rank[:], 1.0, None, ALU.mult))
                        after(kq)
                        k = did(dve.tensor_tensor(pos[:], pos[:], rank[:], ALU.add))
                        after(k)
                        atleast(dve, hs_free, r)
                        dve.tensor_tensor(posi[par][:], pos[:], over[:], ALU.add).then_inc(pos_ready, 1)
                        assert step[0] == RSTEPS, step[0]
                    if project and not (isinstance(i, int) and i == NG - 2):
                        split(i + 2)

                split(0)
                turn(-1, 1, True, False, False, False)
                turn(0, 0, True, True, False, False)
                turn(1, 1, True, True, True, False)
                turn(2, 0, True, True, True, True)
                with dve.Fori(0, (NG - 6) // 2) as k:
                    turn(k * 2 + 3, 1, True, True, True, True)
                    turn(k * 2 + 4, 0, True, True, True, True)
                turn(NG - 3, 1, True, True, True, True)
                turn(NG - 2, 0, True, True, True, True)
                turn(NG - 1, 1, False, True, True, True)
                turn(NG, 0, False, False, True, True)
                turn(NG + 1, 1, False, False, False, True)

                dve.wait_ge(r_step, RSTEPS * NG)
                dve.tensor_scalar(firsts[:], run[:, 0:E], float(CAP), None, ALU.min).then_inc(f_step, 1)
                dve.tensor_scalar(firsts_u[:], run[0:1, 0:E], float(CAP), None, ALU.min).then_inc(f_step, 1)
                dve.tensor_tensor(v3(sel1, E), v3(mask1, E), run[:, 0:E].unsqueeze(1).broadcast_to([P, B, E]), ALU.mult).then_inc(f_step, 1)
                dve.wait_ge(f_step, 3)
                dve.tensor_reduce(before1[:], v3(sel1, E), AX.X, ALU.add).then_inc(f_step, 1)
                dve.wait_ge(f_step, 4)
                ra = rank_all[:].rearrange("p (k q) -> p k q", q=TOPK)
                dve.tensor_tensor(ra[:, :, 1:2], ra[:, :, 1:2], before1[:].unsqueeze(2), ALU.add).then_inc(f_step, 1)
                dve.wait_ge(f_step, 5)
                dve.tensor_scalar(keep[:], rank_all[:], float(CAP), None, ALU.is_le).then_inc(f_step, 1)
                dve.wait_ge(f_step, 6)
                dve.tensor_tensor(gates_all[:], gates_all[:], keep[:], ALU.mult).then_inc(f_step, 1)


R_SHIFTED, R_MASKS, RSTEPS = 2, 19, 31


def phase_experts(nc, d, m):
    bank, ident, vecT = m["bank"], m["ident"], m["vecT"]
    w_hi, w_lo, raw, x1T = m["w_hi"], m["w_lo"], m["raw"], m["x1T"]
    slots, results, wts_in, sent_rows, dispatch = m["slots"], m["results"], m["wts_in"], m["sent_rows"], m["dispatch"]
    g_f, g_hi, g_lo = m["g_f"], m["g_hi"], m["g_lo"]
    firsts, firsts_u = m["firsts"], m["firsts_u"]
    NCK = [(0, 512), (512, 512), (1024, 256)]
    TILES = [(0, 4), (4, 4), (8, 2)]
    WB = [0, 2 * H]
    XB = [4 * H, 4 * H + CAP]
    UN = [(s, hb) for s in range(3) for hb in range(HB)]
    NU = len(UN)
    NY = len(NCK)

    with ExitStack() as ctx:
        def sb(name, shape, dt=F32):
            return ctx.enter_context(nc.sbuf_tensor(name, shape, dt))

        def sem(name):
            return ctx.enter_context(nc.semaphore(name))

        rows = [x1T[:, i * ST * ROWW:(i + 1) * ST * ROWW] for i in range(2)]
        iota8 = m["iota8"]
        touched = sb("touched3", [P, 6])
        touch = sem("touch3")
        dest = [sb(f"dest{i}", [P, ST], U32) for i in range(2)]
        yT = [sb(f"yT{i}", [P, 512]) for i in range(2)]
        yrow = [sb(f"yrow{i}", [P, ST * P]) for i in range(2)]
        b1c = [sb(f"b1c{i}", [P, HB + 1]) for i in range(2)]
        slot_no = sb("slot_no", [P, ST])
        second = sb("second", [P, ST])
        destf = sb("destf", [P, ST])

        joined = [sem(f"joined{e}") for e in range(E)]; slot_no_ready = sem("slot_no_ready"); dest_step = sem("dest_step")
        head_in = [sem("head_in0"), sem("head_in1")]; rows_in = [sem("rows_in0"), sem("rows_in1")]
        dest_ready = sem("dest_ready"); xe_acc = sem("xe_acc"); xe_ready = sem("xe_ready"); fc1_acc = sem("fc1_acc")
        fc1_ready = sem("fc1_ready"); fc2_ready = sem("fc2_ready"); bias_ready = sem("bias_ready")
        h1_done = sem("h1_done"); silu_done = sem("silu_done"); lo_done = sem("lo_done"); y_done = sem("y_done")
        yT_ready = sem("yT_ready"); yr_acc = sem("yr_acc"); yr_ready = sem("yr_ready"); sent = [sem("sent_even"), sem("sent_odd")]

        xbank = [bank[0], bank[1]]
        hbank = [bank[2], bank[3], bank[4]]
        ybank = [bank[5], bank[6]]
        rbank = bank[7]

        X_AT = {1: 0, 4: 1, 7: 2}
        FC1_AT = 9
        YT_AT = {6: (0, 0), 10: (0, 1), 2: (-1, 2)}
        BACK_AT = {7: (0, 0), 11: (0, 1), 3: (-1, 2)}
        YROW_AT = {8: (0, 0), 0: (-1, 1), 4: (-1, 2)}

        def turns(eng, turn):
            turn(0, 0, 0, True)
            turn(1, 1, 0, True)
            with eng.Fori(1, E // 2 - 1) as pair:
                turn(pair * 2, 0, pair, True)
                turn(pair * 2 + 1, 1, pair, True)
            turn(E - 2, 0, E // 2 - 1, True)
            turn(E - 1, 1, E // 2 - 1, False)

        def before_first(e):
            return isinstance(e, int) and e < 0

        with nc.Block() as block:
            @block.sync
            def _(sp):
                def join(e):
                    n1 = sp.value_load(firsts_u[0:1, e:e + 1], min_val=0, max_val=CAP)
                    sp.dma_start(slots[bass.ds(n1 + 2 * CAP * e, CAP), :], slots[SECOND + e * CAP:SECOND + (e + 1) * CAP, :]).then_inc(joined[e], 16)

                for par in range(2):
                    sp.wait_ge(sent_rows[par], 16 * TOPK * B // 2)
                join(0)
                for e in range(E):
                    q = e % 2
                    if e >= 2:
                        sp.wait_ge(fc1_acc, e - 1)
                        sp.wait_ge(fc2_ready, 2 * (e - 1))
                        load_expert_weights(sp, d, raw, wts_in, e)
                        sp.wait_ge(xe_acc, NY * (e - 1))
                        sp.wait_ge(dest_ready, e - 1)
                    sp.wait_ge(joined[e], 16)
                    t0 = 0
                    for t1, done in ((TILES[0][1], head_in[q]), (ST, rows_in[q])):
                        sp.dma_start(rows[q].rearrange("p (n c) -> p n c", c=ROWW)[:, t0:t1, :],
                                     slots[e * 2 * CAP + t0 * P:e * 2 * CAP + t1 * P, :].rearrange("(n p) c -> p n c", p=P)).then_inc(done, 16)
                        t0 = t1
                    if e + 1 < E:
                        join(e + 1)

            @block.gpsimd
            def _(gp):
                last_slot = gp.to_reg(SLOT_ROWS - 1)
                last_result = gp.to_reg(TOPK * N - 1)
                gp.iota(slot_no[:], pattern=[[P, ST]], base=0, channel_multiplier=1, allow_small_or_imprecise_dtypes=True).then_inc(slot_no_ready, 1)
                dispatch(gp, last_slot, NG - 1, 1, NG // 2)

                def send(e, q, s):
                    t0, nt = TILES[s]
                    atleast(gp, yr_ready, NY * e + s + 1)
                    atleast(gp, dest_ready, e + 1)
                    gp.tensor_tensor(touched[:, NY * q + s:NY * q + s + 1], iota8[:, 0:1], iota8[:, 0:1], ALU.add).then_inc(touch, 1)
                    for j in range(t0, t0 + nt):
                        gp.indirect_dma_start(out=results, out_offset=bass.IndirectOffsetOnAxis(ap=dest[q][:, j:j + 1], axis=0),
                                              in_=yrow[q][:, j * P:(j + 1) * P], in_offset=None,
                                              bounds_check=last_result, oob_is_err=False).then_inc(sent[q], 16)

                def turn(e, q, pair):
                    for s in range(NY):
                        send(e, q, s)

                loop_pairs(gp, turn)
                gp.wait_ge(sent[0], 16 * ST * E // 2)
                gp.wait_ge(sent[1], 16 * ST * E // 2)

            @block.tensor
            def _(pe):
                def columns(e, q, half, k):
                    t0, nt = TILES[k]
                    atleast(pe, rows_in[q] if k else head_in[q], 16 * half)
                    if k == 1:
                        atleast(pe, fc1_ready, 2 * e if not isinstance(e, int) or e else 2)
                    else:
                        atleast(pe, xe_ready, 6 * e + (2 if k else 0))
                    for j in range(nt):
                        t = pe.transpose(xbank[k % 2][:, j * P:(j + 1) * P], rows[q][:, (t0 + j) * ROWW:(t0 + j) * ROWW + P], ident[:])
                    t.then_inc(xe_acc, 1)

                def fc1(e, q, half):
                    atleast(pe, wts_in[q], 32 * half)
                    if not isinstance(e, int) or e:
                        atleast(pe, xe_ready, 6 * e + 4)
                    for j in range(HB):
                        t = pe.transpose(xbank[1][:, j * P:(j + 1) * P], raw[q][:, j * P:(j + 1) * P], ident[:])
                    t.then_inc(fc1_acc, 1)

                def first(e, q, u):
                    s, hb = UN[u]
                    c0, w = NCK[s]
                    if hb == 0:
                        atleast(pe, xe_ready, 6 * e + 2 * (s + 1))
                    if u == 0:
                        atleast(pe, fc1_ready, 2 * (e + 1))
                    atleast(pe, silu_done, 2 * (NU * e + u - 2))
                    a = slice(WB[q] + hb * P, WB[q] + (hb + 1) * P)
                    b_ = slice(XB[q] + c0, XB[q] + c0 + w)
                    mm3(pe, hbank[u % 3][:, 0:w], w_hi[:, a], w_lo[:, a], w_hi[:, b_], w_lo[:, b_], True, True).then_inc(h1_done, 1)

                def second_(e, q, u):
                    s, hb = UN[u]
                    w = NCK[s][1]
                    if u == 0:
                        atleast(pe, fc2_ready, 2 * (e + 1))
                    if hb == 0:
                        atleast(pe, yT_ready, NY * e + s - 1)
                    atleast(pe, lo_done, NU * e + u + 1)
                    a = slice(WB[q] + H + hb * P, WB[q] + H + (hb + 1) * P)
                    mm3(pe, ybank[(q + s) % 2][:, 0:w], w_hi[:, a], w_lo[:, a], g_hi[u % 4][:, 0:w], g_lo[u % 4][:, 0:w], hb == 0, hb == HB - 1).then_inc(y_done, 1)

                def back(e, q, s):
                    nt = TILES[s][1]
                    atleast(pe, yT_ready, NY * e + s + 1)
                    atleast(pe, yr_ready, NY * e + s)
                    for j in range(nt):
                        t = pe.transpose(rbank[:, j * P:(j + 1) * P], yT[(q + s) % 2][:, j * P:(j + 1) * P], ident[:])
                    t.then_inc(yr_acc, 1)

                def turn(e, q, pair, more):
                    for u in range(NU):
                        first(e, q, u)
                        if u >= 2:
                            second_(e, q, u - 2)
                        elif not before_first(e - 1):
                            second_(e - 1, 1 - q, NU + u - 2)
                        if u in BACK_AT:
                            o, s = BACK_AT[u]
                            if not before_first(e + o):
                                back(e + o, (q + o) % 2, s)
                        if more and u in X_AT:
                            columns(e + 1, 1 - q, pair + q + 1, X_AT[u])
                        if more and u == FC1_AT:
                            fc1(e + 1, 1 - q, pair + q + 1)

                fc1(0, 0, 1)
                for k in range(NY):
                    columns(0, 0, 1, k)
                turns(pe, turn)
                second_(E - 1, 1, NU - 2)
                second_(E - 1, 1, NU - 1)
                back(E - 1, 1, 2)

            @block.scalar
            def _(act):
                def fc1(e, q):
                    atleast(act, fc1_acc, e + 1)
                    atleast(act, h1_done, NU * (e - 1))
                    act.activation(w_hi[:, WB[q]:WB[q] + H], xbank[1][:], ACT.Copy).then_inc(fc1_ready, 1)

                def results_out(e, q, s):
                    w = NCK[s][1]
                    atleast(act, y_done, NU * e + HB * (s + 1))
                    atleast(act, yr_acc, NY * e + s - 1)
                    act.activation(yT[(q + s) % 2][:, 0:w], ybank[(q + s) % 2][:, 0:w], ACT.Identity, bias=b1c[q][:, HB:HB + 1]).then_inc(yT_ready, 1)

                def turn(e, q, pair, more):
                    for u in range(NU):
                        s, hb = UN[u]
                        w = NCK[s][1]
                        atleast(act, h1_done, NU * e + u + 1)
                        if u == 0:
                            atleast(act, bias_ready, e + 1)
                        atleast(act, lo_done, NU * e + u - 1)
                        atleast(act, y_done, NU * e + u - 3)
                        b_ = b1c[q][:, hb:hb + 1]
                        act.activation(g_f[u % 2][:, 0:w], hbank[u % 3][:, 0:w], ACT.Silu, bias=b_).then_inc(silu_done, 1)
                        act.activation(g_hi[u % 4][:, 0:w], hbank[u % 3][:, 0:w], ACT.Silu, bias=b_).then_inc(silu_done, 1)
                        if u in YT_AT:
                            o, s = YT_AT[u]
                            if not before_first(e + o):
                                results_out(e + o, (q + o) % 2, s)
                        if more and u == FC1_AT + 1:
                            fc1(e + 1, 1 - q)

                fc1(0, 0)
                turns(act, turn)
                results_out(E - 1, 1, 2)

            @block.vector
            def _(dve):
                def biases(e, q):
                    atleast(dve, yT_ready, NY * (e - 1))
                    atleast(dve, silu_done, 2 * NU * (e - 1))
                    dve.tensor_scalar(b1c[q][:, 0:HB], vecT[:, bass.ds(R_FB1 + HB * e, HB)], 1.0, None, ALU.mult)
                    dve.tensor_scalar(b1c[q][:, HB:HB + 1], vecT[:, bass.ds(R_FB2 + e, 1)], 1.0, None, ALU.mult).then_inc(bias_ready, 1)

                def destinations(e, q, half):
                    atleast(dve, sent[q], 16 * ST * (half - 1))
                    atleast(dve, touch, NY * (e - 1))
                    atleast(dve, rows_in[q], 16 * half)
                    atleast(dve, head_in[q], 16 * half)
                    dve.tensor_scalar(destf[:].unsqueeze(2), rows[q].rearrange("p (n c) -> p n c", c=ROWW)[:, :, P:ROWW], 1.0, None, ALU.mult).then_inc(dest_step, 1)
                    dve.tensor_scalar(second[:], slot_no[:], firsts[:, bass.ds(e, 1)], float(N), ALU.is_ge, ALU.mult).then_inc(dest_step, 1)
                    dve.wait_ge(dest_step, e * 2 + 2)
                    dve.tensor_tensor(dest[q][:], destf[:], second[:], ALU.add).then_inc(dest_ready, 1)

                def columns(e, q, k):
                    t0, nt = TILES[k]
                    atleast(dve, xe_acc, NY * e + k + 1)
                    atleast(dve, h1_done, NU * (e - 1))
                    o = slice(XB[q] + t0 * P, XB[q] + (t0 + nt) * P)
                    dve.tensor_copy(w_hi[:, o], xbank[k % 2][:, 0:nt * P]).then_inc(xe_ready, 1)
                    atleast(dve, xe_ready, 6 * e + 2 * k + 1)
                    dve.tensor_tensor(w_lo[:, o], xbank[k % 2][:, 0:nt * P], w_hi[:, o], ALU.subtract).then_inc(xe_ready, 1)

                def fc1(e, q):
                    atleast(dve, fc1_ready, 2 * e + 1)
                    dve.tensor_tensor(w_lo[:, WB[q]:WB[q] + H], xbank[1][:], w_hi[:, WB[q]:WB[q] + H], ALU.subtract).then_inc(fc1_ready, 1)

                def fc2(e, q, half):
                    atleast(dve, wts_in[q], 32 * half)
                    atleast(dve, y_done, NU * (e - 1))
                    dve.tensor_copy(w_hi[:, WB[q] + H:WB[q] + 2 * H], raw[q][:, H:2 * H]).then_inc(fc2_ready, 1)
                    atleast(dve, fc2_ready, 2 * e + 1)
                    dve.tensor_tensor(w_lo[:, WB[q] + H:WB[q] + 2 * H], raw[q][:, H:2 * H], w_hi[:, WB[q] + H:WB[q] + 2 * H], ALU.subtract).then_inc(fc2_ready, 1)

                def rows_out(e, q, s):
                    t0, nt = TILES[s]
                    atleast(dve, yr_acc, NY * e + s + 1)
                    atleast(dve, dest_ready, e + 1)
                    dve.tensor_copy(yrow[q][:, t0 * P:(t0 + nt) * P], rbank[:, 0:nt * P]).then_inc(yr_ready, 1)

                def turn(e, q, pair, more):
                    for u in range(NU):
                        w = NCK[UN[u][0]][1]
                        atleast(dve, silu_done, 2 * (NU * e + u + 1))
                        atleast(dve, y_done, NU * e + u - 3)
                        dve.tensor_tensor(g_lo[u % 4][:, 0:w], g_f[u % 2][:, 0:w], g_hi[u % 4][:, 0:w], ALU.subtract).then_inc(lo_done, 1)
                        if u in YROW_AT:
                            o, s = YROW_AT[u]
                            if not before_first(e + o):
                                rows_out(e + o, (q + o) % 2, s)
                        if more:
                            half = pair + q + 1
                            if u in X_AT:
                                columns(e + 1, 1 - q, X_AT[u])
                            if u == 3:
                                fc2(e + 1, 1 - q, half)
                            if u == FC1_AT - 1:
                                biases(e + 1, 1 - q)
                                destinations(e + 1, 1 - q, half)
                            if u == FC1_AT + 1:
                                fc1(e + 1, 1 - q)

                biases(0, 0)
                fc1(0, 0)
                fc2(0, 0, 1)
                dve.wait_ge(slot_no_ready, 1)
                for k in range(NY):
                    columns(0, 0, k)
                destinations(0, 0, 1)
                turns(dve, turn)
                rows_out(E - 1, 1, 1)
                rows_out(E - 1, 1, 2)


def loop_pairs(eng, turn):
    turn(0, 0, 0)
    turn(1, 1, 0)
    with eng.Fori(1, E // 2) as pair:
        turn(pair * 2, 0, pair)
        turn(pair * 2 + 1, 1, pair)


def phase_norm(nc, d, m, out):
    xT, wide, results, gates_all = m["xT"], m["wide"], m["results"], m["gates_all"]
    x1rows = xT
    hid3 = wide[:].rearrange("p (b c) -> p b c", c=ROWW)
    with ExitStack() as ctx:
        def sb(name, shape, dt=F32):
            return ctx.enter_context(nc.sbuf_tensor(name, shape, dt))

        def sem(name):
            return ctx.enter_context(nc.semaphore(name))

        gb = sb("gamma", [P, P]); bb = sb("beta", [P, P]); epsc = sb("epsc", [P, 1])
        yb = [[sb(f"y{q}{i}", [P, GRP * P]) for i in range(2)] for q in range(TOPK)]
        res = [sb(f"res{i}", [P, GRP * P]) for i in range(2)]
        nrm = [sb(f"nrm{i}", [P, GRP * P]) for i in range(2)]
        fin = [sb(f"fin{i}", [P, GRP * P]) for i in range(2)]
        st = sb("stats", [P, GRP * 6]); mv = sb("mv", [P, GRP * 2]); sd = sb("sd", [P, GRP]); rstd = sb("rstd", [P, GRP])
        n_in = sem("n_in"); y_in = [sem("y_in0"), sem("y_in1")]; eps_ready = sem("eps_ready"); c_step = sem("c_step")
        mv_ready = sem("mv_ready"); sd_ready = sem("sd_ready"); nrm_step = sem("nrm_step"); scaled = sem("scaled"); fin_ready = sem("fin_ready"); stored = [sem("stored_even"), sem("stored_odd")]
        CS = GRP * 3 + 1
        y_src = results.rearrange("(q g b p) c -> q g p b c", q=TOPK, b=GRP, p=P)

        def v3(a):
            return a[:].rearrange("p (b c) -> p b c", c=P)

        with nc.Block() as block:
            @block.sync
            def _(sp):
                sp.dma_start(gb[:], d["L1_ffn_ln_gamma"].rearrange("(a p) -> a p", a=1).broadcast_to([P, P])).then_inc(n_in, 16)
                sp.dma_start(bb[:], d["L1_ffn_ln_beta"].rearrange("(a p) -> a p", a=1).broadcast_to([P, P])).then_inc(n_in, 16)
                for g in range(NG):
                    if g >= 2:
                        sp.wait_ge(c_step, CS * (g - 1))
                    for q in range(TOPK):
                        sp.dma_start(v3(yb[q][g % 2]), y_src[q, g]).then_inc(y_in[g % 2], 16)

            @block.scalar
            def _(act):
                for g in range(NG):
                    act.wait_ge(mv_ready, GRP * (g + 1))
                    act.wait_ge(eps_ready, 1)
                    act.activation(sd[:], mv[:].rearrange("p (b c) -> p b c", c=2)[:, :, 1], ACT.Sqrt, bias=epsc[:]).then_inc(sd_ready, 1)
                    if g >= 1:
                        act.wait_ge(fin_ready, g)
                        act.dma_start(out[GRP * (g - 1):GRP * g].rearrange("b t c -> t b c"), v3(fin[(g - 1) % 2])).then_inc(stored[(g - 1) % 2], 16)
                act.wait_ge(fin_ready, NG)
                act.dma_start(out[GRP * (NG - 1):GRP * NG].rearrange("b t c -> t b c"), v3(fin[(NG - 1) % 2])).then_inc(stored[(NG - 1) % 2], 16)
                act.wait_ge(stored[0], 16 * NG // 2)
                act.wait_ge(stored[1], 16 * NG // 2)

            @block.gpsimd
            def _(gp):
                gp.wait_ge(n_in, 32)
                for g in range(NG):
                    f, w = v3(fin[g % 2]), v3(nrm[g % 2])
                    gp.wait_ge(nrm_step, GRP * (g + 1))
                    if g >= 2:
                        gp.wait_ge(stored[g % 2], 16 * (g // 2))
                    gp.tensor_tensor(f, w, gb[:].unsqueeze(1).broadcast_to([P, GRP, P]), ALU.mult).then_inc(scaled, 1)
                    gp.wait_ge(scaled, 2 * g + 1)
                    gp.tensor_tensor(f, f, bb[:].unsqueeze(1).broadcast_to([P, GRP, P]), ALU.add).then_inc(scaled, 1)

            @block.vector
            def _(dve):
                dve.memset(epsc[:], EPS_LN).then_inc(eps_ready, 1)

                def finish(g):
                    dve.wait_ge(scaled, 2 * (g + 1))
                    dve.tensor_tensor(fin[g % 2][:], fin[g % 2][:], x1rows[:, g * GRP * P:(g + 1) * GRP * P], ALU.add).then_inc(fin_ready, 1)

                for g in range(NG):
                    dve.wait_ge(y_in[g % 2], 32 * (g // 2 + 1))
                    n = CS * g
                    k = 0
                    r = res[g % 2]
                    if g >= 2:
                        dve.wait_ge(nrm_step, GRP * (g - 1))
                    for q in range(TOPK):
                        for j in range(GRP):
                            b = g * GRP + j
                            js = slice(j * P, (j + 1) * P)
                            if q:
                                dve.wait_ge(c_step, n + j + 1)
                            dve.scalar_tensor_tensor(out=r[:, js], in0=yb[q][g % 2][:, js], scalar=gates_all[:, TOPK * b + q:TOPK * b + q + 1],
                                                     in1=(r[:, js] if q else hid3[:, b, 0:P]), op0=ALU.mult, op1=ALU.add).then_inc(c_step, 1)
                    for j in range(GRP):
                        dve.wait_ge(c_step, n + GRP + j + 1)
                        dve.bn_stats(st[:, 6 * j:6 * j + 6], r[:, j * P:(j + 1) * P]).then_inc(c_step, 1)
                    if g >= 1:
                        dve.wait_ge(sd_ready, g)
                    for j in range(GRP):
                        dve.wait_ge(c_step, n + 2 * GRP + j + 1)
                        dve.bn_aggr(mv[:, 2 * j:2 * j + 2], st[:, 6 * j:6 * j + 6]).then_inc(mv_ready, 1)
                    if g >= 1:
                        finish(g - 1)
                    dve.wait_ge(sd_ready, g + 1)
                    dve.reciprocal(rstd[:], sd[:]).then_inc(c_step, 1)
                    dve.wait_ge(c_step, n + 3 * GRP + 1)
                    dve.wait_ge(mv_ready, GRP * (g + 1))
                    if g >= 2:
                        dve.wait_ge(scaled, 2 * g - 3)
                    for j in range(GRP):
                        js = slice(j * P, (j + 1) * P)
                        dve.tensor_scalar(nrm[g % 2][:, js], r[:, js], mv[:, 2 * j:2 * j + 1], rstd[:, j:j + 1], ALU.subtract, ALU.mult).then_inc(nrm_step, 1)
                finish(NG - 1)


NAMES = ['x', 'cond_1024', 'L0_cond_W_z', 'L0_cond_U_z', 'L0_cond_C_z', 'L0_cond_b_z', 'L0_cond_W_r', 'L0_cond_U_r',
         'L0_cond_C_r', 'L0_cond_b_r', 'L0_cond_W', 'L0_cond_U', 'L0_cond_C', 'L0_cond_b', 'L0_ffn_rW', 'L0_ffn_rb',
         'L0_ffn_W1', 'L0_ffn_b1', 'L0_ffn_W2', 'L0_ffn_b2', 'L0_ffn_sW1', 'L0_ffn_sb1', 'L0_ffn_sW2', 'L0_ffn_sb2',
         'L1_cond_Wq1', 'L1_cond_bq1', 'L1_cond_Wq2', 'L1_cond_bq2', 'L1_cond_Wk1', 'L1_cond_bk1', 'L1_cond_Wk2',
         'L1_cond_bk2', 'L1_cond_Wv', 'L1_cond_bv', 'L1_cond_alpha', 'L1_ffn_wg', 'L1_ffn_fc1_w', 'L1_ffn_fc1_b',
         'L1_ffn_fc2_w', 'L1_ffn_fc2_b', 'L1_ffn_ln_gamma', 'L1_ffn_ln_beta']


def kernel(**inputs):
    from concourse import bacc
    from concourse.bass_utils import run_bass_kernel_spmd

    nc = bacc.Bacc("TRN2", target_bir_lowering=False, num_devices=1)
    arrays, d = {}, {}
    for name in NAMES:
        a = np.ascontiguousarray(inputs[name])
        arrays[f"in_{name}"] = a
        d[name] = nc.dram_tensor(f"in_{name}", a.shape, F32, kind="ExternalInput").ap()
    out = nc.dram_tensor("out", (B, T, P), F32, kind="ExternalOutput").ap()
    build(nc, d, out)
    return run_bass_kernel_spmd(nc, [arrays], core_ids=[0]).results[0]["out"]
```

```python
from contextlib import ExitStack

import numpy as np
import concourse.bass as bass
from concourse import mybir

F32 = mybir.dt.float32
F32R = mybir.dt.float32r
U32 = mybir.dt.uint32
ALU = mybir.AluOpType
ACT = mybir.ActivationFunctionType
AX = mybir.AxisListType

P = 128
B, T = 32, 128
N = B * T
H = 512
HB = H // P
E = 8
NSH = 2
NE0 = E + NSH
TOPK = 2
STEPS = 8
CH = STEPS * B
NCH = N // CH
UNITS = NE0 * HB
CT = CH // P
LAG = 5
BEHIND = 6
GRP = 4
NG = B // GRP
CAP = TOPK * int(1.25 * ((N + E - 1) // E))
ST = CAP // P
ROWW = P + 1
SECOND = E * 2 * CAP
SLOT_ROWS = SECOND + E * CAP
FAR = 60000.0
SCALE = 1.0 / float(np.sqrt(np.float32(P)))
EPS_GATE = 1.1920929e-07
EPS_LN = 1e-05

R_SB1, R_B1, R_SB2, R_B2, R_BQ2, R_BK2, R_FB1, R_FB2, NVEC = 0, 8, 40, 42, 50, 51, 52, 84, 92


def atleast(eng, sem, value):
    if isinstance(value, int) and value <= 0:
        return
    eng.wait_ge(sem, value)


def part_slot(p):
    return (p // 2) * (UNITS // STEPS) + (p % 2) * 2


PART_OF_SLOT = {part_slot(p): p for p in range(2 * STEPS)}
NGRP = 1 + E


def unit_at(i, par, s, behind):
    v = s - LAG - behind
    c, cpar, u = (i - 1, 1 - par, v) if v >= 0 else (i - 2, par, v + UNITS)
    if isinstance(c, int) and not 0 <= c < NCH:
        return None
    return c, cpar, u


def bodies(eng, body):
    body(0, 0, UNITS)
    body(1, 1, UNITS)
    with eng.Fori(0, (NCH - 4) // 2) as k:
        body(k * 2 + 2, 0, UNITS)
        body(k * 2 + 3, 1, UNITS)
    body(NCH - 2, 0, UNITS)
    body(NCH - 1, 1, UNITS)
    body(NCH, 0, UNITS)
    body(NCH + 1, 1, LAG + BEHIND + 3)


def within(i, last):
    return not isinstance(i, int) or 0 <= i <= last


def group_of(u):
    if u < NSH * HB:
        return 0, u == 0, u == NSH * HB - 1
    k = u // HB - 1
    return k, u % HB == 0, u % HB == HB - 1


def build(nc, d, out):
    with ExitStack() as ctx:
        def sb(name, shape, dt=F32):
            return ctx.enter_context(nc.sbuf_tensor(name, shape, dt))

        def sem(name):
            return ctx.enter_context(nc.semaphore(name))

        bank = [ctx.enter_context(nc.psum_tensor(f"bank{i}", [P, 512], F32)) for i in range(8)]

        w_dram = nc.dram_tensor("w_dram", (E, CH), F32, kind="Internal").ap()
        slots = nc.dram_tensor("slot_rows", (SLOT_ROWS, ROWW), F32, kind="Internal").ap()
        results = nc.dram_tensor("result_rows", (TOPK * N, P), F32, kind="Internal").ap()

        ident = sb("ident", [P, P])
        identr = sb("identr", [P, P], F32R)
        vecs = sb("vecs", [P, P])
        vecT = sb("vecT", [P, NVEC])
        iota8 = sb("iota8", [P, E])
        condT = sb("condT", [P, B])
        xT = sb("xT", [P, N])
        x1T = sb("x1T", [P, N])
        wide = sb("wide", [P, B * ROWW])
        w_hi = sb("w_hi", [P, NE0 * 2 * H], F32R)
        w_lo = sb("w_lo", [P, NE0 * 2 * H], F32R)
        raw = [sb(f"raw{i}", [P, 2 * H]) for i in range(2)]
        alphaT = sb("alphaT", [P, B])
        firsts = sb("firsts", [P, E])
        firsts_u = sb("firsts_u", [1, E], U32)
        gates_all = sb("gates_all", [P, B * TOPK])
        zt = sb("zt", [P, ST * ROWW])
        g_f = [sb(f"g_f{i}", [P, 512]) for i in range(2)]
        g_hi = [sb(f"g_hi{i}", [P, 512], F32R) for i in range(4)]
        g_lo = [sb(f"g_lo{i}", [P, 512], F32R) for i in range(4)]

        alph = sb("alph", [B, 1]); s1 = sb("s1", [B, 4]); a1 = sb("a1", [B, P]); e1 = sb("e1", [B, P])
        a1_pe = sem("a1_pe"); a1_dve = sem("a1_dve"); a1_act = sem("a1_act")
        wv1 = sb("wv1", [P, P]); bvc = sb("bvc", [P, 1]); wg = sb("wg", [P, E]); att_in = sem("att_in")
        hs = [sb(f"hs{i}", [P, GRP * ROWW]) for i in range(2)]
        posi = [sb(f"posi{i}", [P, GRP * TOPK], U32) for i in range(2)]
        hs_ready = sem("hs_ready"); hs_free = sem("hs_free"); pos_ready = sem("pos_ready"); hid_kept = sem("hid_kept")
        sent_rows = [sem("sent_rows_even"), sem("sent_rows_odd")]; touch = sem("touch")
        touched = sb("touched", [P, 3])
        wts_in = [sem("wts_in0"), sem("wts_in1")]

        def dispatch(gp, last_slot, g, par, before):
            gp.wait_ge(hs_ready, (g + 1) * 16)
            gp.wait_ge(pos_ready, g + 1)
            gp.tensor_tensor(touched[:, par:par + 1], iota8[:, 0:1], iota8[:, 0:1], ALU.add).then_inc(touch, 1)
            for j in range(GRP):
                if j == GRP // 2 and not (isinstance(g, int) and g == NG - 1):
                    atleast(gp, sent_rows[1 - par], 16 * GRP * TOPK * before)
                    gp.wait_ge(hid_kept, (g + 2) * 16)
                    gp.tensor_tensor(touched[:, 2:3], iota8[:, 0:1], iota8[:, 0:1], ALU.add).then_inc(hs_free, 1)
                for q in range(TOPK):
                    k = j * TOPK + q
                    gp.indirect_dma_start(out=slots, out_offset=bass.IndirectOffsetOnAxis(ap=posi[par][:, k:k + 1], axis=0),
                                          in_=hs[par][:, j * ROWW:(j + 1) * ROWW], in_offset=None,
                                          bounds_check=last_slot, oob_is_err=False).then_inc(sent_rows[par], 16)

        phase_scan(nc, d, locals())
        phase_attention(nc, d, locals())
        phase_experts(nc, d, locals())
        phase_norm(nc, d, locals(), out)


def load_expert_weights(sp, d, raw, wts_in, e):
    q = e % 2
    sp.dma_start(raw[q][:, 0:H].rearrange("p (m n) -> p m n", m=HB), d["L1_ffn_fc1_w"][e].rearrange("(m p) n -> p m n", p=P)).then_inc(wts_in[q], 16)
    sp.dma_start(raw[q][:, H:2 * H].rearrange("p (m n) -> p m n", m=HB), d["L1_ffn_fc2_w"][e].rearrange("(m p) n -> p m n", p=P)).then_inc(wts_in[q], 16)


def mm3(pe, out, a_hi, a_lo, b_hi, b_lo, start, stop):
    pe.matmul(out, a_hi, b_hi, start=start, stop=False, skip_group_check=True)
    pe.matmul(out, a_hi, b_lo, start=False, stop=False, skip_group_check=True)
    return pe.matmul(out, a_lo, b_hi, start=False, stop=stop, skip_group_check=True)


def phase_scan(nc, d, m):
    bank, ident, identr, vecs, vecT = m["bank"], m["ident"], m["identr"], m["vecs"], m["vecT"]
    condT, xT, x1T, wide, w_hi, w_lo, raw = (m[k] for k in ("condT", "xT", "x1T", "wide", "w_hi", "w_lo", "raw"))
    iota8, zt, g_f, g_hi, g_lo, alphaT = (m[k] for k in ("iota8", "zt", "g_f", "g_hi", "g_lo", "alphaT"))
    w_dram, slots, results = m["w_dram"], m["slots"], m["results"]
    alph, s1, a1, e1, a1_pe, a1_dve = (m[k] for k in ("alph", "s1", "a1", "e1", "a1_pe", "a1_dve"))
    wb = wide[:, 0:E * CH]
    BF16 = mybir.dt.bfloat16

    with ExitStack() as ctx:
        def sb(name, shape, dt=F32):
            return ctx.enter_context(nc.sbuf_tensor(name, shape, dt))

        def sem(name):
            return ctx.enter_context(nc.semaphore(name))

        xrows = sb("xrows", [P, CH])
        condr = sb("condr", [B + 3, P])
        bcol = sb("bcol", [P, 3])
        wx = sb("wx", [P, 3 * P])
        wx_hi = sb("wx_hi", [P, 3 * P], F32R)
        wx_lo = sb("wx_lo", [P, 3 * P], F32R)
        uh = sb("uh", [P, 3 * P])
        ub = [sb(f"ub{i}", [P, 2 * P], BF16) for i in range(3)]
        urest = sb("urest", [P, 2 * P])
        hb_ = [sb(f"hb{i}", [P, B], BF16) for i in range(3)]
        hrest = sb("hrest", [P, B])
        cv = sb("cv", [P, 3 * P])
        vb = sb("vb", [P, 3 * B])
        vb_hi = sb("vb_hi", [P, 3 * B], F32R)
        vb_lo = sb("vb_lo", [P, 3 * B], F32R)
        x_hi = sb("x_hi", [P, CH], F32R)
        x_lo = sb("x_lo", [P, CH], F32R)
        h = [sb(f"h{i}", [P, CH]) for i in range(2)]
        h_hi = [sb(f"h_hi{i}", [P, CH], F32R) for i in range(2)]
        h_lo = [sb(f"h_lo{i}", [P, CH], F32R) for i in range(2)]
        tzr = sb("tzr", [P, 2 * B])
        rh = sb("rh", [P, B])
        z = sb("z", [P, B])
        kept = sb("kept", [P, B])
        hh = sb("hh", [P, B])
        zhh = sb("zhh", [P, B])
        acc = sb("acc", [P, CH])
        tmp = [sb(f"tmp{i}", [P, CH]) for i in range(2)]
        sbias = sb("sbias", [P, 1])
        rw = sb("rw", [P, E])
        rbb = sb("rbb", [P, E])
        lg = sb("lg", [P, CT * E])
        mx = sb("mx", [P, CT * 8])
        ix = sb("ix", [P, CT * 8], U32)
        ixf = sb("ixf", [P, CT * 2])
        lgmax = sb("lgmax", [P, 1])
        dlt = sb("dlt", [P, CT])
        th = sb("th", [P, CT])
        p0 = sb("p0", [P, CT])
        p1 = sb("p1", [P, CT])
        oh0 = sb("oh0", [P, CT * E])
        oh1 = sb("oh1", [P, CT * E])
        wt = sb("wt", [P, CT * E])
        wT = sb("wT", [E, CH])
        wq1 = sb("wq1", [P, P])
        wk1 = sb("wk1", [P, P])
        bq1 = sb("bq1", [B, P])
        bk1 = sb("bk1", [B, P])
        q1 = sb("q1", [B, P])
        k1 = sb("k1", [B, P])

        scan_in = sem("scan_in"); small_in = sem("small_in"); x_in = sem("x_in"); w_in = [sem(f"w_in{e}") for e in range(NE0)]
        a1_in = sem("a1_in")
        zeroed = sem("zeroed")
        ident_ready = sem("ident_ready"); setup_pe = sem("setup_pe"); setup_dve = sem("setup_dve")
        vec_pe = sem("vec_pe"); vec_step = sem("vec_step")
        w_hi_pool = sem("w_hi_pool"); w_lo_pool = sem("w_lo_pool"); w_hi_act = sem("w_hi_act"); w_lo_dve = sem("w_lo_dve")
        zt_ready = sem("zt_ready");
        xt_acc = sem("xt_acc"); x_kept = sem("x_kept"); x_split = sem("x_split"); prefilled = sem("prefilled")
        zr_acc = sem("zr_acc"); zr_tanh = sem("zr_tanh"); rh_ready = sem("rh_ready"); z_ready = sem("z_ready")
        kept_ready = sem("kept_ready"); hh_acc = sem("hh_acc"); hh_tanh = sem("hh_tanh"); zhh_ready = sem("zhh_ready")
        h_ready = sem("h_ready"); hparts = sem("hparts"); hrest_ready = sem("hrest_ready")
        h_split = sem("h_split"); w1_done = sem("w1_done"); gelu_done = sem("gelu_done")
        lo_dve = sem("lo_dve"); hi_dve = sem("hi_dve"); lo_pool = sem("lo_pool")
        w2_done = sem("w2_done"); y_read = sem("y_read"); acc_added = sem("acc_added"); x1_ready = sem("x1_ready")
        gate_acc = sem("gate_acc"); gate_step = sem("gate_step"); gate_tanh = sem("gate_tanh"); wT_acc = sem("wT_acc")
        wT_ready = sem("wT_ready"); w_out = sem("w_out"); wb_ready = sem("wb_ready")

        zr_bank, hh_bank = bank[0], bank[1]
        gate_bank = bank[7]
        xt_cols = gate_bank[:, CH:2 * CH]
        x1T_tb = x1T[:].rearrange("p (b t) -> p t b", b=B)
        GSTEPS = 10 + 2 * CT

        def half(a, k):
            return a[:, k * CH:(k + 1) * CH]

        def w1_out(cpar, u):
            return half(bank[2 + (u + cpar) % 3], 0)

        def y_out(cpar, k):
            return half(bank[5 + (cpar + k) % 2], 0)

        LO_POOL, HI_DVE = (1, 3), (0,)

        def gf(u):
            return half(g_f[u % 2], u // 2 % 2)

        def ghi(u):
            return half(g_hi[u % 4], u // 4 % 2)

        def glo(u):
            return half(g_lo[u % 4], u // 4 % 2)

        def on_pool(u):
            return u % 4 in LO_POOL

        def on_dve(u):
            return not on_pool(u)

        def hi_on_dve(u):
            return u % 8 in HI_DVE

        def units_up_to(mine, c, u):
            return sum(map(mine, range(UNITS))) * c + sum(map(mine, range(u + 1)))

        def lo_wait(eng, c, u, back=0):
            mine, done = (on_pool, lo_pool) if on_pool(u) else (on_dve, lo_dve)
            atleast(eng, done, units_up_to(mine, c, u) - sum(map(mine, range(back))))

        def loaded(e):
            if e < 4:
                return wide[:, e * 2 * H:(e + 1) * 2 * H]
            return x1T[:, (e - 4) * 2 * H:(e - 3) * 2 * H] if e < 8 else raw[e - 8][:]

        SPLIT_AT = {1: (0, 0), 2: (0, 1), 4: (2, 0), 5: (2, 1), 7: (4, 0), 8: (4, 1), 10: (6, 0), 11: (6, 1), 14: (8, 0), 15: (8, 1)}

        def w1(part, e, hb):
            return part[:, e * 2 * H + hb * P:e * 2 * H + (hb + 1) * P]

        def w2(part, e, hb):
            return part[:, e * 2 * H + H + hb * P:e * 2 * H + H + (hb + 1) * P]

        with nc.Block() as block:
            @block.sync
            def _(sp):
                def load_x(n):
                    for k in range(CT):
                        sp.dma_start(xrows[:, k * P:(k + 1) * P],
                                     d["x"][:, bass.ds(n * STEPS + k * STEPS // CT, STEPS // CT), :].rearrange("b t c -> t b c")).then_inc(x_in, 16)

                load_x(0)
                for dst, src in (
                    (condr[0:B, :], d["cond_1024"]),
                    (condr[B:B + 1, :], d["L0_cond_b_z"].rearrange("(a p) -> a p", a=1)),
                    (condr[B + 1:B + 2, :], d["L0_cond_b_r"].rearrange("(a p) -> a p", a=1)),
                    (condr[B + 2:B + 3, :], d["L0_cond_b"].rearrange("(a p) -> a p", a=1)),
                    (wx[:, 0:P], d["L0_cond_W_z"]), (wx[:, P:2 * P], d["L0_cond_W_r"]), (wx[:, 2 * P:3 * P], d["L0_cond_W"]),
                ):
                    sp.dma_start(dst, src).then_inc(scan_in, 16)
                for dst, src in (
                    (vecs[R_SB1:R_SB1 + 8, :], d["L0_ffn_sb1"].rearrange("s (m p) -> (s m) p", p=P)),
                    (vecs[R_B1:R_B1 + 32, :], d["L0_ffn_b1"].rearrange("s (m p) -> (s m) p", p=P)),
                    (vecs[R_SB2:R_SB2 + 2, :], d["L0_ffn_sb2"]),
                    (vecs[R_B2:R_B2 + 8, :], d["L0_ffn_b2"]),
                    (vecs[R_BQ2:R_BQ2 + 1, :], d["L1_cond_bq2"].rearrange("(a p) -> a p", a=1)),
                ):
                    sp.dma_start(dst, src).then_inc(small_in, 16)
                for e in range(NE0):
                    a, b_ = (d["L0_ffn_sW1"][e], d["L0_ffn_sW2"][e]) if e < NSH else (d["L0_ffn_W1"][e - NSH], d["L0_ffn_W2"][e - NSH])
                    sp.dma_start(loaded(e)[:, 0:H], a).then_inc(w_in[e], 16)
                    sp.dma_start(loaded(e)[:, H:2 * H].rearrange("p (m n) -> p m n", m=HB), b_.rearrange("(m p) n -> p m n", p=P)).then_inc(w_in[e], 16)
                    if e == 1:
                        sp.wait_ge(xt_acc, 1)
                        load_x(1)

                def body(i, par, nslots):
                    if within(i, NCH - 3) and not (isinstance(i, int) and i < 0):
                        sp.wait_ge(xt_acc, i + 2)
                        load_x(i + 2)
                    if nslots == UNITS and within(i - 1, NCH - 1):
                        sp.wait_ge(wT_ready, i)
                        sp.dma_start(w_dram, wT[:]).then_inc(w_out, 16)
                        sp.wait_ge(w_out, i * 16)
                        if isinstance(i, int) and i == 1:
                            sp.wait_ge(w_lo_dve, 4)
                            sp.wait_ge(w_lo_pool, 2)
                        sp.dma_start(wb, w_dram.rearrange("e n -> (e n)").rearrange("(a n) -> a n", a=1).broadcast_to([P, E * CH])).then_inc(wb_ready, 16)
                    if isinstance(i, int) and i == 1:
                        sp.wait_ge(zt_ready, 2)
                        for e in range(E):
                            sp.dma_start(slots[SECOND + e * CAP:SECOND + (e + 1) * CAP, :].rearrange("(p n) c -> p (n c)", p=P), zt[:]).then_inc(zeroed, 16)
                        rows = TOPK * N // E
                        for e in range(E):
                            sp.dma_start(results[e * rows:(e + 1) * rows, :].rearrange("(p n) c -> p n c", p=P),
                                         zt[:].rearrange("p (n c) -> p n c", c=ROWW)[:, 0:rows // P, 0:P]).then_inc(zeroed, 16)

                bodies(sp, body)
                sp.wait_ge(w_lo_dve, NE0)
                for dst, src in ((raw[0][:, 0:P], d["L1_cond_Wq2"]), (raw[0][:, P:2 * P], d["L1_cond_Wk2"]),
                                 (raw[0][:, 2 * P:3 * P], d["L1_cond_Wv"][P:2 * P, :]), (m["wv1"][:], d["L1_cond_Wv"][0:P, :]),
                                 (m["bvc"][:], d["L1_cond_bv"].rearrange("(p a) -> p a", a=1)),
                                 (m["wg"][:], d["L1_ffn_wg"])):
                    sp.dma_start(dst, src).then_inc(m["att_in"], 16)
                sp.wait_ge(zeroed, 16 * 2 * E)

            @block.gpsimd
            def _(gp):
                gp.memset(ident[:], 0.0).then_inc(ident_ready, 1)
                gp.wait_ge(ident_ready, 1)
                gp.affine_select(out=ident[:], in_=ident[:], compare_op=ALU.not_equal, fill=1.0, base=0,
                                 pattern=[[-1, P]], channel_multiplier=1).then_inc(ident_ready, 1)
                gp.iota(iota8[:], pattern=[[1, E]], base=0, channel_multiplier=0, allow_small_or_imprecise_dtypes=True).then_inc(ident_ready, 1)
                for e in range(1, NE0, 2):
                    gp.wait_ge(w_in[e], 32)
                    o = slice(e * 2 * H, (e + 1) * 2 * H)
                    gp.tensor_copy(w_hi[:, o], loaded(e)).then_inc(w_hi_pool, 1)
                    gp.wait_ge(w_hi_pool, e // 2 + 1)
                    gp.tensor_tensor(w_lo[:, o], loaded(e), w_hi[:, o], ALU.subtract).then_inc(w_lo_pool, 1)
                gp.memset(zt[:], 0.0).then_inc(zt_ready, 1)
                gp.wait_ge(zt_ready, 1)
                gp.memset(zt[:].rearrange("p (n c) -> p n c", c=ROWW)[:, :, P:ROWW], FAR).then_inc(zt_ready, 1)

                def body(i, par, nslots):
                    for s in range(nslots):
                        at = unit_at(i, par, s, 1)
                        if at and on_pool(at[2]):
                            c, _, u = at
                            gp.wait_ge(gelu_done, 2 * (UNITS * c + u + 1))
                            atleast(gp, w2_done, UNITS * c + u - 7)
                            gp.tensor_tensor(glo(u), gf(u), ghi(u), ALU.subtract).then_inc(lo_pool, 1)
                        at = unit_at(i, par, s, BEHIND + 2)
                        if at and group_of(at[2])[2] and 1 <= group_of(at[2])[0] < E:
                            c, k = at[0], group_of(at[2])[0]
                            gp.wait_ge(y_read, NGRP * c + k + 1)
                            atleast(gp, acc_added, (E - 1) * c + k - 1)
                            gp.tensor_tensor(acc[:], acc[:], tmp[k % 2][:], ALU.add).then_inc(acc_added, 1)

                bodies(gp, body)

            @block.tensor
            def _(pe):
                def turn_x(n):
                    pe.wait_ge(x_in, 16 * CT * (n + 1))
                    atleast(pe, x_kept, n)
                    atleast(pe, wT_ready, n - 1)
                    for k in range(CT):
                        t = pe.transpose(xt_cols[:, k * P:(k + 1) * P], xrows[:, k * P:(k + 1) * P], ident[:])
                    t.then_inc(xt_acc, 1)

                def prefill(n, q):
                    if q == 0:
                        atleast(pe, x_split, 2 * n + 2)
                    if q < 2:
                        dst = zr_bank[:].rearrange("p (s c) -> p s c", s=STEPS)[:, :, q * B:(q + 1) * B]
                    else:
                        dst = half(hh_bank, 0).rearrange("p (s c) -> p s c", s=STEPS)
                    mm3(pe, dst, wx_hi[:, q * P:(q + 1) * P], wx_lo[:, q * P:(q + 1) * P],
                        x_hi[:].rearrange("p (s b) -> p s b", b=B), x_lo[:].rearrange("p (s b) -> p s b", b=B), q != 1, False)
                    for v in (vb_hi, vb_lo):
                        r = v[:, q * B:(q + 1) * B].unsqueeze(1).broadcast_to([P, STEPS, B])
                        t = pe.matmul(dst, identr[:], r, start=False, stop=False, skip_group_check=True)
                    t.then_inc(prefilled, 1)

                pe.wait_ge(ident_ready, 2)
                turn_x(0)
                pe.wait_ge(scan_in, NSCAN)
                pe.wait_ge(x_split, 2)
                pe.transpose(gate_bank[:, 0:B + 3], condr[:], ident[0:B + 3, 0:B + 3]).then_inc(setup_pe, 1)
                pe.wait_ge(setup_dve, 2)
                for g in range(3):
                    t = pe.matmul(bank[4][:, g * B:(g + 1) * B], cv[:, g * P:(g + 1) * P], condT[:], start=(g == 0), stop=(g == 2), skip_group_check=True)
                t.then_inc(setup_pe, 1)
                pe.wait_ge(setup_dve, SETUP_DVE)
                for q in range(2):
                    prefill(0, q)

                def vectors():
                    pe.wait_ge(small_in, NSMALL)
                    pe.transpose(gate_bank[:, 0:NVEC], vecs[0:NVEC, :], ident[0:NVEC, 0:NVEC]).then_inc(vec_pe, 1)

                def a1_products():
                    pe.wait_ge(a1_in, 80)
                    pe.matmul(bank[5][0:B, 0:P], condT[:], wq1[:], start=True, stop=True, skip_group_check=True)
                    pe.matmul(bank[5][0:B, P:2 * P], condT[:], wk1[:], start=False, stop=True, skip_group_check=True).then_inc(a1_pe, 1)

                def scan_part(i, par, p):
                    t = p // 2
                    n = STEPS * i + t + 1
                    zr = zr_bank[:, t * 2 * B:(t + 1) * 2 * B]
                    if p % 2 == 0:
                        for k in range(3):
                            pe.wait_ge(hparts, 3 * n - 2 + k)
                            for q in (1, 0):
                                for j in range(3 - k):
                                    mm = pe.matmul(zr[:, q * B:(q + 1) * B], ub[j][:, q * P:(q + 1) * P], hb_[k][:], start=False, stop=False, skip_group_check=True)
                        mm.then_inc(zr_acc, 1)
                    else:
                        pe.wait_ge(rh_ready, n)
                        pe.matmul(hh_bank[:, t * B:(t + 1) * B], uh[:, 2 * P:3 * P], rh[:], start=False, stop=False, skip_group_check=True).then_inc(hh_acc, 1)

                def first_layer(c, cpar, u):
                    e, hb = u // HB, u % HB
                    if u == 0:
                        pe.wait_ge(h_split, 2 * (c + 1))
                    if isinstance(c, int) and c == 0 and hb == 0:
                        if e % 2:
                            pe.wait_ge(w_lo_pool, e // 2 + 1)
                        else:
                            pe.wait_ge(w_lo_dve, e + 2)
                    atleast(pe, gelu_done, 2 * (UNITS * c + u - (1 if cpar == 0 and u < 2 else 2)))
                    mm3(pe, w1_out(cpar, u), w1(w_hi, e, hb), w1(w_lo, e, hb), h_hi[cpar][:], h_lo[cpar][:], True, True).then_inc(w1_done, 1)

                def second_layer(c, cpar, u):
                    e, hb = u // HB, u % HB
                    k, first, last = group_of(u)
                    if first:
                        atleast(pe, y_read, NGRP * c + k - 1)
                    lo_wait(pe, c, u)
                    mm3(pe, y_out(cpar, k), w2(w_hi, e, hb), w2(w_lo, e, hb), ghi(u), glo(u), first, last).then_inc(w2_done, 1)

                def gates(c, cpar):
                    pe.wait_ge(h_ready, STEPS * (c + 1) + 1)
                    atleast(pe, wT_ready, c)
                    atleast(pe, x_kept, min(c + 2, NCH) if isinstance(c, int) else c + 2)
                    for k in range(CT):
                        t = pe.matmul(gate_bank[:, k * E:(k + 1) * E], h[cpar][:, k * P:(k + 1) * P], rw[:], start=(k == 0), stop=(k == CT - 1), skip_group_check=True)
                    t.then_inc(gate_acc, 1)

                def body(i, par, nslots):
                    scan, more, ffn = within(i, NCH - 1), within(i, NCH - 2), within(i - 1, NCH - 1)
                    for s in range(nslots):
                        if scan and s in PART_OF_SLOT:
                            scan_part(i, par, PART_OF_SLOT[s])
                        if isinstance(i, int) and i == 0 and s == 5:
                            vectors()
                        if isinstance(i, int) and i == 0 and s == 10:
                            a1_products()
                        if scan and s == 0:
                            prefill(i, 2)
                        if more and s == part_slot(2 * STEPS - 1):
                            for q in range(2):
                                prefill(i + 1, q)
                        at = unit_at(i, par, s, 0)
                        if at:
                            first_layer(*at)
                        at = unit_at(i, par, s, BEHIND)
                        if at:
                            second_layer(*at)
                        if ffn and s == 1:
                            gates(i - 1, 1 - par)
                        if ffn and s == 7:
                            pe.wait_ge(gate_step, GSTEPS * i)
                            for k in range(CT):
                                t = pe.transpose(gate_bank[0:E, k * P:(k + 1) * P], wt[:, k * E:(k + 1) * E], ident[:])
                            t.then_inc(wT_acc, 1)
                        if more and s == 14:
                            turn_x(i + 1)

                bodies(pe, body)
            @block.scalar
            def _(act):
                for dst, src in (
                    (cv[:, 0:P], d["L0_cond_C_z"]), (cv[:, P:2 * P], d["L0_cond_C_r"]), (cv[:, 2 * P:3 * P], d["L0_cond_C"]),
                    (uh[:, 0:P], d["L0_cond_U_z"]), (uh[:, P:2 * P], d["L0_cond_U_r"]), (uh[:, 2 * P:3 * P], d["L0_cond_U"]),
                ):
                    act.dma_start(dst, src).then_inc(scan_in, 16)
                for dst, src in (
                    (vecs[R_BK2:R_BK2 + 1, :], d["L1_cond_bk2"].rearrange("(a p) -> a p", a=1)),
                    (vecs[R_FB1:R_FB1 + 32, :], d["L1_ffn_fc1_b"].rearrange("s (m p) -> (s m) p", p=P)),
                    (vecs[R_FB2:R_FB2 + 8, :], d["L1_ffn_fc2_b"]),
                    (rw[:], d["L0_ffn_rW"]),
                    (rbb[:], d["L0_ffn_rb"].rearrange("(a p) -> a p", a=1).broadcast_to([P, E])),
                ):
                    act.dma_start(dst, src).then_inc(small_in, 16)
                act.wait_ge(ident_ready, 3)
                act.activation(th[:, 0:1], iota8[:, 0:1], ACT.Gelu).then_inc(gate_tanh, 1)
                for dst, src in (
                    (wq1[:], d["L1_cond_Wq1"]), (wk1[:], d["L1_cond_Wk1"]),
                    (bq1[:], d["L1_cond_bq1"].rearrange("(a p) -> a p", a=1).broadcast_to([B, P])),
                    (bk1[:], d["L1_cond_bk1"].rearrange("(a p) -> a p", a=1).broadcast_to([B, P])),
                    (alph[:], d["L1_cond_alpha"].rearrange("(a p) -> a p", a=1).broadcast_to([B, 1])),
                ):
                    act.dma_start(dst, src).then_inc(a1_in, 16)

                def keep_x(n):
                    act.wait_ge(x_split, 2 * n + 2)
                    act.activation(xT[:, bass.ds(n * CH, CH)], xt_cols, ACT.Identity, bias=sbias[:]).then_inc(x_kept, 1)

                def scan_part(i, par, p):
                    t = p // 2
                    n = STEPS * i + t + 1
                    if p % 2 == 0:
                        act.wait_ge(zr_acc, n)
                        act.activation(tzr[:], zr_bank[:, t * 2 * B:(t + 1) * 2 * B], ACT.Tanh, scale=0.5).then_inc(zr_tanh, 1)
                    else:
                        act.wait_ge(hh_acc, n)
                        act.activation(hh[:], hh_bank[:, t * B:(t + 1) * B], ACT.Tanh).then_inc(hh_tanh, 1)

                def split_weights(p):
                    e, k = SPLIT_AT[p]
                    act.wait_ge(w_in[e], 32)
                    act.activation(w_hi[:, (2 * e + k) * H:(2 * e + k + 1) * H], loaded(e)[:, k * H:(k + 1) * H], ACT.Copy).then_inc(w_hi_act, 1)

                def gelu(c, cpar, u):
                    act.wait_ge(w1_done, UNITS * c + u + 1)
                    lo_wait(act, c, u, 4)
                    atleast(act, w2_done, UNITS * c + u - 7)
                    bias = vecT[:, R_SB1 + u:R_SB1 + u + 1]
                    act.activation(gf(u), w1_out(cpar, u), ACT.Gelu, bias=bias).then_inc(gelu_done, 2 if hi_on_dve(u) else 1)
                    if not hi_on_dve(u):
                        act.activation(ghi(u), w1_out(cpar, u), ACT.Gelu, bias=bias).then_inc(gelu_done, 1)

                def body(i, par, nslots):
                    scan, more, ffn = within(i, NCH - 1), within(i, NCH - 2), within(i - 1, NCH - 1)
                    for s in range(nslots):
                        if scan and s in PART_OF_SLOT:
                            scan_part(i, par, PART_OF_SLOT[s])
                            if isinstance(i, int) and i == 0 and PART_OF_SLOT[s] in SPLIT_AT:
                                split_weights(PART_OF_SLOT[s])
                        if isinstance(i, int) and i == 0 and s == 10:
                            act.wait_ge(vec_step, 3)
                            keep_x(0)
                        at = unit_at(i, par, s, 1)
                        if at:
                            gelu(*at)
                        if ffn and s == 4:
                            act.wait_ge(gate_step, GSTEPS * (i - 1) + 2 + CT)
                            act.activation(th[:], dlt[:], ACT.Tanh, scale=0.5).then_inc(gate_tanh, 1)
                        if more and s == 17:
                            keep_x(i + 1)
                        if ffn and s == 12:
                            act.wait_ge(wT_acc, i)
                            atleast(act, y_read, NGRP * (i - 1))
                            act.activation(wT[:], gate_bank[0:E, 0:CH], ACT.Copy).then_inc(wT_ready, 1)

                bodies(act, body)
            @block.vector
            def _(dve):
                def split_x(n):
                    dve.wait_ge(xt_acc, n + 1)
                    atleast(dve, prefilled, 3 * n)
                    dve.tensor_copy(x_hi[:], xt_cols).then_inc(x_split, 1)
                    dve.wait_ge(x_split, 2 * n + 1)
                    dve.tensor_tensor(x_lo[:], xt_cols, x_hi[:], ALU.subtract).then_inc(x_split, 1)

                dve.memset(h[1][:, CH - B:CH], 0.0).then_inc(h_ready, 1)
                for k in range(3):
                    dve.memset(hb_[k][:], 0.0).then_inc(hparts, 1)
                split_x(0)
                dve.wait_ge(setup_pe, 1)
                dve.tensor_copy(condT[:], gate_bank[:, 0:B]).then_inc(setup_dve, 1)
                dve.tensor_copy(bcol[:], gate_bank[:, B:B + 3]).then_inc(setup_dve, 1)
                dve.tensor_scalar(uh[:, 2 * P:3 * P], uh[:, 2 * P:3 * P], 0.5, None, ALU.mult).then_inc(setup_dve, 1)
                dve.tensor_copy(wx_hi[:], wx[:]).then_inc(setup_dve, 1)
                dve.tensor_copy(ub[0][:], uh[:, 0:2 * P]).then_inc(setup_dve, 1)
                dve.wait_ge(ident_ready, 3)
                dve.tensor_copy(identr[:], ident[:]).then_inc(setup_dve, 1)
                dve.wait_ge(setup_dve, 6)
                dve.tensor_tensor(wx_lo[:], wx[:], wx_hi[:], ALU.subtract).then_inc(setup_dve, 1)
                dve.tensor_tensor(urest[:], uh[:, 0:2 * P], ub[0][:], ALU.subtract).then_inc(setup_dve, 1)
                dve.wait_ge(setup_dve, 8)
                dve.tensor_copy(ub[1][:], urest[:]).then_inc(setup_dve, 1)
                dve.wait_ge(setup_pe, 2)
                for g in range(3):
                    dve.tensor_scalar(vb[:, g * B:(g + 1) * B], bank[4][:, g * B:(g + 1) * B], bcol[:, g:g + 1], None, ALU.add).then_inc(setup_dve, 1)
                dve.wait_ge(setup_dve, 12)
                dve.tensor_tensor(ub[2][:], urest[:], ub[1][:], ALU.subtract).then_inc(setup_dve, 1)
                dve.tensor_copy(vb_hi[:], vb[:]).then_inc(setup_dve, 1)
                dve.wait_ge(setup_dve, 14)
                dve.tensor_tensor(vb_lo[:], vb[:], vb_hi[:], ALU.subtract).then_inc(setup_dve, 1)

                def vectors():
                    dve.wait_ge(vec_pe, 1)
                    dve.tensor_copy(vecT[:], gate_bank[:, 0:NVEC]).then_inc(vec_step, 1)
                    dve.wait_ge(vec_step, 1)
                    dve.tensor_tensor(sbias[:], vecT[:, R_SB2:R_SB2 + 1], vecT[:, R_SB2 + 1:R_SB2 + 2], ALU.add).then_inc(vec_step, 1)
                    dve.wait_ge(vec_step, 2)
                    dve.tensor_scalar(sbias[:], sbias[:], 0.5, None, ALU.mult).then_inc(vec_step, 1)

                def a1_scores():
                    dve.wait_ge(a1_pe, 1)
                    dve.tensor_tensor(q1[:], bank[5][0:B, 0:P], bq1[:], ALU.add).then_inc(a1_dve, 1)
                    dve.tensor_tensor(k1[:], bank[5][0:B, P:2 * P], bk1[:], ALU.add).then_inc(a1_dve, 1)
                    dve.wait_ge(a1_dve, 2)
                    dve.tensor_tensor_reduce(out=e1[:], in0=q1[:], in1=k1[:], scale=1.0, scalar=0.0, op0=ALU.mult, op1=ALU.add,
                                             accum_out=s1[:, 0:1]).then_inc(a1_dve, 1)
                    dve.wait_ge(a1_dve, 3)
                    dve.tensor_scalar(a1[:], s1[:, 0:1].broadcast_to([B, P]), SCALE, None, ALU.mult).then_inc(a1_dve, 1)
                    dve.wait_ge(a1_dve, 4)
                    dve.tensor_reduce(s1[:, 1:2], a1[:], AX.X, ALU.max, negate=True).then_inc(a1_dve, 1)

                def scan_part(i, par, p):
                    t = p // 2
                    n = STEPS * i + t + 1
                    hp = h[par][:, (t - 1) * B:t * B] if t else h[1 - par][:, CH - B:CH]
                    if p % 2 == 0:
                        dve.wait_ge(zr_tanh, n)
                        dve.scalar_tensor_tensor(out=rh[:], in0=tzr[:, B:2 * B], scalar=1.0, in1=hp, op0=ALU.add, op1=ALU.mult).then_inc(rh_ready, 1)
                        dve.tensor_scalar(z[:], tzr[:, 0:B], 0.5, 0.5, ALU.mult, ALU.add).then_inc(z_ready, 1)
                        dve.wait_ge(z_ready, n)
                        dve.scalar_tensor_tensor(out=kept[:], in0=z[:], scalar=-1.0, in1=hp, op0=ALU.add, op1=ALU.mult).then_inc(kept_ready, 1)
                    else:
                        dve.wait_ge(hh_tanh, n)
                        dve.tensor_tensor(zhh[:], z[:], hh[:], ALU.mult).then_inc(zhh_ready, 1)
                        dve.wait_ge(zhh_ready, n)
                        dve.wait_ge(kept_ready, n)
                        hn = h[par][:, t * B:(t + 1) * B]
                        dve.tensor_tensor(hb_[0][:], zhh[:], kept[:], ALU.subtract).then_inc(hparts, 1)
                        dve.tensor_tensor(hn, zhh[:], kept[:], ALU.subtract).then_inc(h_ready, 1)
                        dve.wait_ge(hparts, 3 * n + 1)
                        dve.wait_ge(h_ready, n + 1)
                        dve.tensor_tensor(hb_[1][:], hn, hb_[0][:], ALU.subtract).then_inc(hparts, 1)
                        dve.tensor_tensor(hrest[:], hn, hb_[0][:], ALU.subtract).then_inc(hrest_ready, 1)
                        dve.wait_ge(hparts, 3 * n + 2)
                        dve.wait_ge(hrest_ready, n)
                        dve.tensor_tensor(hb_[2][:], hrest[:], hb_[1][:], ALU.subtract).then_inc(hparts, 1)

                def split_weights(p):
                    e, k = SPLIT_AT[p]
                    dve.wait_ge(w_hi_act, e + k + 1)
                    o = slice((2 * e + k) * H, (2 * e + k + 1) * H)
                    dve.tensor_tensor(w_lo[:, o], loaded(e)[:, k * H:(k + 1) * H], w_hi[:, o], ALU.subtract).then_inc(w_lo_dve, 1)

                def low_part(c, cpar, u):
                    dve.wait_ge(gelu_done, 2 * (UNITS * c + u + 1))
                    atleast(dve, w2_done, UNITS * c + u - 7)
                    if hi_on_dve(u):
                        dve.tensor_copy(ghi(u), gf(u)).then_inc(hi_dve, 1)
                        dve.wait_ge(hi_dve, units_up_to(hi_on_dve, c, u))
                    dve.tensor_tensor(glo(u), gf(u), ghi(u), ALU.subtract).then_inc(lo_dve, 1)

                def combine(c, cpar, k):
                    last = NSH * HB + k * HB
                    dve.wait_ge(w2_done, UNITS * c + last)
                    y = y_out(cpar, k)
                    if k == 0:
                        atleast(dve, x1_ready, c)
                        dve.wait_ge(x_kept, c + 1)
                        dve.scalar_tensor_tensor(out=acc[:], in0=y, scalar=0.5, in1=xT[:, bass.ds(c * CH, CH)], op0=ALU.mult, op1=ALU.add).then_inc(y_read, 1)
                        return
                    if k == 1:
                        dve.wait_ge(wb_ready, 16 * (c + 1))
                    if k == 2:
                        atleast(dve, x1_ready, c)
                    else:
                        atleast(dve, acc_added, (E - 1) * c + max(k - 2, 0))
                    dve.scalar_tensor_tensor(out=tmp[k % 2][:], in0=y, scalar=vecT[:, R_B2 + k - 1:R_B2 + k], in1=wb[:, (k - 1) * CH:k * CH],
                                             op0=ALU.add, op1=ALU.mult).then_inc(y_read, 1)
                    if k == E:
                        dve.wait_ge(y_read, NGRP * (c + 1))
                        dve.wait_ge(acc_added, (E - 1) * (c + 1))
                        dve.tensor_tensor(x1T_tb[:, bass.ds(c * STEPS, STEPS), :], acc[:].rearrange("p (t b) -> p t b", b=B),
                                          tmp[k % 2][:].rearrange("p (t b) -> p t b", b=B), ALU.add).then_inc(x1_ready, 1)

                def v3(a, w):
                    return a[:].rearrange("p (k e) -> p k e", e=w)

                def gate_a(c):
                    n = GSTEPS * c
                    dve.wait_ge(gate_acc, c + 1)
                    dve.tensor_tensor(v3(lg, E), gate_bank[:, 0:CT * E].rearrange("p (k e) -> p k e", e=E),
                                      rbb[:].unsqueeze(1).broadcast_to([P, CT, E]), ALU.add).then_inc(gate_step, 1)
                    dve.wait_ge(gate_step, n + 1)
                    dve.tensor_scalar(lgmax[:], lg[:, 0:1], 1.0, None, ALU.mult)
                    for k in range(CT):
                        dve.max(mx[:, k * 8:(k + 1) * 8], lg[:, k * E:(k + 1) * E]).then_inc(gate_step, 1)
                    dve.wait_ge(gate_step, n + 1 + CT)
                    dve.tensor_tensor(dlt[:].unsqueeze(2), v3(mx, 8)[:, :, 0:1], v3(mx, 8)[:, :, 1:2], ALU.subtract).then_inc(gate_step, 1)
                    for k in range(CT):
                        dve.max_index(ix[:, k * 8:(k + 1) * 8], mx[:, k * 8:(k + 1) * 8], lg[:, k * E:(k + 1) * E]).then_inc(gate_step, 1)
                    dve.wait_ge(gate_step, n + 2 + 2 * CT)
                    dve.tensor_scalar(v3(ixf, 2), v3(ix, 8)[:, :, 0:2], 1.0, None, ALU.mult).then_inc(gate_step, 1)

                def gate_b(c):
                    n = GSTEPS * c + 2 * CT
                    dve.wait_ge(gate_tanh, c + 2)
                    dve.tensor_scalar(p0[:], th[:], 0.5, 0.5, ALU.mult, ALU.add).then_inc(gate_step, 1)
                    dve.tensor_scalar(p1[:], th[:], -0.5, 0.5, ALU.mult, ALU.add).then_inc(gate_step, 1)
                    dve.wait_ge(gate_step, n + 3)
                    io = iota8[:].unsqueeze(1).broadcast_to([P, CT, E])
                    for q, oh in enumerate((oh0, oh1)):
                        dve.tensor_tensor(v3(oh, E), io, v3(ixf, 2)[:, :, q:q + 1].broadcast_to([P, CT, E]), ALU.is_equal).then_inc(gate_step, 1)
                    dve.wait_ge(gate_step, n + 7)
                    for oh, p in ((oh0, p0), (oh1, p1)):
                        dve.tensor_tensor(v3(oh, E), v3(oh, E), p[:].unsqueeze(2).broadcast_to([P, CT, E]), ALU.mult).then_inc(gate_step, 1)
                    dve.wait_ge(gate_step, n + 9)
                    dve.tensor_tensor(wt[:], oh0[:], oh1[:], ALU.add).then_inc(gate_step, 1)

                def split_h(c, cpar):
                    dve.wait_ge(h_ready, STEPS * (c + 1) + 1)
                    dve.tensor_copy(h_hi[cpar][:], h[cpar][:]).then_inc(h_split, 1)
                    dve.wait_ge(h_split, 2 * c + 1)
                    dve.tensor_tensor(h_lo[cpar][:], h[cpar][:], h_hi[cpar][:], ALU.subtract).then_inc(h_split, 1)

                def body(i, par, nslots):
                    scan, more, ffn = within(i, NCH - 1), within(i, NCH - 2), within(i - 1, NCH - 1)
                    for s in range(nslots):
                        if scan and s in PART_OF_SLOT:
                            scan_part(i, par, PART_OF_SLOT[s])
                            if isinstance(i, int) and i == 0 and PART_OF_SLOT[s] in SPLIT_AT:
                                split_weights(PART_OF_SLOT[s])
                        if isinstance(i, int) and i == 0 and s == 5:
                            vectors()
                        if isinstance(i, int) and i == 0 and s == 12:
                            a1_scores()
                        if ffn and s == 0:
                            split_h(i - 1, 1 - par)
                        at = unit_at(i, par, s, 1)
                        if at and not on_pool(at[2]):
                            low_part(*at)
                        if ffn and s == 3:
                            gate_a(i - 1)
                        if ffn and s == 5:
                            gate_b(i - 1)
                        if more and s == 15:
                            split_x(i + 1)
                        at = unit_at(i, par, s, BEHIND + 1)
                        if at and group_of(at[2])[2]:
                            combine(at[0], at[1], group_of(at[2])[0])

                bodies(dve, body)


NSCAN, NSMALL = 13 * 16, 10 * 16
SETUP_DVE = 15
A1_DVE = 7


def phase_attention(nc, d, m):
    bank, ident, identr, vecT = m["bank"], m["ident"], m["identr"], m["vecT"]
    condT, xT, x1T, wide, alphaT, iota8 = (m[k] for k in ("condT", "xT", "x1T", "wide", "alphaT", "iota8"))
    w_hi, w_lo, raw, slots = m["w_hi"], m["w_lo"], m["raw"], m["slots"]
    gates_all, firsts, firsts_u = m["gates_all"], m["firsts"], m["firsts_u"]
    alph, s1, a1, e1, a1_pe, a1_dve, a1_act, wv1, bvc, wg, att_in = (m[k] for k in ("alph", "s1", "a1", "e1", "a1_pe", "a1_dve", "a1_act", "wv1", "bvc", "wg", "att_in"))
    hs, dispatch, hs_ready, hs_free, pos_ready, posi, hid_kept, wts_in = (m[k] for k in ("hs", "dispatch", "hs_ready", "hs_free", "pos_ready", "posi", "hid_kept", "wts_in"))
    x1rows, hid = xT, wide
    hid3 = hid[:].rearrange("p (b c) -> p b c", c=ROWW)
    GT = GRP * P
    TE = TOPK * E
    ME = GRP * TE
    BF16 = mybir.dt.bfloat16

    with ExitStack() as ctx:
        def sb(name, shape, dt=F32):
            return ctx.enter_context(nc.sbuf_tensor(name, shape, dt))

        def sem(name):
            return ctx.enter_context(nc.semaphore(name))

        cvT = sb("cvT", [P, B])
        lowtri = sb("lowtri", [P, P])
        lowtri_b = sb("lowtri_b", [P, P], BF16)
        ones_b = sb("ones_b", [P, P], BF16)
        xg = sb("xg", [P, GT])
        xg_hi = sb("xg_hi", [P, GT], F32R)
        xg_lo = sb("xg_lo", [P, GT], F32R)
        qT = sb("qT", [P, GT])
        kT = sb("kT", [P, GT])
        vT = sb("vT", [P, GT])
        v = [sb(f"v{i}", [P, GT]) for i in range(2)]
        smax = sb("smax", [P, GRP])
        nsmax = sb("nsmax", [P, GRP])
        pr = sb("pr", [P, GT])
        rs = sb("rs", [P, GRP])
        rinv = sb("rinv", [P, GRP])
        am = sb("am", [P, GT])
        amT = sb("amT", [P, GT])
        hg = sb("hg", [P, GT])
        hT = sb("hT", [P, GT])
        lmax = sb("lmax", [P, GRP]); lsh = sb("lsh", [P, GRP * E]); lex = sb("lex", [P, GRP * E])
        lsum = sb("lsum", [P, GRP]); lrec = sb("lrec", [P, GRP]); sc = sb("sc", [P, GRP * E]); first_sc = sb("first_sc", [P, 1])
        mx = sb("mx8", [P, GRP * 8]); ix = sb("ix8", [P, GRP * 8], U32); ixf = sb("ixf8", [P, GRP * TOPK])
        den = sb("den", [P, GRP]); dinv = sb("dinv", [P, GRP])
        mask = sb("mask", [P, ME], BF16)
        run = sb("run", [P, TE])
        loc = sb("loc", [P, ME]); sel = sb("sel", [P, ME])
        rank = sb("rank", [P, GRP * TOPK])
        cmul = sb("cmul", [P, TOPK]); cadd = sb("cadd", [P, TOPK])
        over = sb("over", [P, GRP * TOPK]); pos = sb("pos", [P, GRP * TOPK])
        mask1 = sb("mask1", [P, B * E]); rank_all = sb("rank_all", [P, B * TOPK])
        sel1 = sb("sel1", [P, B * E]); before1 = sb("before1", [P, B]); keep = sb("keep", [P, B * TOPK])

        w_conv = sem("att_w_ready"); const_step = sem("const_step"); run_zero = sem("run_zero"); cv_acc = sem("cv_acc")
        x_in = sem("xg_in"); x_ready = sem("x_ready"); q_acc = sem("q_acc"); k_acc = sem("k_acc"); v_acc = sem("v_acc")
        q_ready = sem("q_ready"); k_ready = sem("k_ready"); vT_ready = sem("vT_ready"); vt_acc = sem("vt_acc"); v_ready = sem("v_ready")
        rows_acc = sem("rows_acc"); rows_done = sem("rows_done")
        s_acc = sem("s_acc"); smax_ready = sem("smax_ready"); p_ready = sem("p_ready"); rinv_ready = sem("rinv_ready"); a_ready = sem("a_ready")
        aT_acc = sem("aT_acc"); aT_ready = sem("aT_ready"); hid_acc = sem("hid_acc"); hg_ready = sem("hg_ready")
        hidT_acc = sem("hidT_acc"); hidT_ready = sem("hidT_ready"); logit_acc = sem("logit_acc"); 
        r_step = sem("r_step"); l_exp = sem("l_exp"); rank_acc = sem("rank_acc"); id_step = sem("id_step")
        f_step = sem("f_step")

        LOADS = 6
        bq, bk, bv_, br, bs, ba, bh, bm = bank
        WQ, WK, WV = 0, 1, 2

        def v3(a, w):
            return a[:].rearrange("p (k e) -> p k e", e=w)

        NX = 4

        def x_cols(g):
            return x1T[:, g * GT:(g + 1) * GT] if isinstance(g, int) and g < NX else xg[:]

        mask4 = mask[:].rearrange("p (k q e) -> p k q e", q=TOPK, e=E)

        def pipeline(eng, turn):
            turn(-1, 1, True, False, False, False)
            turn(0, 0, True, True, False, False)
            turn(1, 1, True, True, True, False)
            turn(2, 0, True, True, True, True)
            with eng.Fori(0, (NG - 4) // 2) as k:
                turn(k * 2 + 3, 1, True, True, True, True)
                turn(k * 2 + 4, 0, True, True, True, True)
            turn(NG - 1, 1, False, True, True, True)
            turn(NG, 0, False, False, True, True)
            turn(NG + 1, 1, False, False, False, True)

        with nc.Block() as block:
            @block.sync
            def _(sp):
                sp.dma_start(xg[:], x1T[:, NX * GT:(NX + 1) * GT]).then_inc(x_in, 16)

                def turn(i, par, load):
                    if load:
                        sp.wait_ge(rows_acc, i + 2)
                        sp.dma_start(xg[:], x1T[:, bass.ds((i + 2) * GT, GT)]).then_inc(x_in, 16)
                    b = i - 1
                    sp.wait_ge(hg_ready, b + 1)
                    sp.dma_start(hid3[:, bass.ds(b * GRP, GRP), 0:P], v3(hg, P)).then_inc(hid_kept, 16)
                    if isinstance(b, int) and b == 0:
                        sp.wait_ge(hid_kept, 16)
                    else:
                        sp.wait_ge(hs_free, b)
                    sp.dma_start(hs[1 - par][:], hid[:, bass.ds(b * GRP * ROWW, GRP * ROWW)]).then_inc(hs_ready, 16)

                turn(1, 1, False)
                turn(2, 0, False)
                with sp.Fori(0, (NG - 6) // 2) as k:
                    turn(k * 2 + 3, 1, True)
                    turn(k * 2 + 4, 0, True)
                turn(NG - 3, 1, True)
                sp.wait_ge(w_conv, 4)
                for e in range(2):
                    load_expert_weights(sp, d, raw, wts_in, e)
                turn(NG - 2, 0, False)
                turn(NG - 1, 1, False)
                turn(NG, 0, False)

            @block.gpsimd
            def _(gp):
                gp.memset(lowtri[:], 1.0).then_inc(const_step, 1)
                gp.wait_ge(const_step, 1)
                gp.affine_select(out=lowtri[:], in_=lowtri[:], compare_op=ALU.is_ge, fill=0.0, base=0, pattern=[[1, P]],
                                 channel_multiplier=-1).then_inc(const_step, 1)
                gp.iota(hid3[:, :, P:ROWW], pattern=[[P, B], [1, 1]], base=0, channel_multiplier=1, allow_small_or_imprecise_dtypes=True).then_inc(id_step, 1)
                last_slot = gp.to_reg(SLOT_ROWS - 1)
                dispatch(gp, last_slot, 0, 0, 0)
                with gp.Fori(0, (NG - 4) // 2) as k:
                    dispatch(gp, last_slot, k * 2 + 1, 1, k + 1)
                    dispatch(gp, last_slot, k * 2 + 2, 0, k + 1)
                dispatch(gp, last_slot, NG - 3, 1, (NG - 2) // 2)
                dispatch(gp, last_slot, NG - 2, 0, (NG - 2) // 2)

            @block.tensor
            def _(pe):
                def wpart(t, q):
                    return t[:, q * P:(q + 1) * P]

                def jcols(j, w=P):
                    return slice(j * w, (j + 1) * w)

                pe.wait_ge(att_in, 16 * LOADS)
                pe.matmul(bm[:, 0:B], wv1[:], condT[:], start=True, stop=True).then_inc(cv_acc, 1)
                pe.wait_ge(w_conv, 4)
                pe.wait_ge(id_step, 1)

                def alpha_column():
                    pe.wait_ge(a1_dve, A1_DVE)
                    pe.transpose(bh[:, 0:B], a1[:], ident[0:B, 0:B]).then_inc(a1_pe, 1)

                def turn(i, par, project, soften, attend, route):
                    a, b, r = i + 1, i - 1, i - 2
                    if soften:
                        pe.wait_ge(q_ready, i + 1)
                        pe.wait_ge(k_ready, i + 1)
                        atleast(pe, p_ready, GRP * i)
                        for j in range(GRP):
                            t = pe.matmul(bs[:, jcols(j)], qT[:, jcols(j)], kT[:, jcols(j)], start=(j == 0), stop=True, skip_group_check=True)
                        t.then_inc(s_acc, 1)
                    if route:
                        pe.wait_ge(hidT_ready, r + 1)
                        for j in range(GRP):
                            t = pe.matmul(bm[:, jcols(j, E)], hT[:, jcols(j)], wg[:], start=(j == 0), stop=True, skip_group_check=True)
                        t.then_inc(logit_acc, 1)
                    if attend:
                        pe.wait_ge(a_ready, (b + 1) * GRP)
                        atleast(pe, hidT_ready, b)
                        for j in range(GRP):
                            t = pe.transpose(ba[:, jcols(j)], am[:, jcols(j)], ident[:])
                        t.then_inc(aT_acc, 1)
                    if project:
                        pe.wait_ge(x_ready, (a + 1) * 2)
                        atleast(pe, q_ready, a)
                        atleast(pe, k_ready, a)
                        atleast(pe, vT_ready, a)
                        if route:
                            atleast(pe, pos_ready, i - 2)
                        mm3(pe, bq[:], wpart(w_hi, WQ), wpart(w_lo, WQ), xg_hi[:], xg_lo[:], True, True).then_inc(q_acc, 1)
                        mm3(pe, bk[:], wpart(w_hi, WK), wpart(w_lo, WK), xg_hi[:], xg_lo[:], True, True).then_inc(k_acc, 1)
                        mm3(pe, bv_[:], wpart(w_hi, WV), wpart(w_lo, WV), xg_hi[:], xg_lo[:], True, True).then_inc(v_acc, 1)
                        if isinstance(i, int) and i < 0:
                            alpha_column()
                        atleast(pe, v_ready, a)
                        for j in range(GRP):
                            t = pe.transpose(br[:, jcols(j)], x_cols(a)[:, jcols(j)], ident[:])
                        t.then_inc(rows_acc, 1)
                    if attend:
                        pe.wait_ge(aT_ready, b + 1)
                        pe.wait_ge(v_ready, b + 1)
                        for j in range(GRP):
                            t = pe.matmul(bh[:, jcols(j)], amT[:, jcols(j)], v[1 - par][:, jcols(j)], start=(j == 0), stop=True, skip_group_check=True)
                        t.then_inc(hid_acc, 1)
                    if attend:
                        pe.wait_ge(hg_ready, b + 1)
                        for j in range(GRP):
                            t = pe.transpose(ba[:, jcols(j)], hg[:, jcols(j)], ident[:])
                        t.then_inc(hidT_acc, 1)
                    if project:
                        pe.wait_ge(vT_ready, a + 1)
                        pe.wait_ge(rows_done, a + 1)
                        for j in range(GRP):
                            t = pe.transpose(br[:, jcols(j)], vT[:, jcols(j)], ident[:])
                        t.then_inc(vt_acc, 1)
                    if route:
                        pe.wait_ge(r_step, RSTEPS * r + R_MASKS)
                        if project:
                            pe.wait_ge(k_ready, a + 1)
                        cum = bk[:, 0:ME]
                        pe.matmul(cum, lowtri_b[:], mask[:], start=True, stop=False, skip_group_check=True)
                        for j in range(GRP - 1):
                            later = cum[:, (j + 1) * TE:ME].rearrange("p (k c) -> p k c", c=TE)
                            pe.matmul(later, ones_b[:], mask[:, jcols(j, TE)].unsqueeze(1).broadcast_to([P, GRP - 1 - j, TE]),
                                      start=False, stop=False, skip_group_check=True)
                        for j in range(GRP):
                            t = pe.matmul(bk[:, ME:ME + TE], ones_b[:], mask[:, jcols(j, TE)], start=False, stop=(j == GRP - 1), skip_group_check=True)
                        t.then_inc(rank_acc, 1)

                pipeline(pe, turn)

            @block.scalar
            def _(act):
                act.activation(e1[:], a1[:], ACT.Exp, bias=s1[:, 1:2], accum_out=s1[:, 2:3]).then_inc(a1_act, 1)

                def turn(i, par, project, soften, attend, route):
                    a, b, r = i + 1, i - 1, i - 2
                    if attend:
                        act.wait_ge(aT_acc, b + 1)
                        atleast(act, hid_acc, b)
                        act.activation(amT[:], ba[:], ACT.Copy).then_inc(aT_ready, 1)
                    if route:
                        act.wait_ge(r_step, RSTEPS * r + R_SHIFTED)
                        act.activation(lex[:], lsh[:], ACT.Exp).then_inc(l_exp, 1)
                    if soften:
                        act.wait_ge(smax_ready, (i + 1) * 2)
                        atleast(act, a_ready, GRP * i)
                        for j in range(GRP):
                            c = slice(j * P, (j + 1) * P)
                            act.activation(pr[:, c], bs[:, c], ACT.Exp, bias=nsmax[:, j:j + 1], scale=SCALE, accum_out=rs[:, j:j + 1]).then_inc(p_ready, 1)
                    if project:
                        act.wait_ge(q_acc, a + 1)
                        atleast(act, s_acc, a)
                        act.activation(qT[:], bq[:], ACT.Identity, bias=vecT[:, R_BQ2:R_BQ2 + 1]).then_inc(q_ready, 1)
                        act.wait_ge(k_acc, a + 1)
                        act.activation(kT[:], bk[:], ACT.Identity, bias=vecT[:, R_BK2:R_BK2 + 1]).then_inc(k_ready, 1)
                        act.wait_ge(rows_acc, a + 1)
                        act.activation(x1rows[:, bass.ds(a * GT, GT)], br[:], ACT.Identity).then_inc(rows_done, 1)
                    if attend:
                        act.wait_ge(hid_acc, b + 1)
                        atleast(act, hid_kept, 16 * b)
                        act.activation(hg[:], bh[:], ACT.Copy).then_inc(hg_ready, 1)
                    if attend:
                        act.wait_ge(hidT_acc, b + 1)
                        atleast(act, logit_acc, b)
                        act.activation(hT[:], ba[:], ACT.Copy).then_inc(hidT_ready, 1)
                    if project:
                        act.wait_ge(vt_acc, a + 1)
                        atleast(act, hid_acc, i)
                        act.activation(v[1 - par][:], br[:], ACT.Copy).then_inc(v_ready, 1)

                pipeline(act, turn)

            @block.vector
            def _(dve):
                dve.memset(run[:], 0.0).then_inc(run_zero, 1)
                for q in range(TOPK):
                    dve.memset(cmul[:, q:q + 1], float(CAP * (TOPK - q))).then_inc(run_zero, 1)
                    dve.memset(cadd[:, q:q + 1], float(q * E * 2 * CAP - 1)).then_inc(run_zero, 1)
                dve.wait_ge(const_step, 2)
                dve.tensor_copy(lowtri_b[:], lowtri[:]).then_inc(w_conv, 1)
                dve.tensor_scalar(ones_b[:], lowtri[:], 0.0, 1.0, ALU.mult, ALU.add).then_inc(w_conv, 1)
                dve.wait_ge(att_in, 16 * LOADS)
                dve.tensor_copy(w_hi[:, 0:3 * P], raw[0][:, 0:3 * P]).then_inc(w_conv, 1)
                dve.wait_ge(w_conv, 3)
                dve.tensor_tensor(w_lo[:, 0:3 * P], raw[0][:, 0:3 * P], w_hi[:, 0:3 * P], ALU.subtract).then_inc(w_conv, 1)

                def v_constants():
                    dve.wait_ge(cv_acc, 1)
                    dve.tensor_scalar(cvT[:], bm[:, 0:B], bvc[:], None, ALU.add).then_inc(w_conv, 1)
                    dve.wait_ge(w_conv, 5)
                    dve.wait_ge(run_zero, 1 + 2 * TOPK)
                    dve.wait_ge(a1_act, 1)
                    dve.reciprocal(s1[:, 3:4], s1[:, 2:3]).then_inc(a1_dve, 1)
                    dve.wait_ge(a1_dve, 6)
                    dve.tensor_scalar(a1[:], e1[:], s1[:, 3:4], alph[:], ALU.mult, ALU.mult).then_inc(a1_dve, 1)
                    dve.wait_ge(a1_pe, 2)
                    dve.tensor_copy(alphaT[:], bh[:, 0:B]).then_inc(a1_dve, 1)
                    dve.wait_ge(a1_dve, A1_DVE + 1)

                def split(g):
                    atleast(dve, x_in, (g - (NX - 1)) * 16)
                    atleast(dve, v_acc, g)
                    dve.tensor_copy(xg_hi[:], x_cols(g)).then_inc(x_ready, 1)
                    dve.wait_ge(x_ready, g * 2 + 1)
                    dve.tensor_tensor(xg_lo[:], x_cols(g), xg_hi[:], ALU.subtract).then_inc(x_ready, 1)

                def turn(i, par, project, soften, attend, route):
                    a, b, r = i + 1, i - 1, i - 2
                    n = RSTEPS * r
                    step = [0]

                    def did(ins):
                        step[0] += 1
                        ins.then_inc(r_step, 1)
                        return step[0]

                    def after(k):
                        dve.wait_ge(r_step, n + k)

                    lg = bm[:, 0:GRP * E].rearrange("p (k e) -> p k e", e=E)
                    if soften:
                        dve.wait_ge(s_acc, i + 1)
                        dve.tensor_reduce(smax[:], bs[:].rearrange("p (k c) -> p k c", c=P), AX.X, ALU.max).then_inc(smax_ready, 1)
                        dve.wait_ge(smax_ready, i * 2 + 1)
                        dve.tensor_scalar(nsmax[:], smax[:], -SCALE, None, ALU.mult).then_inc(smax_ready, 1)
                    if route:
                        dve.wait_ge(logit_acc, r + 1)
                        k = did(dve.tensor_reduce(lmax[:], lg, AX.X, ALU.max))
                        after(k)
                        k = did(dve.tensor_tensor(v3(lsh, E), lg, lmax[:].unsqueeze(2).broadcast_to([P, GRP, E]), ALU.subtract))
                        assert k == R_SHIFTED
                    if route:
                        dve.wait_ge(l_exp, r + 1)
                        k = did(dve.tensor_reduce(lsum[:], v3(lex, E), AX.X, ALU.add))
                        after(k)
                        k = did(dve.reciprocal(lrec[:], lsum[:]))
                        after(k)
                        k = did(dve.tensor_tensor(v3(sc, E), v3(lex, E), lrec[:].unsqueeze(2).broadcast_to([P, GRP, E]), ALU.mult))
                        after(k)
                        did(dve.tensor_scalar(first_sc[:], sc[:, 0:1], 1.0, None, ALU.mult))
                        for j in range(GRP):
                            k = did(dve.max(mx[:, j * 8:(j + 1) * 8], sc[:, j * E:(j + 1) * E]))
                        after(k)
                        did(dve.tensor_tensor(den[:].unsqueeze(2), v3(mx, 8)[:, :, 0:1], v3(mx, 8)[:, :, 1:2], ALU.add))
                        for j in range(GRP):
                            k = did(dve.max_index(ix[:, j * 8:(j + 1) * 8], mx[:, j * 8:(j + 1) * 8], sc[:, j * E:(j + 1) * E]))
                        after(k)
                        k = did(dve.tensor_scalar(v3(ixf, TOPK), v3(ix, 8)[:, :, 0:TOPK], 1.0, None, ALU.mult))
                        kd = did(dve.tensor_scalar(den[:], den[:], EPS_GATE, None, ALU.max))
                        after(k)
                        for q in range(TOPK):
                            k = did(dve.tensor_tensor(mask4[:, :, q, :], iota8[:].unsqueeze(1).broadcast_to([P, GRP, E]),
                                                      v3(ixf, TOPK)[:, :, q:q + 1].broadcast_to([P, GRP, E]), ALU.is_equal))
                        assert k == R_MASKS
                        after(kd)
                        kr = did(dve.reciprocal(dinv[:], den[:]))
                    if project:
                        dve.wait_ge(v_acc, a + 1)
                        atleast(dve, vt_acc, a)
                        dve.tensor_tensor(v3(vT, P), bv_[:].rearrange("p (k c) -> p k c", c=P),
                                          cvT[:, bass.ds(a * GRP, GRP)].unsqueeze(2).broadcast_to([P, GRP, P]), ALU.add).then_inc(vT_ready, 1)
                    if soften:
                        dve.wait_ge(p_ready, (i + 1) * GRP)
                        dve.reciprocal(rinv[:], rs[:]).then_inc(rinv_ready, 1)
                        dve.wait_ge(rinv_ready, i + 1)
                        atleast(dve, aT_acc, i)
                        for j in range(GRP):
                            js = slice(j * P, (j + 1) * P)
                            dve.tensor_scalar(am[:, js], pr[:, js], rinv[:, j:j + 1], alphaT[:, bass.ds(i * GRP + j, 1)], ALU.mult, ALU.subtract).then_inc(a_ready, 1)
                    if route:
                        after(kr)
                        ga = gates_all[:].rearrange("p (k q) -> p k q", q=TOPK)
                        did(dve.tensor_tensor(ga[:, bass.ds(r * GRP, GRP), :], v3(mx, 8)[:, :, 0:TOPK], dinv[:].unsqueeze(2).broadcast_to([P, GRP, TOPK]), ALU.mult))
                        did(dve.tensor_scalar(mask1[:].rearrange("p (k e) -> p k e", e=E)[:, bass.ds(r * GRP, GRP), :], mask4[:, :, 1, :], 1.0, None, ALU.mult))
                        dve.wait_ge(rank_acc, r + 1)
                        cum = bk[:, 0:ME].rearrange("p (k c) -> p k c", c=TE)
                        kl = did(dve.tensor_tensor(v3(loc, TE), cum, run[:].unsqueeze(1).broadcast_to([P, GRP, TE]), ALU.add))
                        kp = did(dve.tensor_tensor(v3(pos, TOPK), v3(ixf, TOPK), cmul[:].unsqueeze(1).broadcast_to([P, GRP, TOPK]), ALU.mult))
                        after(kl)
                        k = did(dve.tensor_tensor(sel[:], loc[:], mask[:], ALU.mult))
                        did(dve.tensor_tensor(run[:], run[:], bk[:, ME:ME + TE], ALU.add))
                        after(k)
                        k = did(dve.tensor_reduce(rank[:].rearrange("p (k q) -> p k q", q=TOPK), sel[:].rearrange("p (k q e) -> p k q e", q=TOPK, e=E), AX.X, ALU.add))
                    if route:
                        kq = did(dve.tensor_tensor(v3(pos, TOPK), v3(pos, TOPK), cadd[:].unsqueeze(1).broadcast_to([P, GRP, TOPK]), ALU.add))
                        after(k)
                        ko = did(dve.tensor_scalar(over[:], rank[:], float(CAP), FAR, ALU.is_gt, ALU.mult))
                        did(dve.tensor_scalar(rank_all[:, bass.ds(r * GRP * TOPK, GRP * TOPK)], rank[:], 1.0, None, ALU.mult))
                        after(kq)
                        k = did(dve.tensor_tensor(pos[:], pos[:], rank[:], ALU.add))
                        after(k)
                        atleast(dve, hs_free, r)
                        dve.tensor_tensor(posi[par][:], pos[:], over[:], ALU.add).then_inc(pos_ready, 1)
                        assert step[0] == RSTEPS, step[0]
                    if project and not (isinstance(i, int) and i == NG - 2):
                        split(i + 2)

                split(0)
                v_constants()
                turn(-1, 1, True, False, False, False)
                turn(0, 0, True, True, False, False)
                turn(1, 1, True, True, True, False)
                turn(2, 0, True, True, True, True)
                with dve.Fori(0, (NG - 6) // 2) as k:
                    turn(k * 2 + 3, 1, True, True, True, True)
                    turn(k * 2 + 4, 0, True, True, True, True)
                turn(NG - 3, 1, True, True, True, True)
                turn(NG - 2, 0, True, True, True, True)
                turn(NG - 1, 1, False, True, True, True)
                turn(NG, 0, False, False, True, True)
                turn(NG + 1, 1, False, False, False, True)

                dve.wait_ge(r_step, RSTEPS * NG)
                dve.tensor_scalar(firsts[:], run[:, 0:E], float(CAP), None, ALU.min).then_inc(f_step, 1)
                dve.tensor_scalar(firsts_u[:], run[0:1, 0:E], float(CAP), None, ALU.min).then_inc(f_step, 1)
                dve.tensor_tensor(v3(sel1, E), v3(mask1, E), run[:, 0:E].unsqueeze(1).broadcast_to([P, B, E]), ALU.mult).then_inc(f_step, 1)
                dve.wait_ge(f_step, 3)
                dve.tensor_reduce(before1[:], v3(sel1, E), AX.X, ALU.add).then_inc(f_step, 1)
                dve.wait_ge(f_step, 4)
                ra = rank_all[:].rearrange("p (k q) -> p k q", q=TOPK)
                dve.tensor_tensor(ra[:, :, 1:2], ra[:, :, 1:2], before1[:].unsqueeze(2), ALU.add).then_inc(f_step, 1)
                dve.wait_ge(f_step, 5)
                dve.tensor_scalar(keep[:], rank_all[:], float(CAP), None, ALU.is_le).then_inc(f_step, 1)
                dve.wait_ge(f_step, 6)
                dve.tensor_tensor(gates_all[:], gates_all[:], keep[:], ALU.mult).then_inc(f_step, 1)


R_SHIFTED, R_MASKS, RSTEPS = 2, 19, 31


def phase_experts(nc, d, m):
    bank, ident, vecT = m["bank"], m["ident"], m["vecT"]
    w_hi, w_lo, raw, x1T = m["w_hi"], m["w_lo"], m["raw"], m["x1T"]
    slots, results, wts_in, sent_rows, dispatch = m["slots"], m["results"], m["wts_in"], m["sent_rows"], m["dispatch"]
    g_f, g_hi, g_lo = m["g_f"], m["g_hi"], m["g_lo"]
    firsts, firsts_u = m["firsts"], m["firsts_u"]
    NCK = [(0, 512), (512, 512), (1024, 256)]
    TILES = [(0, 4), (4, 4), (8, 2)]
    WB = [0, 2 * H]
    XB = [4 * H, 4 * H + CAP]
    UN = [(s, hb) for s in range(3) for hb in range(HB)]
    NU = len(UN)
    NY = len(NCK)

    with ExitStack() as ctx:
        def sb(name, shape, dt=F32):
            return ctx.enter_context(nc.sbuf_tensor(name, shape, dt))

        def sem(name):
            return ctx.enter_context(nc.semaphore(name))

        rows = [x1T[:, i * ST * ROWW:(i + 1) * ST * ROWW] for i in range(2)]
        iota8 = m["iota8"]
        touched = sb("touched3", [P, 6])
        touch = sem("touch3")
        dest = [sb(f"dest{i}", [P, ST], U32) for i in range(2)]
        yT = [sb(f"yT{i}", [P, 512]) for i in range(2)]
        yrow = [sb(f"yrow{i}", [P, ST * P]) for i in range(2)]
        b1c = [sb(f"b1c{i}", [P, HB + 1]) for i in range(2)]
        slot_no = sb("slot_no", [P, ST])
        second = sb("second", [P, ST])
        destf = sb("destf", [P, ST])

        joined = [sem(f"joined{e}") for e in range(E)]; slot_no_ready = sem("slot_no_ready"); dest_step = sem("dest_step")
        head_in = [sem("head_in0"), sem("head_in1")]; rows_in = [sem("rows_in0"), sem("rows_in1")]
        dest_ready = sem("dest_ready"); xe_acc = sem("xe_acc"); xe_ready = sem("xe_ready"); fc1_acc = sem("fc1_acc")
        fc1_ready = sem("fc1_ready"); fc2_ready = sem("fc2_ready"); bias_ready = sem("bias_ready")
        h1_done = sem("h1_done"); silu_done = sem("silu_done"); lo_done = sem("lo_done"); y_done = sem("y_done")
        yT_ready = sem("yT_ready"); yr_acc = sem("yr_acc"); yr_ready = sem("yr_ready"); sent = [sem("sent_even"), sem("sent_odd")]

        xbank = [bank[0], bank[1]]
        hbank = [bank[2], bank[3], bank[4]]
        ybank = [bank[5], bank[6]]
        rbank = bank[7]

        X_AT = {1: 0, 4: 1, 7: 2}
        FC1_AT = 8
        YT_AT = {6: (0, 0), 10: (0, 1), 2: (-1, 2)}
        BACK_AT = {7: (0, 0), 11: (0, 1), 3: (-1, 2)}
        YROW_AT = {8: (0, 0), 0: (-1, 1), 4: (-1, 2)}

        def turns(eng, turn):
            turn(0, 0, 0, True)
            turn(1, 1, 0, True)
            with eng.Fori(1, E // 2 - 1) as pair:
                turn(pair * 2, 0, pair, True)
                turn(pair * 2 + 1, 1, pair, True)
            turn(E - 2, 0, E // 2 - 1, True)
            turn(E - 1, 1, E // 2 - 1, False)

        def before_first(e):
            return isinstance(e, int) and e < 0

        with nc.Block() as block:
            @block.sync
            def _(sp):
                def join(e):
                    n1 = sp.value_load(firsts_u[0:1, e:e + 1], min_val=0, max_val=CAP)
                    sp.dma_start(slots[bass.ds(n1 + 2 * CAP * e, CAP), :], slots[SECOND + e * CAP:SECOND + (e + 1) * CAP, :]).then_inc(joined[e], 16)

                for par in range(2):
                    sp.wait_ge(sent_rows[par], 16 * TOPK * B // 2)
                join(0)
                for e in range(E):
                    q = e % 2
                    if e >= 2:
                        sp.wait_ge(fc1_acc, e - 1)
                        sp.wait_ge(fc2_ready, 2 * (e - 1))
                        load_expert_weights(sp, d, raw, wts_in, e)
                        sp.wait_ge(xe_acc, NY * (e - 1))
                        sp.wait_ge(dest_ready, e - 1)
                    sp.wait_ge(joined[e], 16)
                    t0 = 0
                    for t1, done in ((TILES[0][1], head_in[q]), (ST, rows_in[q])):
                        sp.dma_start(rows[q].rearrange("p (n c) -> p n c", c=ROWW)[:, t0:t1, :],
                                     slots[e * 2 * CAP + t0 * P:e * 2 * CAP + t1 * P, :].rearrange("(n p) c -> p n c", p=P)).then_inc(done, 16)
                        t0 = t1
                    if e + 1 < E:
                        join(e + 1)

            @block.gpsimd
            def _(gp):
                last_slot = gp.to_reg(SLOT_ROWS - 1)
                last_result = gp.to_reg(TOPK * N - 1)
                gp.iota(slot_no[:], pattern=[[P, ST]], base=0, channel_multiplier=1, allow_small_or_imprecise_dtypes=True).then_inc(slot_no_ready, 1)
                dispatch(gp, last_slot, NG - 1, 1, NG // 2)

                def send(e, q, s):
                    t0, nt = TILES[s]
                    atleast(gp, yr_ready, NY * e + s + 1)
                    atleast(gp, dest_ready, e + 1)
                    gp.tensor_tensor(touched[:, NY * q + s:NY * q + s + 1], iota8[:, 0:1], iota8[:, 0:1], ALU.add).then_inc(touch, 1)
                    for j in range(t0, t0 + nt):
                        gp.indirect_dma_start(out=results, out_offset=bass.IndirectOffsetOnAxis(ap=dest[q][:, j:j + 1], axis=0),
                                              in_=yrow[q][:, j * P:(j + 1) * P], in_offset=None,
                                              bounds_check=last_result, oob_is_err=False).then_inc(sent[q], 16)

                def turn(e, q, pair):
                    for s in range(NY):
                        send(e, q, s)

                loop_pairs(gp, turn)
                gp.wait_ge(sent[0], 16 * ST * E // 2)
                gp.wait_ge(sent[1], 16 * ST * E // 2)

            @block.tensor
            def _(pe):
                def columns(e, q, half, k):
                    t0, nt = TILES[k]
                    atleast(pe, rows_in[q] if k else head_in[q], 16 * half)
                    if k == 1:
                        atleast(pe, fc1_ready, 2 * e if not isinstance(e, int) or e else 2)
                    else:
                        atleast(pe, xe_ready, 6 * e + (2 if k else 0))
                    for j in range(nt):
                        t = pe.transpose(xbank[k % 2][:, j * P:(j + 1) * P], rows[q][:, (t0 + j) * ROWW:(t0 + j) * ROWW + P], ident[:])
                    t.then_inc(xe_acc, 1)

                def fc1(e, q, half):
                    atleast(pe, wts_in[q], 32 * half)
                    if not isinstance(e, int) or e:
                        atleast(pe, xe_ready, 6 * e + 4)
                    for j in range(HB):
                        t = pe.transpose(xbank[1][:, j * P:(j + 1) * P], raw[q][:, j * P:(j + 1) * P], ident[:])
                    t.then_inc(fc1_acc, 1)

                def first(e, q, u):
                    s, hb = UN[u]
                    c0, w = NCK[s]
                    if hb == 0:
                        atleast(pe, xe_ready, 6 * e + 2 * (s + 1))
                    if u == 0:
                        atleast(pe, fc1_ready, 2 * (e + 1))
                    atleast(pe, silu_done, 2 * (NU * e + u - 2))
                    a = slice(WB[q] + hb * P, WB[q] + (hb + 1) * P)
                    b_ = slice(XB[q] + c0, XB[q] + c0 + w)
                    mm3(pe, hbank[u % 3][:, 0:w], w_hi[:, a], w_lo[:, a], w_hi[:, b_], w_lo[:, b_], True, True).then_inc(h1_done, 1)

                def second_(e, q, u):
                    s, hb = UN[u]
                    w = NCK[s][1]
                    if u == 0:
                        atleast(pe, fc2_ready, 2 * (e + 1))
                    if hb == 0:
                        atleast(pe, yT_ready, NY * e + s - 1)
                    atleast(pe, lo_done, NU * e + u + 1)
                    a = slice(WB[q] + H + hb * P, WB[q] + H + (hb + 1) * P)
                    mm3(pe, ybank[(q + s) % 2][:, 0:w], w_hi[:, a], w_lo[:, a], g_hi[u % 4][:, 0:w], g_lo[u % 4][:, 0:w], hb == 0, hb == HB - 1).then_inc(y_done, 1)

                def back(e, q, s):
                    nt = TILES[s][1]
                    atleast(pe, yT_ready, NY * e + s + 1)
                    atleast(pe, yr_ready, NY * e + s)
                    for j in range(nt):
                        t = pe.transpose(rbank[:, j * P:(j + 1) * P], yT[(q + s) % 2][:, j * P:(j + 1) * P], ident[:])
                    t.then_inc(yr_acc, 1)

                def turn(e, q, pair, more):
                    for u in range(NU):
                        first(e, q, u)
                        if u >= 2:
                            second_(e, q, u - 2)
                        elif not before_first(e - 1):
                            second_(e - 1, 1 - q, NU + u - 2)
                        if u in BACK_AT:
                            o, s = BACK_AT[u]
                            if not before_first(e + o):
                                back(e + o, (q + o) % 2, s)
                        if more and u in X_AT:
                            columns(e + 1, 1 - q, pair + q + 1, X_AT[u])
                        if more and u == FC1_AT:
                            fc1(e + 1, 1 - q, pair + q + 1)

                fc1(0, 0, 1)
                for k in range(NY):
                    columns(0, 0, 1, k)
                turns(pe, turn)
                second_(E - 1, 1, NU - 2)
                second_(E - 1, 1, NU - 1)
                back(E - 1, 1, 2)

            @block.scalar
            def _(act):
                def fc1(e, q):
                    atleast(act, fc1_acc, e + 1)
                    atleast(act, h1_done, NU * (e - 1))
                    act.activation(w_hi[:, WB[q]:WB[q] + H], xbank[1][:], ACT.Copy).then_inc(fc1_ready, 1)

                def results_out(e, q, s):
                    w = NCK[s][1]
                    atleast(act, y_done, NU * e + HB * (s + 1))
                    atleast(act, yr_acc, NY * e + s - 1)
                    act.activation(yT[(q + s) % 2][:, 0:w], ybank[(q + s) % 2][:, 0:w], ACT.Identity, bias=b1c[q][:, HB:HB + 1]).then_inc(yT_ready, 1)

                def turn(e, q, pair, more):
                    for u in range(NU):
                        s, hb = UN[u]
                        w = NCK[s][1]
                        atleast(act, h1_done, NU * e + u + 1)
                        if u == 0:
                            atleast(act, bias_ready, e + 1)
                        atleast(act, lo_done, NU * e + u - 1)
                        atleast(act, y_done, NU * e + u - 3)
                        b_ = b1c[q][:, hb:hb + 1]
                        act.activation(g_f[u % 2][:, 0:w], hbank[u % 3][:, 0:w], ACT.Silu, bias=b_).then_inc(silu_done, 1)
                        act.activation(g_hi[u % 4][:, 0:w], hbank[u % 3][:, 0:w], ACT.Silu, bias=b_).then_inc(silu_done, 1)
                        if u in YT_AT:
                            o, s = YT_AT[u]
                            if not before_first(e + o):
                                results_out(e + o, (q + o) % 2, s)
                        if more and u == FC1_AT + 1:
                            fc1(e + 1, 1 - q)

                fc1(0, 0)
                turns(act, turn)
                results_out(E - 1, 1, 2)

            @block.vector
            def _(dve):
                def biases(e, q):
                    atleast(dve, yT_ready, NY * (e - 1))
                    atleast(dve, silu_done, 2 * NU * (e - 1))
                    dve.tensor_scalar(b1c[q][:, 0:HB], vecT[:, bass.ds(R_FB1 + HB * e, HB)], 1.0, None, ALU.mult)
                    dve.tensor_scalar(b1c[q][:, HB:HB + 1], vecT[:, bass.ds(R_FB2 + e, 1)], 1.0, None, ALU.mult).then_inc(bias_ready, 1)

                def destinations(e, q, half):
                    atleast(dve, sent[q], 16 * ST * (half - 1))
                    atleast(dve, touch, NY * (e - 1))
                    atleast(dve, rows_in[q], 16 * half)
                    atleast(dve, head_in[q], 16 * half)
                    dve.tensor_scalar(destf[:].unsqueeze(2), rows[q].rearrange("p (n c) -> p n c", c=ROWW)[:, :, P:ROWW], 1.0, None, ALU.mult).then_inc(dest_step, 1)
                    dve.tensor_scalar(second[:], slot_no[:], firsts[:, bass.ds(e, 1)], float(N), ALU.is_ge, ALU.mult).then_inc(dest_step, 1)
                    dve.wait_ge(dest_step, e * 2 + 2)
                    dve.tensor_tensor(dest[q][:], destf[:], second[:], ALU.add).then_inc(dest_ready, 1)

                def columns(e, q, k):
                    t0, nt = TILES[k]
                    atleast(dve, xe_acc, NY * e + k + 1)
                    atleast(dve, h1_done, NU * (e - 1))
                    o = slice(XB[q] + t0 * P, XB[q] + (t0 + nt) * P)
                    dve.tensor_copy(w_hi[:, o], xbank[k % 2][:, 0:nt * P]).then_inc(xe_ready, 1)
                    atleast(dve, xe_ready, 6 * e + 2 * k + 1)
                    dve.tensor_tensor(w_lo[:, o], xbank[k % 2][:, 0:nt * P], w_hi[:, o], ALU.subtract).then_inc(xe_ready, 1)

                def fc1(e, q):
                    atleast(dve, fc1_ready, 2 * e + 1)
                    dve.tensor_tensor(w_lo[:, WB[q]:WB[q] + H], xbank[1][:], w_hi[:, WB[q]:WB[q] + H], ALU.subtract).then_inc(fc1_ready, 1)

                def fc2(e, q, half):
                    atleast(dve, wts_in[q], 32 * half)
                    atleast(dve, y_done, NU * (e - 1))
                    dve.tensor_copy(w_hi[:, WB[q] + H:WB[q] + 2 * H], raw[q][:, H:2 * H]).then_inc(fc2_ready, 1)
                    atleast(dve, fc2_ready, 2 * e + 1)
                    dve.tensor_tensor(w_lo[:, WB[q] + H:WB[q] + 2 * H], raw[q][:, H:2 * H], w_hi[:, WB[q] + H:WB[q] + 2 * H], ALU.subtract).then_inc(fc2_ready, 1)

                def rows_out(e, q, s):
                    t0, nt = TILES[s]
                    atleast(dve, yr_acc, NY * e + s + 1)
                    atleast(dve, dest_ready, e + 1)
                    dve.tensor_copy(yrow[q][:, t0 * P:(t0 + nt) * P], rbank[:, 0:nt * P]).then_inc(yr_ready, 1)

                def turn(e, q, pair, more):
                    for u in range(NU):
                        w = NCK[UN[u][0]][1]
                        atleast(dve, silu_done, 2 * (NU * e + u + 1))
                        atleast(dve, y_done, NU * e + u - 3)
                        dve.tensor_tensor(g_lo[u % 4][:, 0:w], g_f[u % 2][:, 0:w], g_hi[u % 4][:, 0:w], ALU.subtract).then_inc(lo_done, 1)
                        if u in YROW_AT:
                            o, s = YROW_AT[u]
                            if not before_first(e + o):
                                rows_out(e + o, (q + o) % 2, s)
                        if more:
                            half = pair + q + 1
                            if u in X_AT:
                                columns(e + 1, 1 - q, X_AT[u])
                            if u == 3:
                                fc2(e + 1, 1 - q, half)
                            if u == FC1_AT - 1:
                                biases(e + 1, 1 - q)
                                destinations(e + 1, 1 - q, half)
                            if u == FC1_AT + 1:
                                fc1(e + 1, 1 - q)

                biases(0, 0)
                fc1(0, 0)
                fc2(0, 0, 1)
                dve.wait_ge(slot_no_ready, 1)
                for k in range(NY):
                    columns(0, 0, k)
                destinations(0, 0, 1)
                turns(dve, turn)
                rows_out(E - 1, 1, 1)
                rows_out(E - 1, 1, 2)


def loop_pairs(eng, turn):
    turn(0, 0, 0)
    turn(1, 1, 0)
    with eng.Fori(1, E // 2) as pair:
        turn(pair * 2, 0, pair)
        turn(pair * 2 + 1, 1, pair)


def phase_norm(nc, d, m, out):
    xT, wide, results, gates_all = m["xT"], m["wide"], m["results"], m["gates_all"]
    x1rows = xT
    hid3 = wide[:].rearrange("p (b c) -> p b c", c=ROWW)
    with ExitStack() as ctx:
        def sb(name, shape, dt=F32):
            return ctx.enter_context(nc.sbuf_tensor(name, shape, dt))

        def sem(name):
            return ctx.enter_context(nc.semaphore(name))

        YB = 4
        gb = sb("gamma", [P, P]); bb = sb("beta", [P, P]); epsc = sb("epsc", [P, 1])
        yb = [[m["x1T"][:, (q * YB + i) * GRP * P:(q * YB + i + 1) * GRP * P] for i in range(YB)] for q in range(TOPK)]
        res = [sb(f"res{i}", [P, GRP * P]) for i in range(3)]
        nrm = [sb(f"nrm{i}", [P, GRP * P]) for i in range(2)]
        fin = [sb(f"fin{i}", [P, GRP * P]) for i in range(YB)]
        st = sb("stats", [P, GRP * 6])
        mv = [sb(f"mv{i}", [P, GRP * 2]) for i in range(2)]
        sd = [sb(f"sd{i}", [P, GRP]) for i in range(2)]
        rstd = [sb(f"rstd{i}", [P, GRP]) for i in range(2)]
        shift = [sb(f"shift{i}", [P, GRP]) for i in range(2)]
        n_in = sem("n_in"); y_in = [sem(f"y_in{i}") for i in range(YB)]; eps_ready = sem("eps_ready"); weighted = sem("weighted")
        summed = sem("summed"); stats_ready = sem("stats_ready"); mv_ready = sem("mv_ready"); sd_ready = sem("sd_ready")
        shift_step = sem("shift_step"); nrm_ready = sem("nrm_ready"); scaled = sem("scaled"); fin_ready = sem("fin_ready")
        stored = [sem(f"stored{i}") for i in range(YB)]
        SUMS = 1 + GRP
        y_src = results.rearrange("(q g b p) c -> q g p b c", q=TOPK, b=GRP, p=P)

        def v3(a):
            return a[:].rearrange("p (b c) -> p b c", c=P)

        def cols(j):
            return slice(j * P, (j + 1) * P)

        with nc.Block() as block:
            @block.sync
            def _(sp):
                for g in range(NG):
                    if g >= YB:
                        sp.wait_ge(summed, SUMS * (g - YB + 1))
                    for q in range(TOPK):
                        sp.dma_start(v3(yb[q][g % YB]), y_src[q, g]).then_inc(y_in[g % YB], 16)
                    if g == 0:
                        sp.dma_start(gb[:], d["L1_ffn_ln_gamma"].rearrange("(a p) -> a p", a=1).broadcast_to([P, P])).then_inc(n_in, 16)
                        sp.dma_start(bb[:], d["L1_ffn_ln_beta"].rearrange("(a p) -> a p", a=1).broadcast_to([P, P])).then_inc(n_in, 16)

            @block.scalar
            def _(act):
                def weigh(g):
                    act.wait_ge(y_in[g % YB], 32 * (g // YB + 1))
                    for j in range(GRP):
                        k = TOPK * (g * GRP + j)
                        act.activation(yb[0][g % YB][:, cols(j)], yb[0][g % YB][:, cols(j)], ACT.Copy, scale=gates_all[:, k:k + 1]).then_inc(weighted, 1)

                def deviation(g):
                    act.wait_ge(mv_ready, GRP * (g + 1))
                    act.wait_ge(shift_step, 2 * max(g - 1, 0))
                    act.activation(sd[g % 2][:], mv[g % 2][:].rearrange("p (b c) -> p b c", c=2)[:, :, 1], ACT.Sqrt, bias=epsc[:]).then_inc(sd_ready, 1)

                def normalize(g):
                    act.wait_ge(shift_step, 2 * (g + 1))
                    atleast(act, scaled, 2 * (g - 1))
                    for j in range(GRP):
                        act.activation(nrm[g % 2][:, cols(j)], res[g % 3][:, cols(j)], ACT.Identity,
                                       bias=shift[g % 2][:, j:j + 1], scale=rstd[g % 2][:, j:j + 1]).then_inc(nrm_ready, 1)

                def store(g):
                    act.wait_ge(fin_ready, g + 1)
                    act.dma_start(out[GRP * g:GRP * (g + 1)].rearrange("b t c -> t b c"), v3(fin[g % YB])).then_inc(stored[g % YB], 16)

                act.wait_ge(eps_ready, 1)
                for g in range(NG + 2):
                    if g < NG:
                        weigh(g)
                    if 1 <= g <= NG:
                        deviation(g - 1)
                    if g >= 2:
                        normalize(g - 2)
                    if g >= 4:
                        store(g - 4)
                for g in range(NG - 2, NG):
                    store(g)
                for i in range(YB):
                    act.wait_ge(stored[i], 16 * NG // YB)

            @block.gpsimd
            def _(gp):
                gp.wait_ge(n_in, 32)
                for g in range(NG):
                    f, w = v3(fin[g % YB]), v3(nrm[g % 2])
                    gp.wait_ge(nrm_ready, GRP * (g + 1))
                    if g >= YB:
                        gp.wait_ge(stored[g % YB], 16 * (g // YB))
                    gp.tensor_tensor(f, w, gb[:].unsqueeze(1).broadcast_to([P, GRP, P]), ALU.mult).then_inc(scaled, 1)
                    gp.wait_ge(scaled, 2 * g + 1)
                    gp.tensor_tensor(f, f, bb[:].unsqueeze(1).broadcast_to([P, GRP, P]), ALU.add).then_inc(scaled, 1)

            @block.vector
            def _(dve):
                dve.memset(epsc[:], EPS_LN).then_inc(eps_ready, 1)

                def finish(g):
                    dve.wait_ge(scaled, 2 * (g + 1))
                    dve.tensor_tensor(fin[g % YB][:], fin[g % YB][:], x1rows[:, g * GRP * P:(g + 1) * GRP * P], ALU.add).then_inc(fin_ready, 1)

                def shifts(g):
                    dve.wait_ge(sd_ready, g + 1)
                    if g >= 2:
                        dve.wait_ge(nrm_ready, GRP * (g - 1))
                    dve.reciprocal(rstd[g % 2][:], sd[g % 2][:]).then_inc(shift_step, 1)
                    dve.wait_ge(shift_step, 2 * g + 1)
                    dve.scalar_tensor_tensor(out=shift[g % 2][:], in0=mv[g % 2][:].rearrange("p (b c) -> p b c", c=2)[:, :, 0], scalar=-1.0,
                                             in1=rstd[g % 2][:], op0=ALU.mult, op1=ALU.mult).then_inc(shift_step, 1)

                for g in range(NG):
                    r = res[g % 3]
                    dve.wait_ge(weighted, GRP * (g + 1))
                    if g >= 3:
                        dve.wait_ge(nrm_ready, GRP * (g - 2))
                    dve.tensor_tensor(v3(r), v3(yb[0][g % YB]), hid3[:, g * GRP:(g + 1) * GRP, 0:P], ALU.add).then_inc(summed, 1)
                    dve.wait_ge(summed, SUMS * g + 1)
                    for j in range(GRP):
                        k = TOPK * (g * GRP + j) + 1
                        dve.scalar_tensor_tensor(out=r[:, cols(j)], in0=yb[1][g % YB][:, cols(j)], scalar=gates_all[:, k:k + 1],
                                                 in1=r[:, cols(j)], op0=ALU.mult, op1=ALU.add).then_inc(summed, 1)
                    if g >= 1:
                        dve.wait_ge(mv_ready, GRP * g)
                    for j in range(GRP):
                        dve.wait_ge(summed, SUMS * g + j + 2)
                        dve.bn_stats(st[:, 6 * j:6 * j + 6], r[:, cols(j)]).then_inc(stats_ready, 1)
                    if g >= 2:
                        dve.wait_ge(shift_step, 2 * (g - 1))
                    for j in range(GRP):
                        dve.wait_ge(stats_ready, GRP * g + j + 1)
                        dve.bn_aggr(mv[g % 2][:, 2 * j:2 * j + 2], st[:, 6 * j:6 * j + 6]).then_inc(mv_ready, 1)
                    if g >= 1:
                        shifts(g - 1)
                    if g >= 3:
                        finish(g - 3)
                shifts(NG - 1)
                for g in range(NG - 3, NG):
                    finish(g)


NAMES = ['x', 'cond_1024', 'L0_cond_W_z', 'L0_cond_U_z', 'L0_cond_C_z', 'L0_cond_b_z', 'L0_cond_W_r', 'L0_cond_U_r',
         'L0_cond_C_r', 'L0_cond_b_r', 'L0_cond_W', 'L0_cond_U', 'L0_cond_C', 'L0_cond_b', 'L0_ffn_rW', 'L0_ffn_rb',
         'L0_ffn_W1', 'L0_ffn_b1', 'L0_ffn_W2', 'L0_ffn_b2', 'L0_ffn_sW1', 'L0_ffn_sb1', 'L0_ffn_sW2', 'L0_ffn_sb2',
         'L1_cond_Wq1', 'L1_cond_bq1', 'L1_cond_Wq2', 'L1_cond_bq2', 'L1_cond_Wk1', 'L1_cond_bk1', 'L1_cond_Wk2',
         'L1_cond_bk2', 'L1_cond_Wv', 'L1_cond_bv', 'L1_cond_alpha', 'L1_ffn_wg', 'L1_ffn_fc1_w', 'L1_ffn_fc1_b',
         'L1_ffn_fc2_w', 'L1_ffn_fc2_b', 'L1_ffn_ln_gamma', 'L1_ffn_ln_beta']


def kernel(**inputs):
    from concourse import bacc
    from concourse.bass_utils import run_bass_kernel_spmd

    nc = bacc.Bacc("TRN2", target_bir_lowering=False, num_devices=1)
    arrays, d = {}, {}
    for name in NAMES:
        a = np.ascontiguousarray(inputs[name])
        arrays[f"in_{name}"] = a
        d[name] = nc.dram_tensor(f"in_{name}", a.shape, F32, kind="ExternalInput").ap()
    out = nc.dram_tensor("out", (B, T, P), F32, kind="ExternalOutput").ap()
    build(nc, d, out)
    return run_bass_kernel_spmd(nc, [arrays], core_ids=[0]).results[0]["out"]
```
